# Optimizing a Trainium2 kernel written in Bass

```python
import numpy as np
import jax
import jax.numpy as jnp

def _softmax(x, axis=-1):
    return jax.nn.softmax(x, axis=axis)

def _gelu(x):
    return jax.nn.gelu(x, approximate=True)

def _silu(x):
    return jax.nn.silu(x)

def _sigmoid(x):
    return jax.nn.sigmoid(x)

def _layernorm(x, axis=-1, eps=1e-05):
    m = jnp.mean(x, axis=axis, keepdims=True)
    v = jnp.var(x, axis=axis, keepdims=True)
    return (x - m) / jnp.sqrt(v + eps)

def _scatter_add(tgt, idx, src, axis=0):
    return tgt.at[idx].add(src)

def _segment_sum(src, seg, n):
    return jax.ops.segment_sum(src, seg, n)
kernel_name = 'mk_adaln_ffn_d2_seqx_r4_87d449'

def setup_inputs(seed: int=0):
    np.random.seed(seed)
    _w = jnp.asarray

    def _rec_inputs():
        import jax
        import jax.numpy as jnp
        _rk = jax.random.key(seed)
        x = -0.000125 + 0.9999 * jax.random.normal(jax.random.fold_in(_rk, 1), (64, 64, 1024), jnp.float32)
        _lenS = 64 - jax.random.randint(jax.random.fold_in(_rk, 7), (64,), 0, max(1, 64 // 4) + 1, jnp.int32)
        _lenS2 = 64 - jax.random.randint(jax.random.fold_in(_rk, 8), (64,), 0, max(1, 64 // 4) + 1, jnp.int32)
        cond_128 = 0.0061147 + 1.02565 * jax.random.normal(jax.random.fold_in(_rk, 11), (64, 128), jnp.float32)
        fside_S_0 = -0.022604 + 0.987366 * jax.random.normal(jax.random.fold_in(_rk, 12), (64,), jnp.float32)
        return (x, cond_128, fside_S_0)
    x, cond_128, fside_S_0 = _rec_inputs()

    def _L0_cond_setup():
        import jax, jax.numpy as jnp
        import numpy as np
        from jax import lax
        N, C_IN, L = (32, 64, 1024)
        C_OUT, K, GROUPS = (64, 9, 4)
        C_DIM, PAD, STRIDE = (128, 4, 1)
        key = jax.random.key(seed)
        k1, k2, k3, k4, k5 = jax.random.split(key, 5)
        x = jax.random.normal(k1, (N, C_IN, L), dtype=jnp.float32)
        c = jax.random.normal(k2, (N, C_DIM), dtype=jnp.float32)
        weight = jax.random.normal(k3, (C_OUT, C_IN // GROUPS, K), dtype=jnp.float32)
        c_weight = jax.random.normal(k4, (C_OUT, C_DIM), dtype=jnp.float32)
        bias = jax.random.normal(k5, (C_OUT,), dtype=jnp.float32)
        return {'x': x, 'c': c, 'weight': weight, 'c_weight': c_weight, 'bias': bias}
    _L0_cond_all = _L0_cond_setup()
    _L0_cond_in = {k: v for k, v in _L0_cond_all.items() if k in ('weight', 'c_weight')}
    del _L0_cond_all

    def _L0_ffn_setup():
        import jax, jax.numpy as jnp
        import numpy as np
        QMAX = 127.0
        key = jax.random.key(seed)
        k1, k2 = jax.random.split(key)
        input_act = jax.random.normal(k1, (4, 512, 1024), dtype=jnp.float32)
        weight = jax.random.normal(k2, (1024, 1024), dtype=jnp.float32) * 0.02
        return {'input_act': input_act, 'weight': weight}
    _L0_ffn_all = _L0_ffn_setup()
    _L0_ffn_in = {k: v for k, v in _L0_ffn_all.items() if k in ('weight',)}
    del _L0_ffn_all

    def _L1_cond_setup():
        import jax, jax.numpy as jnp
        import numpy as np
        K = 8
        T = 1.0
        D_EMBD = 128
        IN_C = 64
        OUT_C = 64
        BS = 32
        H = 1024
        HID = 128
        key = jax.random.key(seed)
        ks = jax.random.split(key, 10)
        s = lambda fan_in: 1.0 / np.sqrt(fan_in)
        return {'x': jax.random.normal(ks[0], (BS, IN_C, H), dtype=jnp.float32), 'embedding': jax.random.normal(ks[1], (BS, D_EMBD), dtype=jnp.float32), 'W0': jax.random.normal(ks[2], (D_EMBD, HID), dtype=jnp.float32) * s(D_EMBD), 'b0': jnp.zeros((HID,), dtype=jnp.float32), 'W1': jax.random.normal(ks[3], (HID, HID), dtype=jnp.float32) * s(HID), 'b1': jnp.zeros((HID,), dtype=jnp.float32), 'W2': jax.random.normal(ks[4], (HID, K), dtype=jnp.float32) * s(HID), 'b2': jnp.zeros((K,), dtype=jnp.float32), 'weight': jax.random.normal(ks[5], (K, OUT_C, IN_C, 1), dtype=jnp.float32) * s(IN_C), 'bias_k': jax.random.normal(ks[6], (K, OUT_C), dtype=jnp.float32) * 0.1}
    _L1_cond_all = _L1_cond_setup()
    _L1_cond_in = {k: v for k, v in _L1_cond_all.items() if k in ('W0', 'b0', 'W1', 'b1', 'W2', 'b2', 'weight', 'bias_k')}
    del _L1_cond_all

    def _L1_ffn_setup():
        import jax, jax.numpy as jnp
        import numpy as np
        NUM_EXPERTS = 8
        RANK = 32
        ALPHA = 16.0
        TOP_K = 2
        TEMPERATURE = 1.0
        GAMMA = 0.5
        SOFT_TOPK_TEMP = 0.5
        N_GRAM = 2
        EPS = 1e-06
        key = jax.random.key(seed)
        ks = jax.random.split(key, 6)
        d_in, d_out = (1024, 1024)
        Bsz, T = (4, 512)
        x = jax.random.normal(ks[0], (Bsz, T, d_in), dtype=jnp.float32)
        W = jax.random.normal(ks[1], (d_out, d_in), dtype=jnp.float32) / np.sqrt(d_in)
        b = jax.random.normal(ks[2], (d_out,), dtype=jnp.float32) * 0.01
        A = jax.random.normal(ks[3], (d_in, RANK), dtype=jnp.float32) / np.sqrt(d_in)
        Bmat = jax.random.normal(ks[4], (RANK, d_out), dtype=jnp.float32) * 0.01
        LiMEs = jax.random.normal(ks[5], (NUM_EXPERTS, RANK), dtype=jnp.float32) * 0.1
        return {'x': x, 'W': W, 'b': b, 'A': A, 'Bmat': Bmat, 'LiMEs': LiMEs}
    _L1_ffn_all = _L1_ffn_setup()
    _L1_ffn_in = {k: v for k, v in _L1_ffn_all.items() if k in ('W', 'b', 'A', 'Bmat', 'LiMEs')}
    del _L1_ffn_all
    return {'x': x, 'cond_128': cond_128, 'fside_S_0': fside_S_0, 'L0_cond_weight': _L0_cond_in['weight'], 'L0_cond_c_weight': _L0_cond_in['c_weight'], 'L0_ffn_weight': _L0_ffn_in['weight'], 'L1_cond_W0': _L1_cond_in['W0'], 'L1_cond_b0': _L1_cond_in['b0'], 'L1_cond_W1': _L1_cond_in['W1'], 'L1_cond_b1': _L1_cond_in['b1'], 'L1_cond_W2': _L1_cond_in['W2'], 'L1_cond_b2': _L1_cond_in['b2'], 'L1_cond_weight': _L1_cond_in['weight'], 'L1_cond_bias_k': _L1_cond_in['bias_k'], 'L1_ffn_W': _L1_ffn_in['W'], 'L1_ffn_b': _L1_ffn_in['b'], 'L1_ffn_A': _L1_ffn_in['A'], 'L1_ffn_Bmat': _L1_ffn_in['Bmat'], 'L1_ffn_LiMEs': _L1_ffn_in['LiMEs']}

def reference(x, cond_128, fside_S_0, L0_cond_weight, L0_cond_c_weight, L0_ffn_weight, L1_cond_W0, L1_cond_b0, L1_cond_W1, L1_cond_b1, L1_cond_W2, L1_cond_b2, L1_cond_weight, L1_cond_bias_k, L1_ffn_W, L1_ffn_b, L1_ffn_A, L1_ffn_Bmat, L1_ffn_LiMEs):
    import jax
    import jax.numpy as jnp

    def _L0_cond_ref(x, c, weight, c_weight, bias):
        import jax, jax.numpy as jnp
        import numpy as np
        from jax import lax
        N, C_IN, L = (32, 64, 1024)
        C_OUT, K, GROUPS = (64, 9, 4)
        C_DIM, PAD, STRIDE = (128, 4, 1)
        out = lax.conv_general_dilated(x, weight, window_strides=(STRIDE,), padding=[(PAD, PAD)], dimension_numbers=('NCH', 'OIH', 'NCH'), feature_group_count=GROUPS)
        ctx = jnp.einsum('nd,od->no', c, c_weight)
        out = out + ctx[:, :, None] + bias[None, :, None]
        return out

    def _L0_ffn_ref(input_act, weight):
        import jax, jax.numpy as jnp
        import numpy as np
        QMAX = 127.0
        w_scale = jnp.max(jnp.abs(weight), axis=-1, keepdims=True) / QMAX
        w_q = jnp.round(weight / w_scale).astype(jnp.int8)
        a_scale = jnp.max(jnp.abs(input_act), axis=-1, keepdims=True) / QMAX
        x_q = jnp.round(input_act / a_scale).astype(jnp.int8)
        acc = jnp.matmul(x_q.astype(jnp.int32), w_q.T.astype(jnp.int32))
        scale = a_scale * w_scale.T[None, :, :]
        out = (acc.astype(jnp.float32) * scale).astype(jnp.float16)
        return out

    def _L1_cond_ref(x, embedding, W0, b0, W1, b1, W2, b2, weight, bias_k):
        import jax, jax.numpy as jnp
        import numpy as np
        K = 8
        T = 1.0
        D_EMBD = 128
        IN_C = 64
        OUT_C = 64
        BS = 32
        H = 1024
        HID = 128
        h = jax.nn.gelu(embedding @ W0 + b0, approximate=False)
        h = jax.nn.gelu(h @ W1 + b1, approximate=False)
        att = jax.nn.softmax((h @ W2 + b2) / T, axis=-1)
        agg_w = jnp.einsum('bk,koi->boi', att, weight[..., 0])
        agg_b = att @ bias_k
        out = jnp.einsum('boi,bih->boh', agg_w, x) + agg_b[:, :, None]
        return out

    def _L1_ffn_ref(x, W, b, A, Bmat, LiMEs):
        import jax, jax.numpy as jnp
        import numpy as np
        NUM_EXPERTS = 8
        RANK = 32
        ALPHA = 16.0
        TOP_K = 2
        TEMPERATURE = 1.0
        GAMMA = 0.5
        SOFT_TOPK_TEMP = 0.5
        N_GRAM = 2
        EPS = 1e-06
        Bsz, T, d_in = x.shape
        E = LiMEs.shape[0]
        scaling = ALPHA / RANK
        H = jnp.einsum('btd,od->bto', x, W) + b
        z = jnp.einsum('btd,dr->btr', x, A)
        anchors = jnp.arange(N_GRAM - 1, T, N_GRAM)
        H_slice = H[:, anchors, :E]
        delta_slice = jnp.einsum('bar,er->bae', z[:, anchors], LiMEs)
        H_scale = jnp.maximum(jnp.max(jnp.abs(H_slice)), EPS)
        d_scale = jnp.maximum(jnp.max(jnp.abs(delta_slice)), EPS)
        logits = ((1.0 - GAMMA) * (H_slice / H_scale) + GAMMA * (delta_slice / d_scale)) / TEMPERATURE
        probs = jax.nn.softmax(logits, axis=-1)
        topk_vals, _ = jax.lax.top_k(probs, TOP_K)
        thresh = topk_vals[..., -1:]
        mask = jax.nn.sigmoid((probs - thresh) / SOFT_TOPK_TEMP)
        weights = probs * mask
        weights = weights / (jnp.sum(weights, axis=-1, keepdims=True) + 1e-09)
        weights_full = jnp.repeat(weights, N_GRAM, axis=1)
        p_mix = jnp.einsum('bte,er->btr', weights_full, LiMEs)
        delta = jnp.einsum('btr,ro->bto', z * p_mix, Bmat) * scaling
        return H + delta
    x = x + _L0_ffn_ref(_L0_cond_ref(x, cond_128, L0_cond_weight, L0_cond_c_weight, fside_S_0), L0_ffn_weight)
    x = x + _L1_ffn_ref(_L1_cond_ref(x, cond_128, L1_cond_W0, L1_cond_b0, L1_cond_W1, L1_cond_b1, L1_cond_W2, L1_cond_b2, L1_cond_weight, L1_cond_bias_k), L1_ffn_W, L1_ffn_b, L1_ffn_A, L1_ffn_Bmat, L1_ffn_LiMEs)
    return x

_drawn_inputs = setup_inputs


def setup_inputs(seed=0):
    import zlib

    import numpy as np

    out = dict(_drawn_inputs(seed))
    spreads = {'L1_cond_b0': (0.0, 0.618), 'L1_cond_b1': (0.0, 0.426), 'L1_cond_b2': (0.0, 0.335)}
    factors = {'L1_cond_bias_k': 8.0,
     'L1_ffn_b': 64.0,
     'L1_ffn_A': 8.0,
     'L1_ffn_Bmat': 8.0,
     'L1_ffn_LiMEs': 8.0}
    for name, (base, spread) in spreads.items():
        noise = np.random.default_rng([zlib.crc32(name.encode()), seed]).standard_normal(out[name].shape)
        drawn = base * np.exp(spread * noise) if base else spread * noise
        out[name] = jnp.asarray(drawn.astype(out[name].dtype))
    for name, factor in factors.items():
        out[name] = (out[name] * factor).astype(out[name].dtype)
    return out
```

```python
from contextlib import ExitStack

import numpy as np
import concourse.bass as bass
from concourse import mybir

F32 = mybir.dt.float32
F16 = mybir.dt.float16
BF16 = mybir.dt.bfloat16
U32 = mybir.dt.uint32
I32 = mybir.dt.int32
ALU = mybir.AluOpType
ACT = mybir.ActivationFunctionType
AX = mybir.AxisListType
RMAX = bass.bass_isa.ReduceOp.absmax

P = 128
B, CH, L = 64, 64, 1024
GRP, CG = 4, 16
TAPS = 9
PH = 8
MB = L // PH
NT = B // 2
NL = L // P
HALF = L // 2
NK, HID = 8, 128
R, E = 32, 8
NTOK = B * CH
NANCH = NTOK // 2
NJ = NANCH // P
ZW = 64 + R + E
QMAX = 127.0
MAGIC = 12582912.0
EXPMASK = 0x7F800000
TOP = 13


def program(nc, x, cond, fside, w_conv, w_ctx, w_q, mlp_w0, mlp_b0, mlp_w1, mlp_b1, mlp_w2, mlp_b2,
            mix_w, mix_b, w_ffn, b_ffn, w_a, w_b, limes, out):
    ctx = ExitStack()
    with ctx:
        ctx.enter_context(nc.allow_non_contiguous_dma(reason="small weights"))

        def sb(name, shape, dt):
            return ctx.enter_context(nc.sbuf_tensor(name, shape, dt))

        sems = {}

        def sem(name):
            if name not in sems:
                sems[name] = ctx.enter_context(nc.semaphore(name))
            return sems[name]

        ffn_wT = sb("ffn_wT", [P, 2, NL, L], F16)
        wq_nat = ffn_wT[:, :, :, :].rearrange("p a c l -> p (a c l)").bitcast(F32)
        stage = sb("stage", [P, NL * L], F32)
        w_nat = stage[:, :].rearrange("p (a l) -> p a l", a=NL)
        zT = stage[:, 0:NTOK]
        x2_cols = stage[:, NTOK:NTOK + 2 * L].bitcast(F16).rearrange("p (s h c t) -> p s h c t", s=2, h=2, c=NL)
        xb = stage[:, NTOK + 2 * L:NTOK + 4 * L].rearrange("p (s l) -> p s l", s=2)
        wqT = sb("wqT", [P, PH, L], BF16)
        mixT = sb("mixT", [P, NT, P], F32)
        mixb_all = sb("mixb_all", [P, NT, P], F32)
        kw = mixb_all[0:NK, :, :].rearrange("k a t -> k (a t)").rearrange("k (o i) -> k o i", o=CH)
        x_in = sb("x_in", [P, 4, L], F32)
        x_blk = sb("x_blk", [P, 4, 2, PH, CG], F32)
        x_ph = sb("x_ph", [P, 2, GRP, MB + 1], F32)
        yb = sb("yb", [P, 8, MB], F32)
        yv = sb("yv", [P, 8, MB], F32)
        yq = sb("yq", [P, 8, MB], BF16)
        yqT = sb("yqT", [P, PH, P], BF16)
        f16 = sb("f16", [P, L], F16)
        x1 = sb("x1", [P, 2, L], F32)
        u = sb("u", [P, L], F32)
        wsc_b = sb("wsc_b", [P, L], F32)
        bias_b = sb("bias_b", [P, L], F32)
        ident = sb("ident", [P, P], F32)
        identb = sb("identb", [P, P], BF16)
        conv_wT = sb("conv_wT", [CG, GRP, TAPS, CG], F32)
        conv_w = sb("conv_w", [P, GRP, 16, CG], F32)
        w_conv_nat = sb("w_conv_nat", [CH, CG, TAPS], F32)
        ybias = sb("ybias", [P, B, GRP], F32)
        fside_b = sb("fside_b", [P, GRP], F32)
        cond_nat = sb("cond_nat", [B, P], F32)
        condT = sb("condT", [P, B], F32)
        w_ctx_nat = sb("w_ctx_nat", [CH, P], F32)
        w_ctxT = sb("w_ctxT", [P, CH], F32)
        w_ctx_rep = sb("w_ctx_rep", [P, GRP, PH, CG], F32)
        mw0 = sb("mw0", [P, HID], F32)
        mw1 = sb("mw1", [HID, HID], F32)
        mw2 = sb("mw2", [HID, NK], F32)
        mb01 = sb("mb01", [HID, 2], F32)
        mb2_b = sb("mb2_b", [B, NK], F32)
        mixb_k = sb("mixb_k", [NK, CH], F32)
        h0 = sb("h0", [HID, B], F32)
        h1 = sb("h1", [HID, B], F32)
        att = sb("att", [B, NK], F32)
        att_e = sb("att_e", [B, NK], F32)
        att_s = sb("att_s", [B, 4], F32)
        attT = sb("attT", [NK, B], F32)
        chan_mask = sb("chan_mask", [P, CG], F32)
        set_rows = sb("set_rows", [8, P], F32)
        wq_max = sb("wq_max", [P, NL], F32)
        wq_scale = sb("wq_scale", [P, NL], F32)
        wq_inv = sb("wq_inv", [P, NL], F32)
        a_nat = sb("a_nat", [P, NL, R], F32)
        z_w = sb("z_w", [P, NL, ZW], F16)
        scal = sb("scal", [P, 16], F32)
        rowmax = sb("rowmax", [P, 8], F32)
        chanmax = sb("chanmax", [8, CG], F32)
        chanmax_rep = sb("chanmax_rep", [8, PH, CG], F32)
        yscale = sb("yscale", [P, 8], F32)
        yinv = sb("yinv", [P, 8], F32)
        tok_junk = sb("tok_junk", [P, CG], F32)
        tok_scale = sb("tok_scale", [P, 4], F32)
        x1max = sb("x1max", [P, 1], F32)
        x1max_all = sb("x1max_all", [P, 1], F32)
        pool_turn = sb("pool_turn", [1, 2], F32)
        bound = sb("bound", [P, 2], F32)
        t_pair = sb("t_pair", [P, 4, 2], F32)
        t_all = sb("t_all", [P, NT, 2], F32)
        z_lo = sb("z_lo", [R + E, P], F32)
        limes_nat = sb("limes_nat", [E, R], F32)
        limesT = sb("limesT", [R, E], F32)
        b_rank = sb("b_rank", [R, L], F32)
        z_scaled = sb("z_scaled", [R, 2, P], F32)
        gate = sb("gate", [P, 8, NJ, E], F32)
        gsm = sb("gsm", [P, 6, NJ], F32)
        gmx = sb("gmx", [P, 8], F32)
        top8 = sb("top8", [P, NJ, E], F32)
        gateT = stage[0:E, NTOK:NTOK + NANCH]
        unscale = sb("unscale", [P, NT], F32)
        x2_in = x_in[:, :, :].rearrange("p s l -> p (s l)").bitcast(F16).rearrange(
            "p (s h c t) -> p s h c t", s=4, h=2, c=NL)
        xb_in = mixb_all[:, :, :].rearrange("p a t -> p (a t)").rearrange("p (s l) -> p s l", s=4)
        o_sb = x1

        ps = ctx.enter_context(nc.psum_tensor("ps", [P, 8 * 512], F32))

        def bank(n, k=1):
            return ps[:, n * 512:(n + k) * 512]

        ps_ph, ps_conv, ps_acc, ps_mix, ps_tr, ps_small = bank(0), bank(1, 2), bank(3, 2), bank(5), bank(6), bank(7)
        ps_trb = ps_tr.bitcast(BF16)

        x2_dram = nc.dram_tensor("x2_scratch", [NT, P, 2 * L], F16, kind="Internal").ap()
        xb_dram = nc.dram_tensor("xb_scratch", [NT, P, L], F32, kind="Internal").ap()

        def mix_bank(n, e):
            return bank(n)[e * CH:(e + 1) * CH, :].rearrange("p (o t) -> p o t", t=NT)

        def mix_block(n, e):
            return mixT[e * CH:(e + 1) * CH, :, e * CH + 16 * n:e * CH + 16 * n + 16].rearrange("p t o -> p o t")

        x_t = x.rearrange("(t b) c l -> t (b c) l", b=2)
        out_t = out.rearrange("(t b) c l -> t (b c) l", b=2)

        block = ctx.enter_context(nc.Block())

        def at(i, c, k=1, d=0):
            return i * (4 * k) + (k * c + d)

        def wait(eng, name, val):
            if not isinstance(val, int) or val > 0:
                eng.wait_ge(sem(name), val)

        def bodies(eng, body):
            for t in range(-1, 4):
                body(0, t, lambda o, t=t: 0 <= t + o < NT)
            n = NT // 4 - 2
            with eng.Fori(0, n) as i:
                for c in range(4, 8):
                    body(i, c, lambda o: True)
            for t in range(NT - 4, NT + 3):
                body(n, t - 4 * n, lambda o, t=t: 0 <= t + o < NT)

        @block.sync
        def _(sp):
            sp.dma_start(w_conv_nat[:, :, :], w_conv).then_inc(sem("conv_w_loaded"), 16)
            sp.dma_start(cond_nat[:, :], cond).then_inc(sem("cond_loaded"), 16)
            sp.dma_start(w_ctx_nat[:, :], w_ctx).then_inc(sem("cond_loaded"), 16)
            sp.dma_start(x_in[:, 0, :], x_t[0]).then_inc(sem("x_loaded0"), 16)
            for a in range(2):
                sp.dma_start(wq_nat.rearrange("p (a l) -> p a l", a=NL)[:, 4 * a:4 * a + 4, :],
                             w_q.rearrange("(a p) l -> p a l", p=P)[:, 4 * a:4 * a + 4, :]).then_inc(sem(f"wq_loaded{a}"), 16)
            for t in range(1, 4):
                sp.dma_start(x_in[:, t, :], x_t[t]).then_inc(sem(f"x_loaded{t}"), 16)
            sp.dma_start(w_nat, w_ffn.rearrange("(a p) l -> p a l", p=P)).then_inc(sem("w_loaded"), 16)
            sp.wait_ge(sem("conv_wT_ready"), 2)
            sp.wait_ge(sem("conv_w_zeroed"), 1)
            for p in range(PH):
                v = (p + 4) % PH
                sp.dma_start(conv_w[p * CG:(p + 1) * CG, :, v:v + TAPS, :], conv_wT[:, :, :, :]).then_inc(sem("conv_w_ready"), 16)

            def step(i, c, load=True, xb_out=True, x2_out=True):
                if load:
                    wait(sp, "x1_ready", at(i, c, 2, -6))
                    sp.dma_start(x_in[:, c % 4, :], x_t[at(i, c)]).then_inc(sem(f"x_loaded{c % 4}"), 16)
                if xb_out:
                    wait(sp, "xb_ready", at(i, c, 1, -3))
                    sp.dma_start(xb_dram[at(i, c, 1, -4)], xb[:, c % 2, :]).then_inc(sem(f"xb_saved{c % 2}"), 16)
                if x2_out:
                    wait(sp, "lo_ready", at(i, c, 2, -10))
                    sp.dma_start(x2_dram[at(i, c, 1, -6)],
                                 x2_cols[:, c % 2].rearrange("p h c t -> p (h c t)")).then_inc(sem(f"x2_saved{c % 2}"), 16)

            for c in range(4):
                step(1, c, x2_out=c >= 2)
            with sp.Fori(2, NT // 4) as i:
                for c in range(4):
                    step(i, c)
            for c in range(6):
                step(NT // 4, c, load=False, xb_out=c < 4)

            for s in range(2):
                sp.wait_ge(sem(f"x2_saved{s}"), 16 * (NT // 2))
                sp.wait_ge(sem(f"xb_saved{s}"), 16 * (NT // 2))

            def fetch(i, c):
                wait(sp, "h_ready", at(i, c, 1, -3))
                sp.dma_start(x2_in[:, c % 4].rearrange("p h c t -> p (h c t)"), x2_dram[at(i, c)]).then_inc(sem(f"x2_loaded{c % 4}"), 16)
                wait(sp, "out_ready", at(i, c, 2, -6))
                sp.dma_start(xb_in[:, c % 4, :], xb_dram[at(i, c)]).then_inc(sem(f"xb_loaded{c % 4}"), 16)

            for c in range(4):
                fetch(0, c)
            with sp.Fori(1, NT // 4) as i:
                for c in range(4):
                    fetch(i, c)

        @block.tensor
        def _(pe):
            mm, tr = nc.tensor.matmul, nc.tensor.transpose
            pe.wait_ge(sem("ident_ready"), 3)
            pe.wait_ge(sem("conv_w_loaded"), 16)
            for k in range(TAPS):
                last = tr(ps_conv[0:CG, (TAPS - 1 - k) * CH:(TAPS - k) * CH], w_conv_nat[:, :, k], ident[0:CH, 0:CH])
            last.then_inc(sem("conv_wT_psum"), 1)
            pe.wait_ge(sem("cond_loaded"), 32)
            tr(ps_small[:, 0:B], cond_nat[:, :], ident[0:B, 0:B])
            tr(ps_small[:, B:B + CH], w_ctx_nat[:, :], ident[0:CH, 0:CH]).then_inc(sem("condT_psum"), 1)
            pe.wait_ge(sem("condT_ready"), 3)
            for g in range(GRP):
                last = mm(ps_small[:, 128 + g * B:128 + (g + 1) * B], w_ctx_rep[:, g].rearrange("p a c -> p (a c)"),
                          condT[:, :], start=True, stop=True)
            last.then_inc(sem("ctx_psum"), 1)
            pe.wait_ge(sem("mlp_loaded"), 16 * 6)
            mm(ps_mix[:, 0:B], mw0[:, :], condT[:, :], start=True, stop=True).then_inc(sem("mlp_psum"), 1)
            pe.wait_ge(sem("h_act"), 1)
            mm(ps_mix[:, 64:64 + B], mw1[:, :], h0[:, :], start=True, stop=True).then_inc(sem("mlp_psum"), 1)
            pe.wait_ge(sem("h_act"), 2)
            mm(ps_mix[0:B, 128:128 + NK], h1[:, :], mw2[:, :], start=True, stop=True).then_inc(sem("mlp_psum"), 1)
            pe.wait_ge(sem("att_ready"), 1)
            tr(ps_mix[0:NK, 192:192 + B], att[:, :], ident[0:B, 0:B]).then_inc(sem("mlp_psum"), 1)
            for o in range(NL):
                pe.wait_ge(sem("wq_ready"), o + 1)
                if o >= 2:
                    pe.wait_ge(sem("wqT_ready"), o - 1)
                bk = (ps_tr if o % 2 == 0 else ps_ph).bitcast(BF16)
                q = yq if o % 2 == 0 else yqT
                qv = q[:, :, :].rearrange("p a b -> p (a b)").rearrange("p (m e) -> p e m", e=PH)
                for p in range(PH):
                    last = tr(bk[:, p * P:(p + 1) * P], qv[:, p, :], identb[:, :])
                last.then_inc(sem("wqT_psum"), 1)
            for o in range(NL):
                last = mm(ps_acc[:, o * P:(o + 1) * P], wq_scale[:, o:o + 1].to_broadcast([P, P]), ident[:, :], start=True, stop=True)
            last.then_inc(sem("wsc_psum"), 1)
            pe.wait_ge(sem("attT_ready"), 1)
            pe.wait_ge(sem("wsc_ready"), 1)
            pe.wait_ge(sem("wqT_ready"), NL)
            pe.wait_ge(sem("conv_wT_ready"), 2)
            pe.wait_ge(sem("ybias_ready"), 1)
            pe.wait_ge(sem("kw_loaded"), 16)
            for o in range(CH):
                for e in range(2):
                    last = mm(ps[e * CH:(e + 1) * CH, o * NT:(o + 1) * NT], kw[:, o, :], attT[:, e::2], start=True, stop=True)
                if o % 16 == 15:
                    last.then_inc(sem("mix_psum"), 1)
            pe.wait_ge(sem("mixb_loaded"), 16)
            for b in (*range(B // 2, B), *range(B // 2)):
                if b == 0:
                    pe.wait_ge(sem("mixT_ready"), 8)
                last = mm(ps[:, b * CH:(b + 1) * CH], attT[:, b:b + 1].to_broadcast([NK, P]), mixb_k[:, :], start=True, stop=True)
                if b % 8 == 7:
                    last.then_inc(sem("mixb_psum"), 1)
            pe.wait_ge(sem("w_loaded"), 16)
            for c in range(NL):
                if c < 2:
                    pe.wait_ge(sem("mixb_ready"), 8)
                else:
                    pe.wait_ge(sem("w_lo_ready"), c - 1)
                bk = ps_conv if c % 2 == 0 else ps_acc
                for o in range(NL):
                    last = tr(bk[:, o * P:(o + 1) * P], w_nat[:, o, c * P:(c + 1) * P], ident[:, :])
                last.then_inc(sem("wT_psum"), 1)
            pe.wait_ge(sem("limes_loaded"), 32)
            tr(ps_small[0:R, 0:E], limes_nat[:, :], ident[0:E, 0:E]).then_inc(sem("limesT_psum"), 1)
            pe.wait_ge(sem("limesT_ready"), 1)
            pe.wait_ge(sem("w_lo_ready"), NL)

            def phases(i, c, s):
                if s == 0:
                    wait(pe, "blk_ready", at(i, c, 1, 1))
                    wait(pe, "ph_ready", at(i, c, 4, 0))
                else:
                    wait(pe, "ph_ready", at(i, c, 4, 2))
                bk = ps_ph.rearrange("p (q m) -> p q m", q=4)
                for m in range(4):
                    last = tr(bk[:, :, m * 32:(m + 1) * 32], x_blk[:, m, s].rearrange("p e c -> p (e c)"), ident[:, :])
                last.then_inc(sem("ph_psum"), 1)

            def conv(i, c):
                wait(pe, "ph_ready", at(i, c, 4, 4))
                wait(pe, "yb_ready", at(i, c))
                for g in range(GRP):
                    o = ps_conv[:, g * 2 * MB:(g + 1) * 2 * MB]
                    w = conv_w[:, g].rearrange("p v c -> p (v c)")
                    xg = x_ph[:, g % 2, g // 2:GRP:2, :]
                    mm(o, w[:, P:2 * P], xg[:, :, 0:MB], start=True, stop=False)
                    last = mm(o, w[:, 0:P], xg[:, :, 1:MB + 1], start=False, stop=True)
                last.then_inc(sem("conv_ready"), 1)

            def max_rows(i, c):
                wait(pe, "rowmax_ready", at(i, c, 1, 1))
                wait(pe, "z_ready", at(i, c, 1, -2))
                tr(ps_small[0:8, 0:P], rowmax[:, :], ident[:, :]).then_inc(sem("rowmaxT_ready"), 1)

            def max_back(i, c):
                wait(pe, "chanmax_ready", at(i, c, 1, 1))
                mm(ps_small[:, 128:136], chanmax_rep[:, :, :].rearrange("p a c -> p (a c)"), ident[0:8, 0:8], start=True, stop=True)
                mm(ps_small[:, 144:144 + CG], set_rows[:, :], chanmax[:, :], start=True, stop=True).then_inc(sem("max_psum"), 1)

            def tokens_out(i, c):
                wait(pe, "yq_ready", at(i, c, 1, 1))
                for s in range(8):
                    last = tr(ps_trb[:, s * P:(s + 1) * P], yq[:, s, :], identb[:, :])
                last.then_inc(sem("yqT_psum"), 1)

            def int_product(i, c, h):
                wait(pe, "yqT_ready", at(i, c, 1, 1))
                wait(pe, "f_ready", at(i, c, 2, h - 1))
                for p in range(PH):
                    last = mm(ps_acc[:, h * HALF:(h + 1) * HALF], yqT[:, p, :], wqT[:, p, h * HALF:(h + 1) * HALF],
                              start=p == 0, stop=p == PH - 1)
                last.then_inc(sem("acc_ready"), 1)

            def mix(i, c, h):
                wait(pe, "x1_ready", at(i, c, 2, 1 + h))
                wait(pe, "u_ready", at(i, c, 2, h))
                for k in range(4):
                    ck = 4 * h + k
                    last = mm(ps_mix[:, k * P:(k + 1) * P], x1[:, c % 2, ck * P:(ck + 1) * P], mixT[:, at(i, c), :],
                              start=True, stop=True)
                last.then_inc(sem("mix_ready"), 1)

            def rank(i, c):
                wait(pe, "lo_ready", at(i, c, 2, 2))
                steps = at(i, c, 1, 3)
                wait(pe, "tok_scale_ready", min(steps, NT) if isinstance(steps, int) else steps)
                for k in range(NL):
                    mm(ps_small[0:ZW, 256:384], z_w[:, k, :], x2_cols[:, c % 2, 0, k, :], start=k == 0, stop=False, skip_group_check=True)
                for k in range(NL):
                    last = mm(ps_small[0:R + E, 256:384], z_w[:, k, 0:R + E], x2_cols[:, c % 2, 1, k, :],
                              start=False, stop=k == NL - 1, skip_group_check=True)
                last.then_inc(sem("z_psum"), 1)

            def body(i, c, on):
                if on(0):
                    conv(i, c)
                if on(-3):
                    rank(i, c - 3)
                if on(1):
                    phases(i, c + 1, 0)
                if on(0):
                    max_rows(i, c)
                if on(-2):
                    mix(i, c - 2, 0)
                if on(0):
                    max_back(i, c)
                if on(-1):
                    int_product(i, c - 1, 0)
                if on(-2):
                    mix(i, c - 2, 1)
                if on(1):
                    phases(i, c + 1, 1)
                if on(-1):
                    int_product(i, c - 1, 1)
                if on(0):
                    tokens_out(i, c)

            pe.wait_ge(sem("conv_w_ready"), 16 * PH)
            pe.wait_ge(sem("x_ph_zeroed"), 2)
            pe.wait_ge(sem("z_w_ready"), 1)
            bodies(pe, body)

            ps_h, ps_g = bank(0, 4), bank(4, 4)
            pe.wait_ge(sem("z_ready"), NT)
            anchors = zT.rearrange("p (j a e) -> p j a e", a=P, e=2)
            for j in range(NJ):
                mm(ps_g[:, j * E:(j + 1) * E], anchors[R:R + E, j, :, 1], ident[R:R + E, R:R + E], start=True, stop=True)
                last = mm(ps_g[:, 512 + j * E:512 + (j + 1) * E], anchors[0:R, j, :, 1], limesT[:, :], start=True, stop=True)
            last.then_inc(sem("logits_psum"), 1)

            def dense(i, c):
                wait(pe, f"x2_loaded{c % 4}", i * 16 + 16 * (c // 4 + 1))
                for h in range(2):
                    wait(pe, "out_ready", at(i, c, 2, h - 3))
                    o = ps_h[:, (c % 2) * L + h * HALF:(c % 2) * L + (h + 1) * HALF]
                    for k in range(NL):
                        for n, (a, w) in enumerate(((0, 0), (0, 1), (1, 0))):
                            mm(o, x2_in[:, c % 4, a, k, :], ffn_wT[:, w, k, h * HALF:(h + 1) * HALF],
                               start=k == 0 and n == 0, stop=False)

            def delta(i, c):
                wait(pe, "z_scaled_ready", at(i, c, 1, 1))
                for h in range(2):
                    o = ps_h[:, (c % 2) * L + h * HALF:(c % 2) * L + (h + 1) * HALF]
                    last = mm(o, z_scaled[:, c % 2, :], b_rank[:, h * HALF:(h + 1) * HALF], start=False, stop=True)
                last.then_inc(sem("h_ready"), 1)

            dense(0, 0)
            pe.wait_ge(sem("gate_ready"), 1)
            pe.wait_ge(sem("logits_read"), 1)
            for j in range(NJ):
                last = tr(ps_g[0:E, j * P:(j + 1) * P], gate[:, 7, j, :], ident[:, :])
            last.then_inc(sem("gateT_psum"), 1)
            dense(0, 1)
            pe.wait_ge(sem("gateT_ready"), 1)
            for k in range(4):
                mm(ps_g[0:R, k * 512:(k + 1) * 512], limes_nat[:, :], gateT[:, k * 512:(k + 1) * 512],
                   start=True, stop=True).then_inc(sem("pmix_psum"), 1)
            delta(0, 0)
            delta(0, 1)
            for t in range(2, 4):
                dense(0, t)
                delta(0, t)
            with pe.Fori(1, NT // 4) as i:
                for c in range(4):
                    dense(i, c)
                    delta(i, c)

        @block.scalar
        def _(act):
            A = nc.scalar.activation
            for dst, src in ((mw0[:, :], mlp_w0), (mw1[:, :], mlp_w1), (mw2[:, :], mlp_w2),
                             (mb01[:, 0:1], mlp_b0.rearrange("(p a) -> p a", a=1)),
                             (mb01[:, 1:2], mlp_b1.rearrange("(p a) -> p a", a=1)),
                             (mb2_b[:, :], mlp_b2.rearrange("(a k) -> a k", a=1).to_broadcast([B, NK]))):
                act.dma_start(dst, src).then_inc(sem("mlp_loaded"), 16)
            for p in range(PH):
                act.dma_start(fside_b[p * CG:(p + 1) * CG, :], fside.rearrange("(g c) -> c g", c=CG)).then_inc(sem("fside_loaded"), 16)
            act.dma_start(kw[:, :, :], mix_w.rearrange("k o i a -> k o (i a)")).then_inc(sem("kw_loaded"), 16)
            act.dma_start(mixb_k[:, :], mix_b).then_inc(sem("mixb_loaded"), 16)
            act.dma_start(a_nat[:, :, :], w_a.rearrange("(c p) r -> p c r", p=P)).then_inc(sem("a_loaded"), 16)
            act.dma_start(limes_nat[:, :], limes).then_inc(sem("limes_loaded"), 16)
            act.dma_start(b_rank[:, :], w_b).then_inc(sem("limes_loaded"), 16)
            act.dma_start(bias_b[:, :], b_ffn.rearrange("(a l) -> a l", a=1).to_broadcast([P, L])).then_inc(sem("bias_loaded"), 16)

            act.wait_ge(sem("conv_wT_psum"), 1)
            A(conv_wT[:, :, 0:8, :].rearrange("p g k o -> p k g o"), ps_conv[0:CG, 0:512].rearrange("p (k g o) -> p k g o", k=8, g=GRP), ACT.Copy).then_inc(sem("conv_wT_ready"), 1)
            A(conv_wT[:, :, 8, :], ps_conv[0:CG, 512:576].rearrange("p (g o) -> p g o", g=GRP), ACT.Copy).then_inc(sem("conv_wT_ready"), 1)
            act.wait_ge(sem("condT_psum"), 1)
            A(condT[:, :], ps_small[:, 0:B], ACT.Copy).then_inc(sem("condT_ready"), 1)
            A(w_ctxT[:, :], ps_small[:, B:B + CH], ACT.Copy).then_inc(sem("w_ctxT_ready"), 1)
            act.wait_ge(sem("w_ctxT_ready"), 1)
            for g in range(GRP):
                last = A(w_ctx_rep[:, g], w_ctxT[:, g * CG:(g + 1) * CG].unsqueeze(1).to_broadcast([P, PH, CG]), ACT.Copy)
            last.then_inc(sem("condT_ready"), 2)
            act.wait_ge(sem("mlp_psum"), 1)
            A(h0[:, :], ps_mix[:, 0:B], ACT.Gelu, bias=mb01[:, 0:1]).then_inc(sem("h_act"), 1)
            act.wait_ge(sem("mlp_psum"), 2)
            A(h1[:, :], ps_mix[:, 64:64 + B], ACT.Gelu, bias=mb01[:, 1:2]).then_inc(sem("h_act"), 1)
            act.wait_ge(sem("att_logits_ready"), 2)
            A(att_e[:, :], att[:, :], ACT.Exp, bias=att_s[:, 0:1]).then_inc(sem("att_exp_ready"), 1)
            act.wait_ge(sem("mlp_psum"), 4)
            A(attT[:, :], ps_mix[0:NK, 192:192 + B], ACT.Copy).then_inc(sem("attT_ready"), 1)
            for o in range(NL + 1):
                if o < NL:
                    act.wait_ge(sem("wq_inv_ready"), o + 1)
                    if o >= 1:
                        act.wait_ge(sem("wq_ready"), o)
                    A(yv[:, :, :].rearrange("p a b -> p (a b)"), wq_nat[:, o * L:(o + 1) * L], ACT.Identity,
                      scale=wq_inv[:, o:o + 1]).then_inc(sem("wq_scaled"), 1)
                if o >= 1:
                    act.wait_ge(sem("wqT_psum"), o)
                    bk = (ps_tr if (o - 1) % 2 == 0 else ps_ph).bitcast(BF16)
                    A(wqT[:, :, (o - 1) * P:o * P], bk.rearrange("p (e c) -> p e c", e=PH), ACT.Copy).then_inc(sem("wqT_ready"), 1)
            act.wait_ge(sem("wsc_psum"), 1)
            A(wsc_b[:, :], ps_acc, ACT.Copy).then_inc(sem("wsc_ready"), 1)
            for n in (1, 3):
                act.wait_ge(sem("mix_psum"), n + 1)
                for e in range(2):
                    A(mix_block(n, e), mix_bank(n, e), ACT.Copy).then_inc(sem("mixT_ready"), 1)
            act.wait_ge(sem("w_scale_ready"), 2)
            for c in range(NL):
                act.wait_ge(sem("wT_psum"), c + 1)
                bk = ps_conv if c % 2 == 0 else ps_acc
                A(ffn_wT[:, 0, c, :], bk, ACT.Copy, scale=scal[:, 2:3]).then_inc(sem("w_hi_ready"), 1)
            act.wait_ge(sem("limesT_psum"), 1)
            A(limesT[:, :], ps_small[0:R, 0:E], ACT.Copy).then_inc(sem("limesT_ready"), 1)

            def phase_rows(i, c, s):
                wait(act, "ph_psum", at(i, c, 2, s + 1))
                bk = ps_ph.rearrange("p (q m) -> p q m", q=4)
                A(x_ph[0:64, s, :, 0:MB], bk[0:64], ACT.Copy).then_inc(sem("ph_ready"), 1)
                A(x_ph[64:128, s, :, 1:MB + 1], bk[64:128], ACT.Copy).then_inc(sem("ph_ready"), 1)

            def scale_rows(i, c):
                wait(act, "yinv_ready", at(i, c, 1, 1))
                wait(act, "yq_ready", at(i, c))
                for s in range(8):
                    last = A(yv[:, s, :], yb[:, s, :], ACT.Copy, scale=yinv[:, s:s + 1])
                last.then_inc(sem("yv_ready"), 1)

            def tokens_sb(i, c):
                wait(act, "yqT_psum", at(i, c, 1, 1))
                A(yqT[:, :, :].rearrange("m p (s c) -> m s p c", s=8),
                  ps_trb.rearrange("m (s p c) -> m s p c", s=8, p=PH), ACT.Copy).then_inc(sem("yqT_ready"), 1)

            def high(i, c, h):
                wait(act, "u_ready", at(i, c, 2, 1 + h))
                if h == 0:
                    wait(act, "t_ready", at(i, c, 1, 1))
                    if not isinstance(i, int) or 4 * i + c >= 2:
                        wait(act, f"x2_saved{c % 2}", i * 32 + 16 * (c // 2))
                A(x2_cols[:, c % 2, 0, 4 * h:4 * h + 4, :].rearrange("p c t -> p (c t)"), u[:, h * HALF:(h + 1) * HALF],
                  ACT.Copy, scale=t_pair[:, c % 4, 0:1]).then_inc(sem("hi_ready"), 1)

            def rank_low(i, c):
                wait(act, "z_psum", at(i, c, 1, 1))
                A(z_lo[:, :], ps_small[64:ZW, 256:384], ACT.Copy, scale=t_pair[64:ZW, c % 4, 1:2]).then_inc(sem("z_lo_ready"), 1)

            def body(i, c, on):
                if on(-1):
                    tokens_sb(i, c - 1)
                if on(-3):
                    rank_low(i, c - 3)
                if on(1):
                    phase_rows(i, c + 1, 0)
                if on(-2):
                    high(i, c - 2, 0)
                if on(0):
                    scale_rows(i, c)
                if on(1):
                    phase_rows(i, c + 1, 1)
                if on(-2):
                    high(i, c - 2, 1)

            act.wait_ge(sem("x_ph_zeroed"), 2)
            act.wait_ge(sem("z_w_ready"), 1)
            bodies(act, body)

            act.wait_ge(sem("gate_in_ready"), 1)
            A(gate[:, 3], gate[:, 2], ACT.Exp).then_inc(sem("gate_exp_ready"), 1)
            act.wait_ge(sem("gate_in_ready"), 2)
            A(gate[:, 5], gate[:, 5], ACT.Exp, scale=-2.0).then_inc(sem("gate_exp_ready"), 1)
            act.wait_ge(sem("gateT_psum"), 1)
            for s in range(2):
                act.wait_ge(sem(f"x2_saved{s}"), 16 * (NT // 2))
            A(gateT[:, :], bank(4, 4)[0:E, :], ACT.Copy).then_inc(sem("gateT_ready"), 1)

            def store(i, c):
                wait(act, "out_ready", at(i, c, 2, 2))
                act.dma_start(out_t[at(i, c)], o_sb[:, c % 2, :]).then_inc(sem(f"out_saved{c % 2}"), 16)

            with act.Fori(0, NT // 4) as i:
                for c in range(4):
                    store(i, c)
            for s in range(2):
                act.wait_ge(sem(f"out_saved{s}"), 16 * (NT // 2))

        @block.gpsimd
        def _(pool):
            g = nc.gpsimd
            g.memset(ident[:, :], 0.0).then_inc(sem("ident_zero"), 1)
            g.memset(identb[:, :], 0.0).then_inc(sem("ident_zero"), 1)
            g.memset(set_rows[:, :], 1.0).then_inc(sem("ident_zero"), 1)
            pool.wait_ge(sem("ident_zero"), 3)
            for m in (ident, identb):
                g.affine_select(out=m[:, :], in_=m[:, :], compare_op=ALU.not_equal, fill=1.0, base=0,
                                pattern=[[-1, P]], channel_multiplier=1).then_inc(sem("ident_ready"), 1)
            g.affine_select(out=set_rows[:, :], in_=set_rows[:, :], compare_op=ALU.is_ge, fill=0.0, base=0,
                            pattern=[[1, P]], channel_multiplier=-CG).then_inc(sem("set_rows_half"), 1)
            pool.wait_ge(sem("set_rows_half"), 1)
            g.affine_select(out=set_rows[:, :], in_=set_rows[:, :], compare_op=ALU.is_ge, fill=0.0, base=CG - 1,
                            pattern=[[-1, P]], channel_multiplier=CG).then_inc(sem("ident_ready"), 1)
            for e in range(2):
                g.memset(mixT[e * CH:(e + 1) * CH, :, (1 - e) * CH:(2 - e) * CH], 0.0).then_inc(sem("mixT_zeroed"), 1)
                pool.wait_ge(sem("mixT_zeroed"), e + 1)
            g.memset(conv_w[:, :, :, :], 0.0).then_inc(sem("conv_w_zeroed"), 1)
            pool.wait_ge(sem("conv_w_zeroed"), 1)
            g.memset(x_ph[0:64, :, :, MB:MB + 1], 0.0).then_inc(sem("x_ph_zeroed"), 1)
            pool.wait_ge(sem("x_ph_zeroed"), 1)
            g.memset(x_ph[64:128, :, :, 0:1], 0.0).then_inc(sem("x_ph_zeroed"), 1)
            pool.wait_ge(sem("x_ph_zeroed"), 2)
            pool.wait_ge(sem("w_max_ready"), 2)
            g.partition_all_reduce(scal[:, 8:10], scal[:, 0:2], P, RMAX).then_inc(sem("w_max_all"), 1)
            pool.wait_ge(sem("mix_max_ready"), 1)
            g.partition_all_reduce(scal[:, 10:11], scal[:, 6:7], P, RMAX).then_inc(sem("mix_max_all"), 1)

            def tile_max(i, c):
                wait(pool, "x1max_ready", at(i, c, 1, 1))
                wait(pool, "t_ready", at(i, c))
                g.tensor_tensor(pool_turn[:, 1:2], pool_turn[:, 0:1], pool_turn[:, 0:1], ALU.add)
                g.partition_all_reduce(x1max_all[:, :], x1max[:, :], P, RMAX).then_inc(sem("x1max_all_ready"), 1)

            def with_bias(i, c):
                wait(pool, "x1_ready", at(i, c, 2, 2))
                if not isinstance(i, int) or 4 * i + c >= 2:
                    wait(pool, f"xb_saved{c % 2}", i * 32 + 16 * (c // 2))
                g.tensor_tensor(xb[:, c % 2, :], x1[:, c % 2, :], bias_b[:, :], ALU.add).then_inc(sem("xb_ready"), 1)

            def add_layer0(i, c, h):
                wait(pool, "f_ready", at(i, c, 2, h + 1))
                if h == 0:
                    wait(pool, "mix_ready", at(i, c, 2, -2))
                    wait(pool, "x1max_ready", at(i, c, 1, -1))
                s = slice(h * HALF, (h + 1) * HALF)
                g.tensor_tensor(x1[:, c % 2, s], x_in[:, c % 4, s], f16[:, s], ALU.add).then_inc(sem("x1_ready"), 1)

            def body(i, c, on):
                if on(-2):
                    tile_max(i, c - 2)
                    with_bias(i, c - 2)
                if on(-1):
                    add_layer0(i, c - 1, 0)
                    add_layer0(i, c - 1, 1)

            g.memset(pool_turn[:, :], 0.0).then_inc(sem("pool_turn_ready"), 1)
            pool.wait_ge(sem("pool_turn_ready"), 1)
            pool.wait_ge(sem("bias_loaded"), 16)
            pool.wait_ge(sem("w_lo_ready"), NL)
            bodies(pool, body)

            pool.wait_ge(sem("gmax_ready"), 2)
            g.partition_all_reduce(gmx[:, 2:4], gmx[:, 0:2], P, RMAX).then_inc(sem("gmax_all"), 1)

        @block.vector
        def _(dve):
            v = nc.vector
            chain = [0]

            def link(ins):
                chain[0] += 1
                ins.then_inc(sem("vector_chain"), 1)
                dve.wait_ge(sem("vector_chain"), chain[0])

            dve.wait_ge(sem("ident_ready"), 3)
            v.tensor_reduce(chan_mask[:, :], ident[:, :].rearrange("p (s c) -> p c s", c=CG), AX.X, ALU.add).then_inc(sem("masks_ready"), 1)
            dve.wait_ge(sem("ctx_psum"), 1)
            dve.wait_ge(sem("fside_loaded"), 16 * PH)
            v.tensor_tensor(ybias[:, :, :].rearrange("p b g -> p g b"), ps_small[:, 128:128 + GRP * B].rearrange("p (g b) -> p g b", g=GRP),
                            fside_b[:, :].unsqueeze(2).to_broadcast([P, GRP, B]), ALU.add).then_inc(sem("ybias_ready"), 1)
            dve.wait_ge(sem("mlp_psum"), 3)
            v.tensor_tensor(att[:, :], ps_mix[0:B, 128:128 + NK], mb2_b[:, :], ALU.add).then_inc(sem("att_logits_ready"), 1)
            dve.wait_ge(sem("att_logits_ready"), 1)
            v.tensor_reduce(att_s[:, 0:1], att[:, :], AX.X, ALU.max, negate=True).then_inc(sem("att_logits_ready"), 1)
            dve.wait_ge(sem("att_exp_ready"), 1)
            link(v.tensor_reduce(att_s[:, 1:2], att_e[:, :], AX.X, ALU.add))
            link(v.reciprocal(att_s[:, 2:3], att_s[:, 1:2]))
            v.tensor_scalar(att[:, :], att_e[:, :], att_s[:, 2:3], None, ALU.mult).then_inc(sem("att_ready"), 1)
            for o in range(NL):
                if o % 4 == 0:
                    dve.wait_ge(sem(f"wq_loaded{o // 4}"), 16)
                link(v.tensor_reduce(wq_max[:, o:o + 1], wq_nat[:, o * L:(o + 1) * L], AX.X, ALU.max, apply_absolute_value=True))
                link(v.tensor_scalar(wq_scale[:, o:o + 1], wq_max[:, o:o + 1], 1.0 / QMAX, 1e-30, ALU.mult, ALU.max))
                v.reciprocal(wq_inv[:, o:o + 1], wq_scale[:, o:o + 1]).then_inc(sem("wq_inv_ready"), 1)
                dve.wait_ge(sem("wq_scaled"), o + 1)
                if o >= 2:
                    dve.wait_ge(sem("wqT_psum"), o - 1)
                q = yq if o % 2 == 0 else yqT
                v.tensor_scalar(q[:, :, :].rearrange("p a b -> p (a b)"), yv[:, :, :].rearrange("p a b -> p (a b)"),
                                MAGIC, -MAGIC, ALU.add, ALU.add).then_inc(sem("wq_ready"), 1)
            for n in (0, 2):
                dve.wait_ge(sem("mix_psum"), n + 1)
                for e in range(2):
                    v.tensor_copy(mix_block(n, e), mix_bank(n, e)).then_inc(sem("mixT_ready"), 1)
            for j, n in enumerate((4, 5, 6, 7, 0, 1, 2, 3)):
                dve.wait_ge(sem("mixb_psum"), j + 1)
                v.tensor_copy(mixb_all[:, 4 * n:4 * n + 4, :].rearrange("p t c -> p (t c)"), bank(n)).then_inc(sem("mixb_ready"), 1)
            dve.wait_ge(sem("mixT_ready"), 8)
            dve.wait_ge(sem("mixT_zeroed"), 2)
            dve.wait_ge(sem("mixb_ready"), 8)
            v.tensor_reduce(scal[:, 6:7], mixT[:, :, :], AX.XY, ALU.max, apply_absolute_value=True).then_inc(sem("mix_max_ready"), 1)
            link(v.tensor_reduce(scal[:, 7:8], mixb_all[:, :, :], AX.XY, ALU.max, apply_absolute_value=True))
            dve.wait_ge(sem("w_loaded"), 16)
            v.tensor_reduce(scal[:, 0:1], stage[:, :], AX.X, ALU.max, apply_absolute_value=True).then_inc(sem("w_max_ready"), 1)
            dve.wait_ge(sem("a_loaded"), 16)
            v.tensor_reduce(scal[:, 1:2], a_nat[:, :, :], AX.XY, ALU.max, apply_absolute_value=True).then_inc(sem("w_max_ready"), 1)
            dve.wait_ge(sem("w_max_all"), 1)
            link(v.tensor_scalar(scal[:, 8:10], scal[:, 8:10], 1e-20, None, ALU.max))
            link(v.tensor_scalar(scal[:, 8:10].bitcast(U32), scal[:, 8:10].bitcast(U32), EXPMASK, None, ALU.bitwise_and))
            v.tensor_scalar(scal[:, 2:4].bitcast(I32), scal[:, 8:10].bitcast(I32), -1.0, float((254 + TOP) << 23),
                            ALU.mult, ALU.add).then_inc(sem("w_scale_ready"), 1)
            v.tensor_scalar(scal[:, 4:6].bitcast(I32), scal[:, 8:10].bitcast(I32), float(-(TOP << 23)), None,
                            ALU.add).then_inc(sem("w_scale_ready"), 1)
            dve.wait_ge(sem("w_scale_ready"), 2)
            for c in range(NL):
                dve.wait_ge(sem("w_hi_ready"), c + 1)
                bk = ps_conv if c % 2 == 0 else ps_acc
                v.scalar_tensor_tensor(ffn_wT[:, 1, c, :], bk, scal[:, 2:3], ffn_wT[:, 0, c, :], ALU.mult, ALU.subtract).then_inc(sem("w_lo_ready"), 1)
            dve.wait_ge(sem("w_lo_ready"), NL)
            link(v.memset(z_w[:, :, :], 0.0))
            link(v.tensor_scalar(z_w[:, :, 0:R], a_nat[:, :, :], scal[:, 3:4], None, ALU.mult))
            v.scalar_tensor_tensor(z_w[:, :, 64:64 + R], a_nat[:, :, :], scal[:, 3:4], z_w[:, :, 0:R], ALU.mult, ALU.subtract)
            v.tensor_copy(z_w[:, :, R:R + E], ffn_wT[:, 0, :, 0:E])
            v.tensor_copy(z_w[:, :, 64 + R:64 + R + E], ffn_wT[:, 1, :, 0:E]).then_inc(sem("z_w_ready"), 1)
            dve.wait_ge(sem("limes_loaded"), 32)
            link(v.tensor_scalar(b_rank[:, :], b_rank[:, :], scal[0:R, 2:3], 16.0 / R, ALU.mult, ALU.mult))
            link(v.tensor_scalar(b_rank[:, :], b_rank[:, :], scal[0:R, 5:6], None, ALU.mult))
            dve.wait_ge(sem("mix_max_all"), 1)
            link(v.tensor_scalar(scal[:, 11:12], scal[:, 10:11], float(CH), None, ALU.mult))
            link(v.tensor_scalar(scal[:, 12:13], scal[:, 7:8], 1e-20, None, ALU.add))

            def blocks(i, c):
                wait(dve, f"x_loaded{c % 4}", i * 16 + 16 * (c // 4 + 1))
                wait(dve, "ph_psum", at(i, c, 2, 0))
                for a in range(4):
                    last = v.transpose(x_blk[:, a].rearrange("p s e c -> p e s c"),
                                       x_in[:, c % 4, a * 256:(a + 1) * 256].rearrange("p (m e) -> p e m", e=PH))
                last.then_inc(sem("blk_ready"), 1)

            def tile_bound(i, c):
                wait(dve, "x1_ready", at(i, c, 2, 2))
                wait(dve, "x1max_all_ready", at(i, c))
                v.tensor_reduce(x1max[:, :], x1[:, c % 2, :], AX.X, ALU.max, apply_absolute_value=True).then_inc(sem("x1max_ready"), 1)

            def conv_bias(i, c):
                wait(dve, "conv_ready", at(i, c, 1, 1))
                wait(dve, "yv_ready", at(i, c))
                v.tensor_tensor(yb[:, :, :].rearrange("p (b g) m -> p b g m", b=2), ps_conv.rearrange("p (g b m) -> p b g m", g=GRP, b=2),
                                ybias[:, bass.ds(at(i, c, 2), 2), :].unsqueeze(3).to_broadcast([P, 2, GRP, MB]), ALU.add).then_inc(sem("yb_ready"), 1)
                wait(dve, "yb_ready", at(i, c, 1, 1))
                v.tensor_reduce(rowmax[:, :], yb[:, :, :], AX.X, ALU.max, apply_absolute_value=True).then_inc(sem("rowmax_ready"), 1)

            def tile_scale(i, c):
                wait(dve, "x1max_all_ready", at(i, c, 1, 1))
                v.tensor_scalar(bound[:, 0:1], x1max_all[:, :], scal[:, 11:12], scal[:, 12:13], ALU.mult, ALU.add).then_inc(sem("bound_ready"), 1)
                wait(dve, "bound_ready", at(i, c, 2, 1))
                v.tensor_scalar(bound[:, 1:2].bitcast(U32), bound[:, 0:1].bitcast(U32), EXPMASK, None, ALU.bitwise_and).then_inc(sem("bound_ready"), 1)
                wait(dve, "bound_ready", at(i, c, 2, 2))
                v.tensor_scalar(t_pair[:, c % 4, 0:1].bitcast(I32), bound[:, 1:2].bitcast(I32), -1.0, float((254 + TOP) << 23), ALU.mult, ALU.add).then_inc(sem("t_half"), 1)
                v.tensor_scalar(t_pair[:, c % 4, 1:2].bitcast(I32), bound[:, 1:2].bitcast(I32), float(-(TOP << 23)), None, ALU.add).then_inc(sem("t_half"), 1)
                wait(dve, "t_half", at(i, c, 2, 2))
                v.tensor_copy(t_all[:, at(i, c), :], t_pair[:, c % 4, :]).then_inc(sem("t_ready"), 1)

            def rank_out(i, c):
                wait(dve, "z_lo_ready", at(i, c, 1, 1))
                v.scalar_tensor_tensor(zT[0:R + E, bass.ds(at(i, c, P), P)], ps_small[0:R + E, 256:384], t_pair[0:R + E, c % 4, 1:2],
                                       z_lo[:, :], ALU.mult, ALU.add).then_inc(sem("z_ready"), 1)

            def chan_max(i, c):
                wait(dve, "rowmaxT_ready", at(i, c, 1, 1))
                v.tensor_reduce(chanmax[:, :], ps_small[0:8, 0:P].rearrange("p (a c) -> p c a", a=PH), AX.X, ALU.max).then_inc(sem("chanmax_half"), 1)
                wait(dve, "chanmax_half", at(i, c, 1, 1))
                v.tensor_copy(chanmax_rep[:, :, :], chanmax[:, :].unsqueeze(1).to_broadcast([8, PH, CG])).then_inc(sem("chanmax_ready"), 1)

            def scales(i, c):
                wait(dve, "max_psum", at(i, c, 1, 1))
                v.tensor_scalar(yscale[:, :], ps_small[:, 128:136], 1.0 / QMAX, 1e-30, ALU.mult, ALU.max).then_inc(sem("yscale_ready"), 1)
                v.tensor_tensor_reduce(tok_junk[:, :], ps_small[:, 144:144 + CG], chan_mask[:, :], scale=1.0 / QMAX, scalar=0.0,
                                       op0=ALU.mult, op1=ALU.add, accum_out=tok_scale[:, c % 4:c % 4 + 1]).then_inc(sem("tok_scale_ready"), 1)
                wait(dve, "yscale_ready", at(i, c, 1, 1))
                wait(dve, "yv_ready", at(i, c))
                v.reciprocal(yinv[:, :], yscale[:, :]).then_inc(sem("yinv_ready"), 1)

            def mixed(i, c, h):
                wait(dve, "mix_ready", at(i, c, 2, h + 1))
                wait(dve, "hi_ready", at(i, c, 2, h - 1))
                v.tensor_tensor(u[:, h * HALF:(h + 1) * HALF].rearrange("p (k t) -> p k t", k=4),
                                ps_mix.rearrange("p (k t) -> p k t", k=4),
                                mixb_all[:, bass.ds(at(i, c), 1), :].to_broadcast([P, 4, P]), ALU.add).then_inc(sem("u_ready"), 1)

            def low(i, c, h):
                wait(dve, "hi_ready", at(i, c, 2, h + 1))
                v.scalar_tensor_tensor(x2_cols[:, c % 2, 1, 4 * h:4 * h + 4, :].rearrange("p k t -> p (k t)"), u[:, h * HALF:(h + 1) * HALF],
                                       t_pair[:, c % 4, 0:1], x2_cols[:, c % 2, 0, 4 * h:4 * h + 4, :].rearrange("p k t -> p (k t)"),
                                       ALU.mult, ALU.subtract).then_inc(sem("lo_ready"), 1)

            def layer0(i, c, h):
                wait(dve, "acc_ready", at(i, c, 2, h + 1))
                wait(dve, "tok_scale_ready", at(i, c, 1, 1))
                wait(dve, "x1_ready", at(i, c, 2, h - 1))
                s = slice(h * HALF, (h + 1) * HALF)
                v.scalar_tensor_tensor(f16[:, s], ps_acc[:, s], tok_scale[:, c % 4:c % 4 + 1], wsc_b[:, s], ALU.mult, ALU.mult).then_inc(sem("f_ready"), 1)

            def rounded(i, c):
                wait(dve, "yv_ready", at(i, c, 1, 1))
                wait(dve, "yqT_psum", at(i, c))
                v.tensor_scalar(yq[:, :, :].rearrange("p s m -> p (s m)"), yv[:, :, :].rearrange("p s m -> p (s m)"), MAGIC, -MAGIC,
                                ALU.add, ALU.add).then_inc(sem("yq_ready"), 1)

            def body(i, c, on):
                if on(1):
                    blocks(i, c + 1)
                if on(-2):
                    tile_bound(i, c - 2)
                if on(0):
                    conv_bias(i, c)
                if on(-2):
                    tile_scale(i, c - 2)
                if on(-3):
                    rank_out(i, c - 3)
                if on(0):
                    chan_max(i, c)
                if on(-2):
                    mixed(i, c - 2, 0)
                if on(0):
                    scales(i, c)
                if on(-2):
                    low(i, c - 2, 0)
                if on(-1):
                    layer0(i, c - 1, 0)
                if on(0):
                    rounded(i, c)
                if on(-2):
                    mixed(i, c - 2, 1)
                if on(-1):
                    layer0(i, c - 1, 1)
                if on(-2):
                    low(i, c - 2, 1)

            bodies(dve, body)

            ps_g = bank(4, 4)
            dve.wait_ge(sem("logits_psum"), 1)
            h_log, d_log, lg, ex, pr, mk, wt, gt = (gate[:, n] for n in range(8))
            flat = lambda a: a.rearrange("p j e -> p (j e)")
            link(v.tensor_scalar(flat(h_log), ps_g[:, 0:NJ * E], scal[:, 4:5], None, ALU.mult))
            link(v.tensor_tensor(h_log, h_log, bias_b[:, 0:E].unsqueeze(1).to_broadcast([P, NJ, E]), ALU.add))
            v.tensor_scalar(flat(d_log), ps_g[:, 512:512 + NJ * E], scal[:, 5:6], None, ALU.mult).then_inc(sem("logits_read"), 1)
            v.tensor_reduce(gmx[:, 0:1], h_log, AX.XY, ALU.max, apply_absolute_value=True).then_inc(sem("gmax_ready"), 1)
            dve.wait_ge(sem("logits_read"), 1)
            v.tensor_reduce(gmx[:, 1:2], d_log, AX.XY, ALU.max, apply_absolute_value=True).then_inc(sem("gmax_ready"), 1)
            dve.wait_ge(sem("gmax_all"), 1)
            link(v.tensor_scalar(gmx[:, 4:6], gmx[:, 2:4], 1e-6, None, ALU.max))
            link(v.reciprocal(gmx[:, 6:8], gmx[:, 4:6]))
            link(v.tensor_scalar(flat(h_log), flat(h_log), gmx[:, 6:7], 0.5, ALU.mult, ALU.mult))
            link(v.tensor_scalar(flat(d_log), flat(d_log), gmx[:, 7:8], 0.5, ALU.mult, ALU.mult))
            link(v.tensor_tensor(lg, h_log, d_log, ALU.add))
            link(v.tensor_reduce(gsm[:, 0, :], lg, AX.X, ALU.max))
            v.tensor_tensor(lg, lg, gsm[:, 0, :].unsqueeze(2).to_broadcast([P, NJ, E]), ALU.subtract).then_inc(sem("gate_in_ready"), 1)
            dve.wait_ge(sem("gate_exp_ready"), 1)
            link(v.tensor_reduce(gsm[:, 1, :], ex, AX.X, ALU.add))
            link(v.reciprocal(gsm[:, 2, :], gsm[:, 1, :]))
            link(v.tensor_tensor(pr, ex, gsm[:, 2, :].unsqueeze(2).to_broadcast([P, NJ, E]), ALU.mult))
            for j in range(NJ):
                last = v.max(top8[:, j, :], pr[:, j, :])
            link(last)
            v.tensor_tensor(mk, pr, top8[:, :, 1:2].to_broadcast([P, NJ, E]), ALU.subtract).then_inc(sem("gate_in_ready"), 1)
            dve.wait_ge(sem("gate_exp_ready"), 2)
            link(v.tensor_scalar(flat(mk), flat(mk), 1.0, None, ALU.add))
            link(v.reciprocal(flat(mk), flat(mk)))
            link(v.tensor_tensor(wt, pr, mk, ALU.mult))
            link(v.tensor_reduce(gsm[:, 3, :], wt, AX.X, ALU.add))
            link(v.tensor_scalar(gsm[:, 4, :], gsm[:, 3, :], 1e-9, None, ALU.add))
            link(v.reciprocal(gsm[:, 5, :], gsm[:, 4, :]))
            v.tensor_tensor(gt, wt, gsm[:, 5, :].unsqueeze(2).to_broadcast([P, NJ, E]), ALU.mult).then_inc(sem("gate_ready"), 1)
            link(v.tensor_scalar(unscale[:, :], t_all[:, :, 1], scal[:, 4:5], None, ALU.mult))
            for k in range(4):
                dve.wait_ge(sem("pmix_psum"), k + 1)
                zk = zT[0:R, k * 1024:(k + 1) * 1024].rearrange("p (a e) -> p a e", e=2)
                link(v.tensor_tensor(zk, zk, ps_g[0:R, k * 512:(k + 1) * 512].unsqueeze(2).to_broadcast([R, 512, 2]), ALU.mult))

            def rank_cols(i, c):
                wait(dve, "h_ready", at(i, c, 1, -1))
                v.tensor_scalar(z_scaled[:, c % 2, :], zT[0:R, bass.ds(at(i, c, P), P)], t_all[0:R, at(i, c), 0:1], None,
                                ALU.mult).then_inc(sem("z_scaled_ready"), 1)

            def finish(i, c):
                wait(dve, "h_ready", at(i, c, 1, 1))
                wait(dve, f"xb_loaded{c % 4}", i * 16 + 16 * (c // 4 + 1))
                if not isinstance(i, int) or 4 * i + c >= 2:
                    wait(dve, f"out_saved{c % 2}", i * 32 + 16 * (c // 2))
                for h in range(2):
                    s = slice(h * HALF, (h + 1) * HALF)
                    v.scalar_tensor_tensor(o_sb[:, c % 2, s], bank(2 * (c % 2) + h), unscale[:, bass.ds(at(i, c), 1)], xb_in[:, c % 4, s],
                                           ALU.mult, ALU.add).then_inc(sem("out_ready"), 1)

            rank_cols(0, 0)
            rank_cols(0, 1)
            for c in range(2, 6):
                finish(0, c - 2)
                rank_cols(0, c)
            with dve.Fori(1, NT // 4 - 1) as i:
                for c in range(2, 6):
                    finish(i, c - 2)
                    rank_cols(i, c)
            n = NT // 4 - 1
            finish(n, 0)
            rank_cols(n, 2)
            finish(n, 1)
            rank_cols(n, 3)
            finish(n, 2)
            finish(n, 3)


_INS = ['x', 'cond_128', 'fside_S_0', 'L0_cond_weight', 'L0_cond_c_weight', 'L0_ffn_weight', 'L1_cond_W0', 'L1_cond_b0',
        'L1_cond_W1', 'L1_cond_b1', 'L1_cond_W2', 'L1_cond_b2', 'L1_cond_weight', 'L1_cond_bias_k', 'L1_ffn_W', 'L1_ffn_b',
        'L1_ffn_A', 'L1_ffn_Bmat', 'L1_ffn_LiMEs']


def kernel(**inputs):
    import numpy as _np
    import concourse.bacc as _bacc
    from concourse import mybir as _mybir
    from concourse.bass_utils import run_bass_kernel_spmd as _run

    nc = _bacc.Bacc("TRN2", target_bir_lowering=False, num_devices=1)
    arrays, args = {}, []
    for name in _INS:
        a = _np.ascontiguousarray(inputs[name])
        arrays[f"in_{name}"] = a
        args.append(nc.dram_tensor(f"in_{name}", a.shape, _mybir.dt.from_np(a.dtype), kind="ExternalInput").ap())
    args.append(nc.dram_tensor("out", (B, CH, L), F32, kind="ExternalOutput").ap())
    program(nc, *args)
    r = _run(nc, [arrays], core_ids=[0])
    return r.results[0]["out"]
```

```python
from contextlib import ExitStack

import numpy as np
import concourse.bass as bass
from concourse import mybir

F32 = mybir.dt.float32
F16 = mybir.dt.float16
BF16 = mybir.dt.bfloat16
U32 = mybir.dt.uint32
I32 = mybir.dt.int32
ALU = mybir.AluOpType
ACT = mybir.ActivationFunctionType
AX = mybir.AxisListType
RMAX = bass.bass_isa.ReduceOp.absmax

P = 128
B, CH, L = 64, 64, 1024
GRP, CG = 4, 16
TAPS = 9
PH = 8
MB = L // PH
NT = B // 2
NL = L // P
HALF = L // 2
NK, HID = 8, 128
R, E = 32, 8
NTOK = B * CH
NANCH = NTOK // 2
NJ = NANCH // P
ZW = 64 + R + E
QMAX = 127.0
MAGIC = 12582912.0
EXPMASK = 0x7F800000
TOP = 13


def program(nc, x, cond, fside, w_conv, w_ctx, w_q, mlp_w0, mlp_b0, mlp_w1, mlp_b1, mlp_w2, mlp_b2,
            mix_w, mix_b, w_ffn, b_ffn, w_a, w_b, limes, out):
    ctx = ExitStack()
    with ctx:
        ctx.enter_context(nc.allow_non_contiguous_dma(reason="small weights"))

        def sb(name, shape, dt):
            return ctx.enter_context(nc.sbuf_tensor(name, shape, dt))

        sems = {}

        def sem(name):
            if name not in sems:
                sems[name] = ctx.enter_context(nc.semaphore(name))
            return sems[name]

        ffn_wT = sb("ffn_wT", [P, 2, NL, L], F16)
        wq_nat = ffn_wT[:, :, :, :].rearrange("p a c l -> p (a c l)").bitcast(F32)
        stage = sb("stage", [P, NL * L], F32)
        w_nat = stage[:, :].rearrange("p (a l) -> p a l", a=NL)
        zT = stage[:, 0:NTOK]
        x2_cols = stage[:, NTOK:NTOK + 2 * L].bitcast(F16).rearrange("p (s h c t) -> p s h c t", s=2, h=2, c=NL)
        xb = stage[:, NTOK + 2 * L:NTOK + 4 * L].rearrange("p (s l) -> p s l", s=2)
        wqT = sb("wqT", [P, PH, L], BF16)
        mixT = sb("mixT", [P, NT, P], F32)
        mixb_all = sb("mixb_all", [P, NT, P], F32)
        kw = mixb_all[0:NK, :, :].rearrange("k a t -> k (a t)").rearrange("k (o i) -> k o i", o=CH)
        x_in = sb("x_in", [P, 4, L], F32)
        x_blk = sb("x_blk", [P, 4, 2, PH, CG], F32)
        x_ph = sb("x_ph", [P, 2, GRP, MB + 1], F32)
        yb = sb("yb", [P, 2, 8, MB], F32)
        yv = sb("yv", [P, 8, MB], F32)
        yq = sb("yq", [P, 8, MB], BF16)
        yqT = sb("yqT", [P, PH, P], BF16)
        f16 = sb("f16", [P, L], F16)
        x1 = sb("x1", [P, 2, L], F32)
        u = sb("u", [P, L], F32)
        wsc_b = sb("wsc_b", [P, L], F32)
        bias_b = sb("bias_b", [P, L], F32)
        ident = sb("ident", [P, P], F32)
        identb = sb("identb", [P, P], BF16)
        conv_wT = sb("conv_wT", [CG, GRP, TAPS, CG], F32)
        conv_w = sb("conv_w", [P, GRP, 16, CG], F32)
        w_conv_nat = sb("w_conv_nat", [CH, CG, TAPS], F32)
        ybias = sb("ybias", [P, B, GRP], F32)
        fside_b = sb("fside_b", [P, GRP], F32)
        cond_nat = sb("cond_nat", [B, P], F32)
        condT = sb("condT", [P, B], F32)
        w_ctx_nat = sb("w_ctx_nat", [CH, P], F32)
        w_ctxT = sb("w_ctxT", [P, CH], F32)
        w_ctx_rep = sb("w_ctx_rep", [P, GRP, PH, CG], F32)
        mw0 = sb("mw0", [P, HID], F32)
        mw1 = sb("mw1", [HID, HID], F32)
        mw2 = sb("mw2", [HID, NK], F32)
        mb01 = sb("mb01", [HID, 2], F32)
        mb2_b = sb("mb2_b", [B, NK], F32)
        mixb_k = sb("mixb_k", [NK, CH], F32)
        h0 = sb("h0", [HID, B], F32)
        h1 = sb("h1", [HID, B], F32)
        att = sb("att", [B, NK], F32)
        att_e = sb("att_e", [B, NK], F32)
        att_s = sb("att_s", [B, 4], F32)
        attT = sb("attT", [NK, B], F32)
        chan_mask = sb("chan_mask", [P, CG], F32)
        set_rows = sb("set_rows", [8, P], F32)
        wq_max = sb("wq_max", [P, NL], F32)
        wq_scale = sb("wq_scale", [P, NL], F32)
        wq_inv = sb("wq_inv", [P, NL], F32)
        a_nat = sb("a_nat", [P, NL, R], F32)
        z_w = sb("z_w", [P, NL, ZW], F16)
        scal = sb("scal", [P, 16], F32)
        w_max = sb("w_max", [P, 4], F32)
        w_exp = sb("w_exp", [P, 4], F32)
        w_up = sb("w_up", [P, 4], F32)
        w_down = sb("w_down", [P, 4], F32)
        rowmax = sb("rowmax", [P, 8], F32)
        chanmax = sb("chanmax", [8, CG], F32)
        chanmax_rep = sb("chanmax_rep", [8, PH, CG], F32)
        yscale = sb("yscale", [P, 8], F32)
        yinv = sb("yinv", [P, 8], F32)
        tok_junk = sb("tok_junk", [P, CG], F32)
        tok_scale = sb("tok_scale", [P, 4], F32)
        abs_junk = sb("abs_junk", [P, L], BF16)
        x1max = sb("x1max", [P, 1], F32)
        x1max_all = sb("x1max_all", [P, 1], F32)
        pool_turn = sb("pool_turn", [1, 2], F32)
        bound = sb("bound", [P, 2], F32)
        t_pair = sb("t_pair", [P, 4, 2], F32)
        t_all = sb("t_all", [P, NT, 2], F32)
        z_lo = sb("z_lo", [R + E, P], F32)
        limes_nat = sb("limes_nat", [E, R], F32)
        limesT = sb("limesT", [R, E], F32)
        limes_n = sb("limes_n", [E, R], F32)
        b_rank = x_blk[0:R].rearrange("p a s e c -> p (a s e c)")
        b_parts = sb("b_parts", [3 * R, L], F16)
        z_scaled = sb("z_scaled", [R, 2, P], F32)
        z_parts = sb("z_parts", [3 * R, 2, P], F16)
        z_max = sb("z_max", [P, NT], F32)
        z_exp = sb("z_exp", [P, NT], F32)
        z_up = sb("z_up", [P, NT], F32)
        unscale_d = sb("unscale_d", [P, NT], F32)
        gsm = sb("gsm", [P, 6, NJ], F32)
        gmx = sb("gmx", [P, 8], F32)
        gateT = stage[0:E, NTOK:NTOK + NANCH]
        unscale = sb("unscale", [P, NT], F32)
        gate = yb[:, 0].rearrange("p n (j e) -> p n j e", e=E)
        top8 = yb[:, 1, 0, :].rearrange("p (j e) -> p j e", e=E)
        x2_in = x_in[:, :, :].rearrange("p s l -> p (s l)").bitcast(F16).rearrange(
            "p (s h c t) -> p s h c t", s=4, h=2, c=NL)
        xb_in = mixb_all[:, :, :].rearrange("p a t -> p (a t)").rearrange("p (s l) -> p s l", s=4)
        o_sb = x1

        ps = ctx.enter_context(nc.psum_tensor("ps", [P, 8 * 512], F32))

        def bank(n, k=1):
            return ps[:, n * 512:(n + k) * 512]

        ps_ph, ps_conv, ps_acc, ps_mix, ps_tr, ps_small = bank(0), bank(1, 2), bank(3, 2), bank(5), bank(6), bank(7)
        ps_trb = ps_tr.bitcast(BF16)

        x2_dram = nc.dram_tensor("x2_scratch", [NT, P, 2 * L], F16, kind="Internal").ap()
        xb_dram = nc.dram_tensor("xb_scratch", [NT, P, L], F32, kind="Internal").ap()

        def mix_bank(n, e):
            return bank(n)[e * CH:(e + 1) * CH, :].rearrange("p (o t) -> p o t", t=NT)

        def mix_block(n, e):
            return mixT[e * CH:(e + 1) * CH, :, e * CH + 16 * n:e * CH + 16 * n + 16].rearrange("p t o -> p o t")

        x_t = x.rearrange("(t b) c l -> t (b c) l", b=2)
        out_t = out.rearrange("(t b) c l -> t (b c) l", b=2)

        block = ctx.enter_context(nc.Block())

        def at(i, c, k=1, d=0):
            return i * (4 * k) + (k * c + d)

        def wait(eng, name, val):
            if not isinstance(val, int) or val > 0:
                eng.wait_ge(sem(name), val)

        def bodies(eng, body):
            first = 5
            n = (NT - 1 - first) // 4
            for t in range(-1, first):
                body(0, t, lambda o, t=t: 0 <= t + o < NT)
            with eng.Fori(0, n) as i:
                for c in range(first, first + 4):
                    body(i, c, lambda o: True)
            for t in range(first + 4 * n, NT + 4):
                body(n, t - 4 * n, lambda o, t=t: 0 <= t + o < NT)

        @block.sync
        def _(sp):
            sp.dma_start(w_conv_nat[:, :, :], w_conv).then_inc(sem("conv_w_loaded"), 16)
            sp.dma_start(cond_nat[:, :], cond).then_inc(sem("cond_loaded"), 16)
            sp.dma_start(w_ctx_nat[:, :], w_ctx).then_inc(sem("cond_loaded"), 16)
            sp.dma_start(x_in[:, 0, :], x_t[0]).then_inc(sem("x_loaded0"), 16)
            for a in range(2):
                sp.dma_start(wq_nat.rearrange("p (a l) -> p a l", a=NL)[:, 4 * a:4 * a + 4, :],
                             w_q.rearrange("(a p) l -> p a l", p=P)[:, 4 * a:4 * a + 4, :]).then_inc(sem(f"wq_loaded{a}"), 16)
            for t in range(1, 4):
                sp.dma_start(x_in[:, t, :], x_t[t]).then_inc(sem(f"x_loaded{t}"), 16)
            sp.dma_start(w_nat, w_ffn.rearrange("(a p) l -> p a l", p=P)).then_inc(sem("w_loaded"), 16)
            sp.wait_ge(sem("conv_wT_ready"), 2)
            sp.wait_ge(sem("conv_w_zeroed"), 1)
            for p in range(PH):
                v = (p + 4) % PH
                sp.dma_start(conv_w[p * CG:(p + 1) * CG, :, v:v + TAPS, :], conv_wT[:, :, :, :]).then_inc(sem("conv_w_ready"), 16)

            def step(i, c, load=True, xb_out=True, x2_out=True):
                if load:
                    wait(sp, "x1_ready", at(i, c, 2, -6))
                    sp.dma_start(x_in[:, c % 4, :], x_t[at(i, c)]).then_inc(sem(f"x_loaded{c % 4}"), 16)
                if x2_out:
                    wait(sp, "lo_ready", at(i, c, 2, -8))
                    sp.dma_start(x2_dram[at(i, c, 1, -5)],
                                 x2_cols[:, (c + 1) % 2].rearrange("p h c t -> p (h c t)")).then_inc(sem(f"x2_saved{(c + 1) % 2}"), 16)
                if xb_out:
                    wait(sp, "xb_ready", at(i, c, 1, -3))
                    sp.dma_start(xb_dram[at(i, c, 1, -4)], xb[:, c % 2, :]).then_inc(sem(f"xb_saved{c % 2}"), 16)

            for c in range(4):
                step(1, c, x2_out=c >= 1)
            with sp.Fori(2, NT // 4) as i:
                for c in range(4):
                    step(i, c)
            for c in range(5):
                step(NT // 4, c, load=False, xb_out=c < 4)

            for s in range(2):
                sp.wait_ge(sem(f"x2_saved{s}"), 16 * (NT // 2))
                sp.wait_ge(sem(f"xb_saved{s}"), 16 * (NT // 2))

            def fetch(i, c):
                wait(sp, "h_ready", at(i, c, 1, -3))
                sp.dma_start(x2_in[:, c % 4].rearrange("p h c t -> p (h c t)"), x2_dram[at(i, c)]).then_inc(sem(f"x2_loaded{c % 4}"), 16)
                wait(sp, "out_ready", at(i, c, 2, -6))
                sp.dma_start(xb_in[:, c % 4, :], xb_dram[at(i, c)]).then_inc(sem(f"xb_loaded{c % 4}"), 16)

            for c in range(4):
                fetch(0, c)
            with sp.Fori(1, NT // 4) as i:
                for c in range(4):
                    fetch(i, c)

        @block.tensor
        def _(pe):
            mm, tr = nc.tensor.matmul, nc.tensor.transpose
            pe.wait_ge(sem("ident_ready"), 3)
            pe.wait_ge(sem("conv_w_loaded"), 16)
            for k in range(TAPS):
                last = tr(ps_conv[0:CG, (TAPS - 1 - k) * CH:(TAPS - k) * CH], w_conv_nat[:, :, k], ident[0:CH, 0:CH])
            last.then_inc(sem("conv_wT_psum"), 1)
            pe.wait_ge(sem("cond_loaded"), 32)
            tr(ps_small[:, 0:B], cond_nat[:, :], ident[0:B, 0:B])
            tr(ps_small[:, B:B + CH], w_ctx_nat[:, :], ident[0:CH, 0:CH]).then_inc(sem("condT_psum"), 1)
            pe.wait_ge(sem("condT_ready"), 3)
            for g in range(GRP):
                last = mm(ps_small[:, 128 + g * B:128 + (g + 1) * B], w_ctx_rep[:, g].rearrange("p a c -> p (a c)"),
                          condT[:, :], start=True, stop=True)
            last.then_inc(sem("ctx_psum"), 1)
            pe.wait_ge(sem("mlp_loaded"), 16 * 6)
            mm(ps_mix[:, 0:B], mw0[:, :], condT[:, :], start=True, stop=True).then_inc(sem("mlp_psum"), 1)
            pe.wait_ge(sem("h_act"), 1)
            mm(ps_mix[:, 64:64 + B], mw1[:, :], h0[:, :], start=True, stop=True).then_inc(sem("mlp_psum"), 1)
            pe.wait_ge(sem("h_act"), 2)
            mm(ps_mix[0:B, 128:128 + NK], h1[:, :], mw2[:, :], start=True, stop=True).then_inc(sem("mlp_psum"), 1)
            pe.wait_ge(sem("att_ready"), 1)
            tr(ps_mix[0:NK, 192:192 + B], att[:, :], ident[0:B, 0:B]).then_inc(sem("mlp_psum"), 1)
            for o in range(NL):
                pe.wait_ge(sem("wq_ready"), o + 1)
                if o >= 2:
                    pe.wait_ge(sem("wqT_ready"), o - 1)
                bk = (ps_tr if o % 2 == 0 else ps_ph).bitcast(BF16)
                q = yq if o % 2 == 0 else yqT
                qv = q[:, :, :].rearrange("p a b -> p (a b)").rearrange("p (m e) -> p e m", e=PH)
                for p in range(PH):
                    last = tr(bk[:, p * P:(p + 1) * P], qv[:, p, :], identb[:, :])
                last.then_inc(sem("wqT_psum"), 1)
            for o in range(NL):
                last = mm(ps_acc[:, o * P:(o + 1) * P], wq_scale[:, o:o + 1].to_broadcast([P, P]), ident[:, :], start=True, stop=True)
            last.then_inc(sem("wsc_psum"), 1)
            pe.wait_ge(sem("attT_ready"), 1)
            pe.wait_ge(sem("wsc_ready"), 1)
            pe.wait_ge(sem("wqT_ready"), NL)
            pe.wait_ge(sem("conv_wT_ready"), 2)
            pe.wait_ge(sem("ybias_ready"), 1)
            pe.wait_ge(sem("kw_loaded"), 16)
            for o in range(CH):
                for e in range(2):
                    last = mm(ps[e * CH:(e + 1) * CH, o * NT:(o + 1) * NT], kw[:, o, :], attT[:, e::2], start=True, stop=True)
                if o % 16 == 15:
                    last.then_inc(sem("mix_psum"), 1)
            pe.wait_ge(sem("mixb_loaded"), 16)
            for b in (*range(B // 2, B), *range(B // 2)):
                if b == 0:
                    pe.wait_ge(sem("mixT_ready"), 8)
                last = mm(ps[:, b * CH:(b + 1) * CH], attT[:, b:b + 1].to_broadcast([NK, P]), mixb_k[:, :], start=True, stop=True)
                if b % 8 == 7:
                    last.then_inc(sem("mixb_psum"), 1)
            pe.wait_ge(sem("w_loaded"), 16)
            for c in range(NL):
                if c < 2:
                    pe.wait_ge(sem("mixb_ready"), 8)
                else:
                    pe.wait_ge(sem("w_lo_ready"), c - 1)
                bk = ps_conv if c % 2 == 0 else ps_acc
                for o in range(NL):
                    last = tr(bk[:, o * P:(o + 1) * P], w_nat[:, o, c * P:(c + 1) * P], ident[:, :])
                last.then_inc(sem("wT_psum"), 1)
            pe.wait_ge(sem("limes_loaded"), 32)
            tr(ps_small[0:R, 0:E], limes_nat[:, :], ident[0:E, 0:E]).then_inc(sem("limesT_psum"), 1)
            pe.wait_ge(sem("limesT_ready"), 1)
            pe.wait_ge(sem("w_lo_ready"), NL)

            def phases(i, c, s):
                if s == 0:
                    wait(pe, "blk_ready", at(i, c, 1, 1))
                    wait(pe, "ph_ready", at(i, c, 4, 0))
                else:
                    wait(pe, "ph_ready", at(i, c, 4, 2))
                bk = ps_ph.rearrange("p (q m) -> p q m", q=4)
                for m in range(4):
                    last = tr(bk[:, :, m * 32:(m + 1) * 32], x_blk[:, m, s].rearrange("p e c -> p (e c)"), ident[:, :])
                last.then_inc(sem("ph_psum"), 1)

            def conv(i, c):
                wait(pe, "ph_ready", at(i, c, 4, 4))
                wait(pe, "yb_ready", at(i, c))
                for g in range(GRP):
                    o = ps_conv[:, g * 2 * MB:(g + 1) * 2 * MB]
                    w = conv_w[:, g].rearrange("p v c -> p (v c)")
                    xg = x_ph[:, g % 2, g // 2:GRP:2, :]
                    mm(o, w[:, P:2 * P], xg[:, :, 0:MB], start=True, stop=False)
                    last = mm(o, w[:, 0:P], xg[:, :, 1:MB + 1], start=False, stop=True)
                last.then_inc(sem("conv_ready"), 1)

            def max_rows(i, c):
                wait(pe, "rowmax_ready", at(i, c, 1, 1))
                wait(pe, "z_ready", at(i, c, 1, -3))
                tr(ps_small[0:8, 0:P], rowmax[:, :], ident[:, :]).then_inc(sem("rowmaxT_ready"), 1)

            def max_back(i, c):
                wait(pe, "chanmax_ready", at(i, c, 1, 1))
                mm(ps_small[:, 128:136], chanmax_rep[:, :, :].rearrange("p a c -> p (a c)"), ident[0:8, 0:8], start=True, stop=True)
                mm(ps_small[:, 144:144 + CG], set_rows[:, :], chanmax[:, :], start=True, stop=True).then_inc(sem("max_psum"), 1)

            def tokens_out(i, c):
                wait(pe, "yq_ready", at(i, c, 1, 1))
                for s in range(8):
                    last = tr(ps_trb[:, s * P:(s + 1) * P], yq[:, s, :], identb[:, :])
                last.then_inc(sem("yqT_psum"), 1)

            def int_product(i, c, h):
                wait(pe, "yqT_ready", at(i, c, 1, 1))
                wait(pe, "f_ready", at(i, c, 2, h - 1))
                for p in range(PH):
                    last = mm(ps_acc[:, h * HALF:(h + 1) * HALF], yqT[:, p, :], wqT[:, p, h * HALF:(h + 1) * HALF],
                              start=p == 0, stop=p == PH - 1)
                last.then_inc(sem("acc_ready"), 1)

            def mix(i, c, h):
                wait(pe, "x1_ready", at(i, c, 2, 1 + h))
                wait(pe, "u_ready", at(i, c, 2, h))
                for k in range(4):
                    ck = 4 * h + k
                    last = mm(ps_mix[:, k * P:(k + 1) * P], x1[:, c % 2, ck * P:(ck + 1) * P], mixT[:, at(i, c), :],
                              start=True, stop=True)
                last.then_inc(sem("mix_ready"), 1)

            def rank(i, c):
                wait(pe, "lo_ready", at(i, c, 2, 2))
                steps = at(i, c, 1, 4)
                wait(pe, "tok_scale_ready", min(steps, NT) if isinstance(steps, int) else steps)
                wait(pe, "z_ready", at(i, c))
                for k in range(NL):
                    mm(ps_small[0:ZW, 256:384], z_w[:, k, :], x2_cols[:, c % 2, 0, k, :], start=k == 0, stop=False, skip_group_check=True)
                for k in range(NL):
                    last = mm(ps_small[0:R + E, 256:384], z_w[:, k, 0:R + E], x2_cols[:, c % 2, 1, k, :],
                              start=False, stop=k == NL - 1, skip_group_check=True)
                last.then_inc(sem("z_psum"), 1)

            def body(i, c, on):
                if on(-3):
                    mix(i, c - 3, 0)
                if on(-1):
                    max_rows(i, c - 1)
                if on(0):
                    conv(i, c)
                if on(-1):
                    max_back(i, c - 1)
                if on(-3):
                    mix(i, c - 3, 1)
                if on(-2):
                    int_product(i, c - 2, 0)
                if on(-4):
                    rank(i, c - 4)
                if on(1):
                    phases(i, c + 1, 0)
                if on(-2):
                    int_product(i, c - 2, 1)
                if on(1):
                    phases(i, c + 1, 1)
                if on(-1):
                    tokens_out(i, c - 1)

            pe.wait_ge(sem("conv_w_ready"), 16 * PH)
            pe.wait_ge(sem("x_ph_zeroed"), 2)
            pe.wait_ge(sem("z_w_ready"), 1)
            bodies(pe, body)

            ps_h, ps_g = bank(0, 4), bank(4, 4)
            pe.wait_ge(sem("z_ready"), NT)
            anchors = zT.rearrange("p (j a e) -> p j a e", a=P, e=2)
            for j in range(NJ):
                mm(ps_g[:, j * E:(j + 1) * E], anchors[R:R + E, j, :, 1], ident[R:R + E, R:R + E], start=True, stop=True)
                last = mm(ps_g[:, 512 + j * E:512 + (j + 1) * E], anchors[0:R, j, :, 1], limesT[:, :], start=True, stop=True)
            last.then_inc(sem("logits_psum"), 1)

            def dense(i, c):
                wait(pe, f"x2_loaded{c % 4}", i * 16 + 16 * (c // 4 + 1))
                for h in range(2):
                    wait(pe, "out_ready", at(i, c, 2, h - 3))
                    o = ps_h[:, (c % 2) * L + h * HALF:(c % 2) * L + (h + 1) * HALF]
                    for k in range(NL):
                        for n, (a, w) in enumerate(((0, 0), (0, 1), (1, 0))):
                            mm(o, x2_in[:, c % 4, a, k, :], ffn_wT[:, w, k, h * HALF:(h + 1) * HALF],
                               start=k == 0 and n == 0, stop=k == NL - 1 and n == 2)

            def delta(i, c):
                wait(pe, "z_parts_ready", at(i, c, 1, 1))
                wait(pe, "out_ready", at(i, c, 2, -2))
                for h in range(2):
                    last = mm(bank(4 + 2 * (c % 2) + h), z_parts[:, c % 2, :], b_parts[:, h * HALF:(h + 1) * HALF], start=True, stop=True)
                last.then_inc(sem("h_ready"), 1)

            dense(0, 0)
            pe.wait_ge(sem("gate_ready"), 1)
            pe.wait_ge(sem("logits_read"), 1)
            for j in range(NJ):
                last = tr(ps_g[0:E, j * P:(j + 1) * P], gate[:, 7, j, :], ident[:, :])
            last.then_inc(sem("gateT_psum"), 1)
            dense(0, 1)
            pe.wait_ge(sem("gateT_ready"), 1)
            for k in range(4):
                mm(ps_g[0:R, k * 512:(k + 1) * 512], limes_n[:, :], gateT[:, k * 512:(k + 1) * 512],
                   start=True, stop=True).then_inc(sem("pmix_psum"), 1)
            delta(0, 0)
            delta(0, 1)
            for t in range(2, 4):
                dense(0, t)
                delta(0, t)
            with pe.Fori(1, NT // 4) as i:
                for c in range(4):
                    dense(i, c)
                    delta(i, c)

        @block.scalar
        def _(act):
            A = nc.scalar.activation
            for dst, src in ((mw0[:, :], mlp_w0), (mw1[:, :], mlp_w1), (mw2[:, :], mlp_w2),
                             (mb01[:, 0:1], mlp_b0.rearrange("(p a) -> p a", a=1)),
                             (mb01[:, 1:2], mlp_b1.rearrange("(p a) -> p a", a=1)),
                             (mb2_b[:, :], mlp_b2.rearrange("(a k) -> a k", a=1).to_broadcast([B, NK]))):
                act.dma_start(dst, src).then_inc(sem("mlp_loaded"), 16)
            for p in range(PH):
                act.dma_start(fside_b[p * CG:(p + 1) * CG, :], fside.rearrange("(g c) -> c g", c=CG)).then_inc(sem("fside_loaded"), 16)
            act.dma_start(kw[:, :, :], mix_w.rearrange("k o i a -> k o (i a)")).then_inc(sem("kw_loaded"), 16)
            act.dma_start(mixb_k[:, :], mix_b).then_inc(sem("mixb_loaded"), 16)
            act.dma_start(a_nat[:, :, :], w_a.rearrange("(c p) r -> p c r", p=P)).then_inc(sem("a_loaded"), 16)
            act.dma_start(limes_nat[:, :], limes).then_inc(sem("limes_loaded"), 16)
            act.dma_start(b_rank[:, :], w_b).then_inc(sem("limes_loaded"), 16)
            act.dma_start(bias_b[:, :], b_ffn.rearrange("(a l) -> a l", a=1).to_broadcast([P, L])).then_inc(sem("bias_loaded"), 16)

            act.wait_ge(sem("conv_wT_psum"), 1)
            A(conv_wT[:, :, 0:8, :].rearrange("p g k o -> p k g o"), ps_conv[0:CG, 0:512].rearrange("p (k g o) -> p k g o", k=8, g=GRP), ACT.Copy).then_inc(sem("conv_wT_ready"), 1)
            A(conv_wT[:, :, 8, :], ps_conv[0:CG, 512:576].rearrange("p (g o) -> p g o", g=GRP), ACT.Copy).then_inc(sem("conv_wT_ready"), 1)
            act.wait_ge(sem("condT_psum"), 1)
            A(condT[:, :], ps_small[:, 0:B], ACT.Copy).then_inc(sem("condT_ready"), 1)
            A(w_ctxT[:, :], ps_small[:, B:B + CH], ACT.Copy).then_inc(sem("w_ctxT_ready"), 1)
            act.wait_ge(sem("w_ctxT_ready"), 1)
            for g in range(GRP):
                last = A(w_ctx_rep[:, g], w_ctxT[:, g * CG:(g + 1) * CG].unsqueeze(1).to_broadcast([P, PH, CG]), ACT.Copy)
            last.then_inc(sem("condT_ready"), 2)
            act.wait_ge(sem("mlp_psum"), 1)
            A(h0[:, :], ps_mix[:, 0:B], ACT.Gelu, bias=mb01[:, 0:1]).then_inc(sem("h_act"), 1)
            act.wait_ge(sem("mlp_psum"), 2)
            A(h1[:, :], ps_mix[:, 64:64 + B], ACT.Gelu, bias=mb01[:, 1:2]).then_inc(sem("h_act"), 1)
            act.wait_ge(sem("att_logits_ready"), 2)
            A(att_e[:, :], att[:, :], ACT.Exp, bias=att_s[:, 0:1]).then_inc(sem("att_exp_ready"), 1)
            act.wait_ge(sem("mlp_psum"), 4)
            A(attT[:, :], ps_mix[0:NK, 192:192 + B], ACT.Copy).then_inc(sem("attT_ready"), 1)
            for o in range(NL + 1):
                if o < NL:
                    act.wait_ge(sem("wq_inv_ready"), o + 1)
                    if o >= 1:
                        act.wait_ge(sem("wq_ready"), o)
                    A(yv[:, :, :].rearrange("p a b -> p (a b)"), wq_nat[:, o * L:(o + 1) * L], ACT.Identity,
                      scale=wq_inv[:, o:o + 1]).then_inc(sem("wq_scaled"), 1)
                if o >= 1:
                    act.wait_ge(sem("wqT_psum"), o)
                    bk = (ps_tr if (o - 1) % 2 == 0 else ps_ph).bitcast(BF16)
                    A(wqT[:, :, (o - 1) * P:o * P], bk.rearrange("p (e c) -> p e c", e=PH), ACT.Copy).then_inc(sem("wqT_ready"), 1)
            act.wait_ge(sem("wsc_psum"), 1)
            A(wsc_b[:, :], ps_acc, ACT.Copy).then_inc(sem("wsc_ready"), 1)
            for n in (1, 3):
                act.wait_ge(sem("mix_psum"), n + 1)
                for e in range(2):
                    A(mix_block(n, e), mix_bank(n, e), ACT.Copy).then_inc(sem("mixT_ready"), 1)
            act.wait_ge(sem("w_scale_ready"), 2)
            for c in range(NL):
                act.wait_ge(sem("wT_psum"), c + 1)
                bk = ps_conv if c % 2 == 0 else ps_acc
                A(ffn_wT[:, 0, c, :], bk, ACT.Copy, scale=w_up[:, 0:1]).then_inc(sem("w_hi_ready"), 1)
            act.wait_ge(sem("limesT_psum"), 1)
            A(limesT[:, :], ps_small[0:R, 0:E], ACT.Copy).then_inc(sem("limesT_ready"), 1)

            def phase_rows(i, c, s):
                wait(act, "ph_psum", at(i, c, 2, s + 1))
                bk = ps_ph.rearrange("p (q m) -> p q m", q=4)
                A(x_ph[0:64, s, :, 0:MB], bk[0:64], ACT.Copy).then_inc(sem("ph_ready"), 1)
                A(x_ph[64:128, s, :, 1:MB + 1], bk[64:128], ACT.Copy).then_inc(sem("ph_ready"), 1)

            def scale_rows(i, c):
                wait(act, "yinv_ready", at(i, c, 1, 1))
                wait(act, "yq_ready", at(i, c))
                for s in range(8):
                    last = A(yv[:, s, :], yb[:, c % 2, s, :], ACT.Copy, scale=yinv[:, s:s + 1])
                last.then_inc(sem("yv_ready"), 1)

            def tokens_sb(i, c):
                wait(act, "yqT_psum", at(i, c, 1, 1))
                A(yqT[:, :, :].rearrange("m p (s c) -> m s p c", s=8),
                  ps_trb.rearrange("m (s p c) -> m s p c", s=8, p=PH), ACT.Copy).then_inc(sem("yqT_ready"), 1)

            def high(i, c, h):
                wait(act, "u_ready", at(i, c, 2, 1 + h))
                if h == 0:
                    wait(act, "t_ready", at(i, c, 1, 1))
                    if not isinstance(i, int) or 4 * i + c >= 2:
                        wait(act, f"x2_saved{c % 2}", i * 32 + 16 * (c // 2))
                    wait(act, "z_psum", at(i, c, 1, -1))
                A(x2_cols[:, c % 2, 0, 4 * h:4 * h + 4, :].rearrange("p c t -> p (c t)"), u[:, h * HALF:(h + 1) * HALF],
                  ACT.Copy, scale=t_pair[:, c % 4, 0:1]).then_inc(sem("hi_ready"), 1)

            def rank_low(i, c):
                wait(act, "z_psum", at(i, c, 1, 1))
                wait(act, "z_ready", at(i, c))
                A(z_lo[:, :], ps_small[64:ZW, 256:384], ACT.Copy, scale=t_pair[64:ZW, c % 4, 1:2]).then_inc(sem("z_lo_ready"), 1)

            def row_sums(i, c):
                wait(act, "x1_ready", at(i, c, 2, 2))
                wait(act, "x1max_all_ready", at(i, c))
                A(abs_junk[:, :], x1[:, c % 2, :], ACT.Abs, accum_out=x1max[:, :]).then_inc(sem("x1max_ready"), 1)

            def body(i, c, on):
                if on(-3):
                    row_sums(i, c - 3)
                if on(-2):
                    tokens_sb(i, c - 2)
                if on(-3):
                    high(i, c - 3, 0)
                if on(-1):
                    scale_rows(i, c - 1)
                if on(-3):
                    high(i, c - 3, 1)
                if on(-4):
                    rank_low(i, c - 4)
                if on(1):
                    phase_rows(i, c + 1, 0)
                    phase_rows(i, c + 1, 1)

            act.wait_ge(sem("x_ph_zeroed"), 2)
            act.wait_ge(sem("z_w_ready"), 1)
            bodies(act, body)

            act.wait_ge(sem("gate_in_ready"), 1)
            A(gate[:, 3], gate[:, 2], ACT.Exp).then_inc(sem("gate_exp_ready"), 1)
            act.wait_ge(sem("gate_in_ready"), 2)
            A(gate[:, 5], gate[:, 5], ACT.Exp, scale=-2.0).then_inc(sem("gate_exp_ready"), 1)
            act.wait_ge(sem("gateT_psum"), 1)
            for s in range(2):
                act.wait_ge(sem(f"x2_saved{s}"), 16 * (NT // 2))
            A(gateT[:, :], bank(4, 4)[0:E, :], ACT.Copy).then_inc(sem("gateT_ready"), 1)

            def store(i, c):
                wait(act, "out_ready", at(i, c, 2, 2))
                act.dma_start(out_t[at(i, c)], o_sb[:, c % 2, :]).then_inc(sem(f"out_saved{c % 2}"), 16)

            with act.Fori(0, NT // 4) as i:
                for c in range(4):
                    store(i, c)
            for s in range(2):
                act.wait_ge(sem(f"out_saved{s}"), 16 * (NT // 2))

        @block.gpsimd
        def _(pool):
            g = nc.gpsimd
            g.memset(ident[:, :], 0.0).then_inc(sem("ident_zero"), 1)
            g.memset(identb[:, :], 0.0).then_inc(sem("ident_zero"), 1)
            g.memset(set_rows[:, :], 1.0).then_inc(sem("ident_zero"), 1)
            pool.wait_ge(sem("ident_zero"), 3)
            for m in (ident, identb):
                g.affine_select(out=m[:, :], in_=m[:, :], compare_op=ALU.not_equal, fill=1.0, base=0,
                                pattern=[[-1, P]], channel_multiplier=1).then_inc(sem("ident_ready"), 1)
            g.affine_select(out=set_rows[:, :], in_=set_rows[:, :], compare_op=ALU.is_ge, fill=0.0, base=0,
                            pattern=[[1, P]], channel_multiplier=-CG).then_inc(sem("set_rows_half"), 1)
            pool.wait_ge(sem("set_rows_half"), 1)
            g.affine_select(out=set_rows[:, :], in_=set_rows[:, :], compare_op=ALU.is_ge, fill=0.0, base=CG - 1,
                            pattern=[[-1, P]], channel_multiplier=CG).then_inc(sem("ident_ready"), 1)
            for e in range(2):
                g.memset(mixT[e * CH:(e + 1) * CH, :, (1 - e) * CH:(2 - e) * CH], 0.0).then_inc(sem("mixT_zeroed"), 1)
                pool.wait_ge(sem("mixT_zeroed"), e + 1)
            g.memset(conv_w[:, :, :, :], 0.0).then_inc(sem("conv_w_zeroed"), 1)
            pool.wait_ge(sem("conv_w_zeroed"), 1)
            g.memset(x_ph[0:64, :, :, MB:MB + 1], 0.0).then_inc(sem("x_ph_zeroed"), 1)
            pool.wait_ge(sem("x_ph_zeroed"), 1)
            g.memset(x_ph[64:128, :, :, 0:1], 0.0).then_inc(sem("x_ph_zeroed"), 1)
            pool.wait_ge(sem("x_ph_zeroed"), 2)
            pool.wait_ge(sem("w_max_ready"), 4)
            g.partition_all_reduce(w_exp[:, :], w_max[:, :], P, RMAX).then_inc(sem("w_max_all"), 1)
            pool.wait_ge(sem("mix_max_ready"), 1)
            g.partition_all_reduce(scal[:, 10:11], scal[:, 6:7], P, RMAX).then_inc(sem("mix_max_all"), 1)

            def tile_max(i, c):
                wait(pool, "x1max_ready", at(i, c, 1, 1))
                wait(pool, "t_ready", at(i, c))
                g.tensor_tensor(pool_turn[:, 1:2], pool_turn[:, 0:1], pool_turn[:, 0:1], ALU.add)
                g.partition_all_reduce(x1max_all[:, :], x1max[:, :], P, RMAX).then_inc(sem("x1max_all_ready"), 1)

            def with_bias(i, c):
                wait(pool, "x1_ready", at(i, c, 2, 2))
                if not isinstance(i, int) or 4 * i + c >= 2:
                    wait(pool, f"xb_saved{c % 2}", i * 32 + 16 * (c // 2))
                g.tensor_tensor(xb[:, c % 2, :], x1[:, c % 2, :], bias_b[:, :], ALU.add).then_inc(sem("xb_ready"), 1)

            def add_layer0(i, c, h):
                wait(pool, "f_ready", at(i, c, 2, h + 1))
                if h == 0:
                    wait(pool, "mix_ready", at(i, c, 2, -2))
                    wait(pool, "x1max_ready", at(i, c, 1, -1))
                s = slice(h * HALF, (h + 1) * HALF)
                g.tensor_tensor(x1[:, c % 2, s], x_in[:, c % 4, s], f16[:, s], ALU.add).then_inc(sem("x1_ready"), 1)

            def body(i, c, on):
                if on(-3):
                    tile_max(i, c - 3)
                    with_bias(i, c - 3)
                if on(-2):
                    add_layer0(i, c - 2, 0)
                    add_layer0(i, c - 2, 1)

            g.memset(pool_turn[:, :], 0.0).then_inc(sem("pool_turn_ready"), 1)
            pool.wait_ge(sem("pool_turn_ready"), 1)
            pool.wait_ge(sem("bias_loaded"), 16)
            pool.wait_ge(sem("w_lo_ready"), NL)
            bodies(pool, body)

            pool.wait_ge(sem("gmax_ready"), 2)
            g.partition_all_reduce(gmx[:, 2:4], gmx[:, 0:2], P, RMAX).then_inc(sem("gmax_all"), 1)
            pool.wait_ge(sem("z_max_ready"), 4)
            g.partition_all_reduce(z_exp[:, :], z_max[:, :], P, RMAX).then_inc(sem("z_max_all_ready"), 1)

        @block.vector
        def _(dve):
            v = nc.vector
            chain = [0]

            def link(ins):
                chain[0] += 1
                ins.then_inc(sem("vector_chain"), 1)
                dve.wait_ge(sem("vector_chain"), chain[0])

            dve.wait_ge(sem("ident_ready"), 3)
            v.tensor_reduce(chan_mask[:, :], ident[:, :].rearrange("p (s c) -> p c s", c=CG), AX.X, ALU.add).then_inc(sem("masks_ready"), 1)
            dve.wait_ge(sem("ctx_psum"), 1)
            dve.wait_ge(sem("fside_loaded"), 16 * PH)
            v.tensor_tensor(ybias[:, :, :].rearrange("p b g -> p g b"), ps_small[:, 128:128 + GRP * B].rearrange("p (g b) -> p g b", g=GRP),
                            fside_b[:, :].unsqueeze(2).to_broadcast([P, GRP, B]), ALU.add).then_inc(sem("ybias_ready"), 1)
            dve.wait_ge(sem("mlp_psum"), 3)
            v.tensor_tensor(att[:, :], ps_mix[0:B, 128:128 + NK], mb2_b[:, :], ALU.add).then_inc(sem("att_logits_ready"), 1)
            dve.wait_ge(sem("att_logits_ready"), 1)
            v.tensor_reduce(att_s[:, 0:1], att[:, :], AX.X, ALU.max, negate=True).then_inc(sem("att_logits_ready"), 1)
            dve.wait_ge(sem("att_exp_ready"), 1)
            link(v.tensor_reduce(att_s[:, 1:2], att_e[:, :], AX.X, ALU.add))
            link(v.reciprocal(att_s[:, 2:3], att_s[:, 1:2]))
            v.tensor_scalar(att[:, :], att_e[:, :], att_s[:, 2:3], None, ALU.mult).then_inc(sem("att_ready"), 1)
            for o in range(NL):
                if o % 4 == 0:
                    dve.wait_ge(sem(f"wq_loaded{o // 4}"), 16)
                link(v.tensor_reduce(wq_max[:, o:o + 1], wq_nat[:, o * L:(o + 1) * L], AX.X, ALU.max, apply_absolute_value=True))
                link(v.tensor_scalar(wq_scale[:, o:o + 1], wq_max[:, o:o + 1], 1.0 / QMAX, 1e-30, ALU.mult, ALU.max))
                v.reciprocal(wq_inv[:, o:o + 1], wq_scale[:, o:o + 1]).then_inc(sem("wq_inv_ready"), 1)
                dve.wait_ge(sem("wq_scaled"), o + 1)
                if o >= 2:
                    dve.wait_ge(sem("wqT_psum"), o - 1)
                q = yq if o % 2 == 0 else yqT
                v.tensor_scalar(q[:, :, :].rearrange("p a b -> p (a b)"), yv[:, :, :].rearrange("p a b -> p (a b)"),
                                MAGIC, -MAGIC, ALU.add, ALU.add).then_inc(sem("wq_ready"), 1)
            for n in (0, 2):
                dve.wait_ge(sem("mix_psum"), n + 1)
                for e in range(2):
                    v.tensor_copy(mix_block(n, e), mix_bank(n, e)).then_inc(sem("mixT_ready"), 1)
            for j, n in enumerate((4, 5, 6, 7, 0, 1, 2, 3)):
                dve.wait_ge(sem("mixb_psum"), j + 1)
                v.tensor_copy(mixb_all[:, 4 * n:4 * n + 4, :].rearrange("p t c -> p (t c)"), bank(n)).then_inc(sem("mixb_ready"), 1)
            dve.wait_ge(sem("mixT_ready"), 8)
            dve.wait_ge(sem("mixT_zeroed"), 2)
            dve.wait_ge(sem("mixb_ready"), 8)
            v.tensor_reduce(scal[:, 6:7], mixT[:, :, :], AX.XY, ALU.max, apply_absolute_value=True).then_inc(sem("mix_max_ready"), 1)
            link(v.tensor_reduce(scal[:, 7:8], mixb_all[:, :, :], AX.XY, ALU.max, apply_absolute_value=True))
            link(v.memset(w_max[:, :], 0.0))
            dve.wait_ge(sem("limes_loaded"), 32)
            v.tensor_reduce(w_max[0:E, 2:3], limes_nat[:, :], AX.X, ALU.max, apply_absolute_value=True).then_inc(sem("w_max_ready"), 1)
            v.tensor_reduce(w_max[0:R, 3:4], b_rank[:, :], AX.X, ALU.max, apply_absolute_value=True).then_inc(sem("w_max_ready"), 1)
            dve.wait_ge(sem("a_loaded"), 16)
            v.tensor_reduce(w_max[:, 1:2], a_nat[:, :, :], AX.XY, ALU.max, apply_absolute_value=True).then_inc(sem("w_max_ready"), 1)
            dve.wait_ge(sem("w_loaded"), 16)
            v.tensor_reduce(w_max[:, 0:1], w_nat, AX.XY, ALU.max, apply_absolute_value=True).then_inc(sem("w_max_ready"), 1)
            dve.wait_ge(sem("w_max_all"), 1)
            link(v.tensor_scalar(w_exp[:, :], w_exp[:, :], 1e-20, None, ALU.max))
            link(v.tensor_scalar(w_exp[:, :].bitcast(U32), w_exp[:, :].bitcast(U32), EXPMASK, None, ALU.bitwise_and))
            v.tensor_scalar(w_up[:, :].bitcast(I32), w_exp[:, :].bitcast(I32), -1.0, float((254 + TOP) << 23),
                            ALU.mult, ALU.add).then_inc(sem("w_scale_ready"), 1)
            v.tensor_scalar(w_down[:, :].bitcast(I32), w_exp[:, :].bitcast(I32), float(-(TOP << 23)), None,
                            ALU.add).then_inc(sem("w_scale_ready"), 1)
            dve.wait_ge(sem("w_scale_ready"), 2)
            for c in range(NL):
                dve.wait_ge(sem("w_hi_ready"), c + 1)
                bk = ps_conv if c % 2 == 0 else ps_acc
                v.scalar_tensor_tensor(ffn_wT[:, 1, c, :], bk, w_up[:, 0:1], ffn_wT[:, 0, c, :], ALU.mult, ALU.subtract).then_inc(sem("w_lo_ready"), 1)
            dve.wait_ge(sem("w_lo_ready"), NL)
            link(v.memset(z_w[:, :, :], 0.0))
            link(v.tensor_scalar(z_w[:, :, 0:R], a_nat[:, :, :], w_up[:, 1:2], None, ALU.mult))
            v.scalar_tensor_tensor(z_w[:, :, 64:64 + R], a_nat[:, :, :], w_up[:, 1:2], z_w[:, :, 0:R], ALU.mult, ALU.subtract)
            v.tensor_copy(z_w[:, :, R:R + E], ffn_wT[:, 0, :, 0:E])
            v.tensor_copy(z_w[:, :, 64 + R:64 + R + E], ffn_wT[:, 1, :, 0:E]).then_inc(sem("z_w_ready"), 1)
            for n in (0, 2):
                last = v.tensor_scalar(b_parts[n * R:(n + 1) * R, :], b_rank[:, :], w_up[0:R, 3:4], None, ALU.mult)
            link(last)
            v.scalar_tensor_tensor(b_parts[R:2 * R, :], b_rank[:, :], w_up[0:R, 3:4], b_parts[0:R, :], ALU.mult, ALU.subtract).then_inc(sem("b_parts_ready"), 1)
            v.tensor_scalar(limes_n[:, :], limes_nat[:, :], w_up[0:E, 2:3], 2.0 ** -(TOP + 1), ALU.mult, ALU.mult).then_inc(sem("b_parts_ready"), 1)
            dve.wait_ge(sem("mix_max_all"), 1)
            link(v.tensor_scalar(scal[:, 11:12], scal[:, 10:11], float(CH), None, ALU.mult))
            link(v.tensor_scalar(scal[:, 12:13], scal[:, 7:8], 1e-20, None, ALU.add))

            def blocks(i, c):
                wait(dve, f"x_loaded{c % 4}", i * 16 + 16 * (c // 4 + 1))
                wait(dve, "ph_psum", at(i, c, 2, 0))
                for a in range(4):
                    last = v.transpose(x_blk[:, a].rearrange("p s e c -> p e s c"),
                                       x_in[:, c % 4, a * 256:(a + 1) * 256].rearrange("p (m e) -> p e m", e=PH))
                last.then_inc(sem("blk_ready"), 1)

            def conv_bias(i, c):
                wait(dve, "conv_ready", at(i, c, 1, 1))
                wait(dve, "yv_ready", at(i, c, 1, -1))
                v.tensor_tensor(yb[:, c % 2].rearrange("p (b g) m -> p b g m", b=2), ps_conv.rearrange("p (g b m) -> p b g m", g=GRP, b=2),
                                ybias[:, bass.ds(at(i, c, 2), 2), :].unsqueeze(3).to_broadcast([P, 2, GRP, MB]), ALU.add).then_inc(sem("yb_ready"), 1)

            def row_max(i, c):
                wait(dve, "yb_ready", at(i, c, 1, 1))
                v.tensor_reduce(rowmax[:, :], yb[:, c % 2], AX.X, ALU.max, apply_absolute_value=True).then_inc(sem("rowmax_ready"), 1)

            def tile_scale(i, c):
                wait(dve, "x1max_all_ready", at(i, c, 1, 1))
                v.tensor_scalar(bound[:, 0:1], x1max_all[:, :], scal[:, 11:12], scal[:, 12:13], ALU.mult, ALU.add).then_inc(sem("bound_ready"), 1)
                wait(dve, "bound_ready", at(i, c, 2, 1))
                v.tensor_scalar(bound[:, 1:2].bitcast(U32), bound[:, 0:1].bitcast(U32), EXPMASK, None, ALU.bitwise_and).then_inc(sem("bound_ready"), 1)
                wait(dve, "bound_ready", at(i, c, 2, 2))
                v.tensor_scalar(t_pair[:, c % 4, 0:1].bitcast(I32), bound[:, 1:2].bitcast(I32), -1.0, float((254 + TOP) << 23), ALU.mult, ALU.add).then_inc(sem("t_half"), 1)
                v.tensor_scalar(t_pair[:, c % 4, 1:2].bitcast(I32), bound[:, 1:2].bitcast(I32), float(-(TOP << 23)), None, ALU.add).then_inc(sem("t_half"), 1)
                wait(dve, "t_half", at(i, c, 2, 2))
                v.tensor_copy(t_all[:, at(i, c), :], t_pair[:, c % 4, :]).then_inc(sem("t_ready"), 1)

            def rank_out(i, c):
                wait(dve, "z_lo_ready", at(i, c, 1, 1))
                v.scalar_tensor_tensor(zT[0:R + E, bass.ds(at(i, c, P), P)], ps_small[0:R + E, 256:384], t_pair[0:R + E, c % 4, 1:2],
                                       z_lo[:, :], ALU.mult, ALU.add).then_inc(sem("z_ready"), 1)

            def chan_max(i, c):
                wait(dve, "rowmaxT_ready", at(i, c, 1, 1))
                v.tensor_reduce(chanmax[:, :], ps_small[0:8, 0:P].rearrange("p (a c) -> p c a", a=PH), AX.X, ALU.max).then_inc(sem("chanmax_half"), 1)
                wait(dve, "chanmax_half", at(i, c, 1, 1))
                v.tensor_copy(chanmax_rep[:, :, :], chanmax[:, :].unsqueeze(1).to_broadcast([8, PH, CG])).then_inc(sem("chanmax_ready"), 1)

            def scales(i, c):
                wait(dve, "max_psum", at(i, c, 1, 1))
                v.tensor_scalar(yscale[:, :], ps_small[:, 128:136], 1.0 / QMAX, 1e-30, ALU.mult, ALU.max).then_inc(sem("yscale_ready"), 1)
                v.tensor_tensor_reduce(tok_junk[:, :], ps_small[:, 144:144 + CG], chan_mask[:, :], scale=1.0 / QMAX, scalar=0.0,
                                       op0=ALU.mult, op1=ALU.add, accum_out=tok_scale[:, c % 4:c % 4 + 1]).then_inc(sem("tok_scale_ready"), 1)
                wait(dve, "yscale_ready", at(i, c, 1, 1))
                wait(dve, "yv_ready", at(i, c))
                v.reciprocal(yinv[:, :], yscale[:, :]).then_inc(sem("yinv_ready"), 1)

            def mixed(i, c, h):
                wait(dve, "mix_ready", at(i, c, 2, h + 1))
                wait(dve, "hi_ready", at(i, c, 2, h - 1))
                v.tensor_tensor(u[:, h * HALF:(h + 1) * HALF].rearrange("p (k t) -> p k t", k=4),
                                ps_mix.rearrange("p (k t) -> p k t", k=4),
                                mixb_all[:, bass.ds(at(i, c), 1), :].to_broadcast([P, 4, P]), ALU.add).then_inc(sem("u_ready"), 1)

            def low(i, c, h):
                wait(dve, "hi_ready", at(i, c, 2, h + 1))
                v.scalar_tensor_tensor(x2_cols[:, c % 2, 1, 4 * h:4 * h + 4, :].rearrange("p k t -> p (k t)"), u[:, h * HALF:(h + 1) * HALF],
                                       t_pair[:, c % 4, 0:1], x2_cols[:, c % 2, 0, 4 * h:4 * h + 4, :].rearrange("p k t -> p (k t)"),
                                       ALU.mult, ALU.subtract).then_inc(sem("lo_ready"), 1)

            def layer0(i, c, h):
                wait(dve, "acc_ready", at(i, c, 2, h + 1))
                wait(dve, "tok_scale_ready", at(i, c, 1, 1))
                wait(dve, "x1_ready", at(i, c, 2, h - 1))
                s = slice(h * HALF, (h + 1) * HALF)
                v.scalar_tensor_tensor(f16[:, s], ps_acc[:, s], tok_scale[:, c % 4:c % 4 + 1], wsc_b[:, s], ALU.mult, ALU.mult).then_inc(sem("f_ready"), 1)

            def rounded(i, c):
                wait(dve, "yv_ready", at(i, c, 1, 1))
                wait(dve, "yqT_psum", at(i, c))
                v.tensor_scalar(yq[:, :, :].rearrange("p s m -> p (s m)"), yv[:, :, :].rearrange("p s m -> p (s m)"), MAGIC, -MAGIC,
                                ALU.add, ALU.add).then_inc(sem("yq_ready"), 1)

            def body(i, c, on):
                if on(-1):
                    chan_max(i, c - 1)
                if on(-3):
                    mixed(i, c - 3, 0)
                    tile_scale(i, c - 3)
                if on(-1):
                    scales(i, c - 1)
                if on(0):
                    conv_bias(i, c)
                if on(-3):
                    mixed(i, c - 3, 1)
                if on(1):
                    blocks(i, c + 1)
                if on(-3):
                    low(i, c - 3, 0)
                if on(-2):
                    layer0(i, c - 2, 0)
                if on(-1):
                    rounded(i, c - 1)
                if on(-3):
                    low(i, c - 3, 1)
                if on(-4):
                    rank_out(i, c - 4)
                if on(0):
                    row_max(i, c)
                if on(-2):
                    layer0(i, c - 2, 1)

            bodies(dve, body)

            ps_g = bank(4, 4)
            dve.wait_ge(sem("logits_psum"), 1)
            h_log, d_log, lg, ex, pr, mk, wt, gt = (gate[:, n] for n in range(8))
            flat = lambda a: a.rearrange("p j e -> p (j e)")
            link(v.tensor_scalar(flat(h_log), ps_g[:, 0:NJ * E], w_down[:, 0:1], None, ALU.mult))
            link(v.tensor_tensor(h_log, h_log, bias_b[:, 0:E].unsqueeze(1).to_broadcast([P, NJ, E]), ALU.add))
            v.tensor_scalar(flat(d_log), ps_g[:, 512:512 + NJ * E], w_down[:, 1:2], None, ALU.mult).then_inc(sem("logits_read"), 1)
            v.tensor_reduce(gmx[:, 0:1], h_log, AX.XY, ALU.max, apply_absolute_value=True).then_inc(sem("gmax_ready"), 1)
            dve.wait_ge(sem("logits_read"), 1)
            v.tensor_reduce(gmx[:, 1:2], d_log, AX.XY, ALU.max, apply_absolute_value=True).then_inc(sem("gmax_ready"), 1)
            dve.wait_ge(sem("gmax_all"), 1)
            link(v.tensor_scalar(gmx[:, 4:6], gmx[:, 2:4], 1e-6, None, ALU.max))
            link(v.reciprocal(gmx[:, 6:8], gmx[:, 4:6]))
            link(v.tensor_scalar(flat(h_log), flat(h_log), gmx[:, 6:7], 0.5, ALU.mult, ALU.mult))
            link(v.tensor_scalar(flat(d_log), flat(d_log), gmx[:, 7:8], 0.5, ALU.mult, ALU.mult))
            link(v.tensor_tensor(lg, h_log, d_log, ALU.add))
            link(v.tensor_reduce(gsm[:, 0, :], lg, AX.X, ALU.max))
            v.tensor_tensor(lg, lg, gsm[:, 0, :].unsqueeze(2).to_broadcast([P, NJ, E]), ALU.subtract).then_inc(sem("gate_in_ready"), 1)
            dve.wait_ge(sem("gate_exp_ready"), 1)
            link(v.tensor_reduce(gsm[:, 1, :], ex, AX.X, ALU.add))
            link(v.reciprocal(gsm[:, 2, :], gsm[:, 1, :]))
            link(v.tensor_tensor(pr, ex, gsm[:, 2, :].unsqueeze(2).to_broadcast([P, NJ, E]), ALU.mult))
            for j in range(NJ):
                last = v.max(top8[:, j, :], pr[:, j, :])
            link(last)
            v.tensor_tensor(mk, pr, top8[:, :, 1:2].to_broadcast([P, NJ, E]), ALU.subtract).then_inc(sem("gate_in_ready"), 1)
            dve.wait_ge(sem("gate_exp_ready"), 2)
            link(v.tensor_scalar(flat(mk), flat(mk), 1.0, None, ALU.add))
            link(v.reciprocal(flat(mk), flat(mk)))
            link(v.tensor_tensor(wt, pr, mk, ALU.mult))
            link(v.tensor_reduce(gsm[:, 3, :], wt, AX.X, ALU.add))
            link(v.tensor_scalar(gsm[:, 4, :], gsm[:, 3, :], 1e-9, None, ALU.add))
            link(v.reciprocal(gsm[:, 5, :], gsm[:, 4, :]))
            v.tensor_tensor(gt, wt, gsm[:, 5, :].unsqueeze(2).to_broadcast([P, NJ, E]), ALU.mult).then_inc(sem("gate_ready"), 1)
            v.tensor_scalar(unscale[:, :], t_all[:, :, 1], w_down[:, 0:1], None, ALU.mult)
            link(v.memset(z_max[:, :], 0.0))
            for k in range(4):
                dve.wait_ge(sem("pmix_psum"), k + 1)
                zk = zT[0:R, k * 1024:(k + 1) * 1024].rearrange("p (a e) -> p a e", e=2)
                link(v.tensor_tensor(zk, zk, ps_g[0:R, k * 512:(k + 1) * 512].unsqueeze(2).to_broadcast([R, 512, 2]), ALU.mult))
                v.tensor_reduce(z_max[0:R, 8 * k:8 * k + 8], zT[0:R, k * 1024:(k + 1) * 1024].rearrange("p (t c) -> p t c", c=P),
                                AX.X, ALU.max, apply_absolute_value=True).then_inc(sem("z_max_ready"), 1)
            dve.wait_ge(sem("z_max_all_ready"), 1)
            link(v.tensor_scalar(z_exp[:, :], z_exp[:, :], 1e-20, None, ALU.max))
            link(v.tensor_scalar(z_exp[:, :].bitcast(U32), z_exp[:, :].bitcast(U32), EXPMASK, None, ALU.bitwise_and))
            v.tensor_scalar(z_up[:, :].bitcast(I32), z_exp[:, :].bitcast(I32), -1.0, float((254 + TOP) << 23), ALU.mult, ALU.add)
            link(v.tensor_scalar(unscale_d[:, :].bitcast(I32), z_exp[:, :].bitcast(I32), float(-(TOP << 23)), None, ALU.add))
            link(v.tensor_scalar(unscale_d[:, :], unscale_d[:, :], w_down[:, 1:2], w_down[:, 2:3], ALU.mult, ALU.mult))
            link(v.tensor_scalar(unscale_d[:, :], unscale_d[:, :], w_down[:, 3:4], 2.0 ** (TOP + 1) * 16.0 / R, ALU.mult, ALU.mult))

            def rank_cols(i, c):
                wait(dve, "h_ready", at(i, c, 1, -1))
                ztile, up = zT[0:R, bass.ds(at(i, c, P), P)], z_up[0:R, bass.ds(at(i, c), 1)]
                v.tensor_scalar(z_scaled[:, c % 2, :], ztile, up, None, ALU.mult).then_inc(sem("z_high"), 1)
                for n in range(2):
                    v.tensor_scalar(z_parts[n * R:(n + 1) * R, c % 2, :], ztile, up, None, ALU.mult).then_inc(sem("z_high"), 1)
                wait(dve, "z_high", at(i, c, 3, 3))
                v.tensor_tensor(z_parts[2 * R:3 * R, c % 2, :], z_scaled[:, c % 2, :], z_parts[0:R, c % 2, :], ALU.subtract).then_inc(sem("z_parts_ready"), 1)

            def finish(i, c):
                wait(dve, "h_ready", at(i, c, 1, 1))
                wait(dve, f"xb_loaded{c % 4}", i * 16 + 16 * (c // 4 + 1))
                if not isinstance(i, int) or 4 * i + c >= 2:
                    wait(dve, f"out_saved{c % 2}", i * 32 + 16 * (c // 2))
                for h in range(2):
                    s = slice(h * HALF, (h + 1) * HALF)
                    v.scalar_tensor_tensor(o_sb[:, c % 2, s], bank(4 + 2 * (c % 2) + h), unscale_d[:, bass.ds(at(i, c), 1)], xb_in[:, c % 4, s],
                                           ALU.mult, ALU.add).then_inc(sem("delta_added"), 1)
                for h in range(2):
                    s = slice(h * HALF, (h + 1) * HALF)
                    wait(dve, "delta_added", at(i, c, 2, h + 1))
                    v.scalar_tensor_tensor(o_sb[:, c % 2, s], bank(2 * (c % 2) + h), unscale[:, bass.ds(at(i, c), 1)], o_sb[:, c % 2, s],
                                           ALU.mult, ALU.add).then_inc(sem("out_ready"), 1)

            rank_cols(0, 0)
            rank_cols(0, 1)
            for c in range(2, 6):
                finish(0, c - 2)
                rank_cols(0, c)
            with dve.Fori(1, NT // 4 - 1) as i:
                for c in range(2, 6):
                    finish(i, c - 2)
                    rank_cols(i, c)
            n = NT // 4 - 1
            finish(n, 0)
            rank_cols(n, 2)
            finish(n, 1)
            rank_cols(n, 3)
            finish(n, 2)
            finish(n, 3)


_INS = ['x', 'cond_128', 'fside_S_0', 'L0_cond_weight', 'L0_cond_c_weight', 'L0_ffn_weight', 'L1_cond_W0', 'L1_cond_b0',
        'L1_cond_W1', 'L1_cond_b1', 'L1_cond_W2', 'L1_cond_b2', 'L1_cond_weight', 'L1_cond_bias_k', 'L1_ffn_W', 'L1_ffn_b',
        'L1_ffn_A', 'L1_ffn_Bmat', 'L1_ffn_LiMEs']


def kernel(**inputs):
    import numpy as _np
    import concourse.bacc as _bacc
    from concourse import mybir as _mybir
    from concourse.bass_utils import run_bass_kernel_spmd as _run

    nc = _bacc.Bacc("TRN2", target_bir_lowering=False, num_devices=1)
    arrays, args = {}, []
    for name in _INS:
        a = _np.ascontiguousarray(inputs[name])
        arrays[f"in_{name}"] = a
        args.append(nc.dram_tensor(f"in_{name}", a.shape, _mybir.dt.from_np(a.dtype), kind="ExternalInput").ap())
    args.append(nc.dram_tensor("out", (B, CH, L), F32, kind="ExternalOutput").ap())
    program(nc, *args)
    r = _run(nc, [arrays], core_ids=[0])
    return r.results[0]["out"]
```

```python
from contextlib import ExitStack

import numpy as np
import concourse.bass as bass
from concourse import mybir

F32 = mybir.dt.float32
F16 = mybir.dt.float16
BF16 = mybir.dt.bfloat16
U32 = mybir.dt.uint32
I32 = mybir.dt.int32
ALU = mybir.AluOpType
ACT = mybir.ActivationFunctionType
AX = mybir.AxisListType
RMAX = bass.bass_isa.ReduceOp.absmax

P = 128
B, CH, L = 64, 64, 1024
GRP, CG = 4, 16
TAPS = 9
PH = 8
MB = L // PH
NT = B // 2
NL = L // P
HALF = L // 2
NK, HID = 8, 128
R, E = 32, 8
NTOK = B * CH
NANCH = NTOK // 2
NJ = NANCH // P
ZW = 64 + R + E
QMAX = 127.0
MAGIC = 12582912.0
EXPMASK = 0x7F800000
TOP = 13


def program(nc, x, cond, fside, w_conv, w_ctx, w_q, mlp_w0, mlp_b0, mlp_w1, mlp_b1, mlp_w2, mlp_b2,
            mix_w, mix_b, w_ffn, b_ffn, w_a, w_b, limes, out):
    ctx = ExitStack()
    with ctx:
        ctx.enter_context(nc.allow_non_contiguous_dma(reason="small weights"))

        def sb(name, shape, dt):
            return ctx.enter_context(nc.sbuf_tensor(name, shape, dt))

        sems = {}

        def sem(name):
            if name not in sems:
                sems[name] = ctx.enter_context(nc.semaphore(name))
            return sems[name]

        ffn_wT = sb("ffn_wT", [P, 2, NL, L], F16)
        wq_nat = ffn_wT[:, :, :, :].rearrange("p a c l -> p (a c l)").bitcast(F32)
        stage = sb("stage", [P, NL * L], F32)
        w_nat = stage[:, :].rearrange("p (a l) -> p a l", a=NL)
        zT = stage[:, 0:NTOK]
        x2_cols = stage[:, NTOK:NTOK + 2 * L].bitcast(F16).rearrange("p (s h c t) -> p s h c t", s=2, h=2, c=NL)
        xb = stage[:, NTOK + 2 * L:NTOK + 4 * L].rearrange("p (s l) -> p s l", s=2)
        wqT = sb("wqT", [P, PH, L], BF16)
        mixT = sb("mixT", [P, NT, P], F32)
        mixb_all = sb("mixb_all", [P, NT, P], F32)
        kw = mixT[0:NK, :, :].rearrange("k a t -> k (a t)")
        agg = mixb_all[0:B, :, :].rearrange("b a t -> b (a t)").rearrange("b (i o) -> b i o", i=CH)
        x_in = sb("x_in", [P, 4, L], F32)
        x_blk = sb("x_blk", [P, 4, 2, PH, CG], F32)
        x_ph = sb("x_ph", [P, 2, GRP, MB + 1], F32)
        yb = sb("yb", [P, 2, 8, MB], F32)
        yv = sb("yv", [P, 8, MB], F32)
        yq = sb("yq", [P, 8, MB], BF16)
        yqT = sb("yqT", [P, PH, P], BF16)
        f16 = sb("f16", [P, L], F16)
        x1 = sb("x1", [P, 2, L], F32)
        b_rank = x1[0:R, 1, :]
        u = sb("u", [P, L], F32)
        wsc_b = sb("wsc_b", [P, L], F32)
        bias_b = sb("bias_b", [P, L], F32)
        ident = sb("ident", [P, P], F32)
        identb = sb("identb", [P, P], BF16)
        conv_wT = sb("conv_wT", [CG, GRP, TAPS, CG], F32)
        conv_w = sb("conv_w", [P, GRP, 16, CG], F32)
        w_conv_nat = sb("w_conv_nat", [CH, CG, TAPS], F32)
        ybias = sb("ybias", [P, B, GRP], F32)
        fside_b = sb("fside_b", [P, GRP], F32)
        cond_nat = sb("cond_nat", [B, P], F32)
        condT = sb("condT", [P, B], F32)
        w_ctx_nat = sb("w_ctx_nat", [CH, P], F32)
        w_ctxT = sb("w_ctxT", [P, CH], F32)
        w_ctx_rep = sb("w_ctx_rep", [P, GRP, PH, CG], F32)
        mw0 = sb("mw0", [P, HID], F32)
        mw1 = sb("mw1", [HID, HID], F32)
        mw2 = sb("mw2", [HID, NK], F32)
        mb01 = sb("mb01", [HID, 2], F32)
        mb2_b = sb("mb2_b", [B, NK], F32)
        mixb_k = sb("mixb_k", [NK, CH], F32)
        agg_b = sb("agg_b", [B, CH], F32)
        kw_flat = sb("kw_flat", [P, NK * CH * CH // P], F32)
        h0 = sb("h0", [HID, B], F32)
        h1 = sb("h1", [HID, B], F32)
        att = sb("att", [B, NK], F32)
        att_e = sb("att_e", [B, NK], F32)
        att_s = sb("att_s", [B, 4], F32)
        attT = sb("attT", [NK, B], F32)
        chan_mask = sb("chan_mask", [P, CG], F32)
        set_rows = sb("set_rows", [8, P], F32)
        wq_max = sb("wq_max", [P, NL], F32)
        wq_scale = sb("wq_scale", [P, NL], F32)
        wq_inv = sb("wq_inv", [P, NL], F32)
        a_nat = sb("a_nat", [P, NL, R], F32)
        z_w = sb("z_w", [P, NL, ZW], F16)
        scal = sb("scal", [P, 2], F32)
        w_part = sb("w_part", [P, 6], F32)
        w_max = sb("w_max", [P, 6], F32)
        w_exp = sb("w_exp", [P, 6], F32)
        w_up = sb("w_up", [P, 4], F32)
        w_down = sb("w_down", [P, 4], F32)
        rowmax = sb("rowmax", [P, 8], F32)
        chanmax = sb("chanmax", [8, CG], F32)
        chanmax_rep = sb("chanmax_rep", [8, PH, CG], F32)
        yscale = sb("yscale", [P, 8], F32)
        yinv = sb("yinv", [P, 8], F32)
        tok_junk = sb("tok_junk", [P, CG], F32)
        tok_scale = sb("tok_scale", [P, 4], F32)
        abs_junk = sb("abs_junk", [P, L], BF16)
        x1max = sb("x1max", [P, 1], F32)
        x1max_all = sb("x1max_all", [P, 1], F32)
        pool_turn = sb("pool_turn", [1, 2], F32)
        bound = sb("bound", [P, 2], F32)
        t_pair = sb("t_pair", [P, 4, 2], F32)
        t_all = sb("t_all", [P, NT, 2], F32)
        z_lo = sb("z_lo", [R + E, P], F32)
        limes_nat = sb("limes_nat", [E, R], F32)
        gate_w = sb("gate_w", [R + E, 2 * E], F32)
        limes_n = sb("limes_n", [E, R], F32)
        b_parts = sb("b_parts", [3 * R, L], F16)
        z_scaled = sb("z_scaled", [R, 2, P], F32)
        z_parts = sb("z_parts", [3 * R, 2, P], F16)
        z_max = sb("z_max", [P, NT], F32)
        z_exp = sb("z_exp", [P, NT], F32)
        z_up = sb("z_up", [P, NT], F32)
        unscale_d = sb("unscale_d", [P, NT], F32)
        gsm = sb("gsm", [P, 6, NJ], F32)
        gmx = sb("gmx", [P, 8], F32)
        gateT = stage[0:E, NTOK:NTOK + NANCH]
        unscale = sb("unscale", [P, NT], F32)
        gate = yb[:, 0].rearrange("p n (j e) -> p n j e", e=E)
        top8 = yb[:, 1, 0, :].rearrange("p (j e) -> p j e", e=E)
        x2_in = x_in[:, :, :].rearrange("p s l -> p (s l)").bitcast(F16).rearrange(
            "p (s h c t) -> p s h c t", s=4, h=2, c=NL)
        xb_in = mixb_all[:, :, :].rearrange("p a t -> p (a t)").rearrange("p (s l) -> p s l", s=4)
        o_sb = x1

        ps = ctx.enter_context(nc.psum_tensor("ps", [P, 8 * 512], F32))

        def bank(n, k=1):
            return ps[:, n * 512:(n + k) * 512]

        ps_ph, ps_conv, ps_acc, ps_mix, ps_tr, ps_small = bank(0), bank(1, 2), bank(3, 2), bank(5), bank(6), bank(7)
        ps_trb = ps_tr.bitcast(BF16)

        agg_dram = nc.dram_tensor("agg_scratch", [B, CH, CH], F32, kind="Internal").ap()
        aggb_dram = nc.dram_tensor("aggb_scratch", [B * CH], F32, kind="Internal").ap()
        x2_dram = nc.dram_tensor("x2_scratch", [NT, P, 2 * L], F16, kind="Internal").ap()
        xb_dram = nc.dram_tensor("xb_scratch", [NT, P, L], F32, kind="Internal").ap()

        W_BANKS = (3, 4, 6) * 3 + (5, 3, 4) * 2 + (5,)

        def w_bank(n):
            return bank(W_BANKS[n])

        def agg_bank(n):
            return bank(5 if n % 2 == 0 else 7 if n < NL - 1 else 2)[0:B, :]

        def wq_buf(o):
            return yv[:, :, :].rearrange("p a b -> p (a b)") if o % 2 == 0 else u[:, :]

        x_t = x.rearrange("(t b) c l -> t (b c) l", b=2)
        out_t = out.rearrange("(t b) c l -> t (b c) l", b=2)

        block = ctx.enter_context(nc.Block())

        def at(i, c, k=1, d=0):
            return i * (4 * k) + (k * c + d)

        def wait(eng, name, val):
            if not isinstance(val, int) or val > 0:
                eng.wait_ge(sem(name), val)

        def bodies(eng, body, begin=2):
            first = 5
            n = (NT - 1 - first) // 8
            for t in range(begin, first):
                body(0, t, lambda o, t=t: 0 <= t + o < NT)
            with eng.Fori(0, n) as i:
                for c in range(first, first + 8):
                    body(i * 2, c, lambda o: True)
            for t in range(first + 8 * n, NT):
                body(2 * n, t - 8 * n, lambda o, t=t: 0 <= t + o < NT)

        @block.sync
        def _(sp):
            sp.dma_start(w_conv_nat[:, :, :], w_conv).then_inc(sem("conv_w_loaded"), 16)
            sp.dma_start(cond_nat[:, :], cond).then_inc(sem("cond_loaded"), 16)
            sp.dma_start(w_ctx_nat[:, :], w_ctx).then_inc(sem("cond_loaded"), 16)

            def load_wq(o):
                sp.dma_start(wq_nat[:, o * L:(o + 1) * L], w_q[o * P:(o + 1) * P, :]).then_inc(sem(f"wq_loaded{o}"), 16)

            load_wq(0)
            for g in range(GRP):
                sp.dma_start(fside_b[:, g:g + 1], fside[g * CG:(g + 1) * CG].rearrange("(a c) -> a c", a=1).to_broadcast([PH, CG])).then_inc(sem("fside_loaded"), 16)
            load_wq(1)
            sp.dma_start(mb2_b[:, :], mlp_b2.rearrange("(a k) -> a k", a=1).to_broadcast([B, NK])).then_inc(sem("mlp_loaded"), 16)
            load_wq(2)
            sp.dma_start(kw, mix_w.rearrange("k o i a -> k (o i a)")).then_inc(sem("kw_loaded"), 16)
            sp.dma_start(mixb_k[:, :], mix_b).then_inc(sem("kw_loaded"), 16)
            for o in range(3, NL):
                load_wq(o)
            sp.wait_ge(sem("conv_wT_ready"), 2)
            sp.wait_ge(sem("conv_w_zeroed"), 1)
            for p in range(PH):
                v = (p + 4) % PH
                sp.dma_start(conv_w[p * CG:(p + 1) * CG, :, v:v + TAPS, :], conv_wT[:, :, :, :]).then_inc(sem("conv_w_ready"), 16)
            sp.dma_start(x_in[:, 0, :], x_t[0]).then_inc(sem("x_loaded0"), 16)
            sp.dma_start(limes_nat[:, :], limes).then_inc(sem("limes_loaded"), 16)
            sp.dma_start(b_rank, w_b).then_inc(sem("limes_loaded"), 16)
            sp.dma_start(a_nat[:, :, :], w_a.rearrange("(c p) r -> p c r", p=P)).then_inc(sem("a_loaded"), 16)
            sp.dma_start(kw_flat[:, :], mix_w.rearrange("k o i a -> (k o i a)").rearrange("(p n) -> p n", p=P)).then_inc(sem("kw_flat_loaded"), 16)
            for a in range(4):
                sp.dma_start(w_nat[:, 2 * a:2 * a + 2, :],
                             w_ffn.rearrange("(a p) l -> p a l", p=P)[:, 2 * a:2 * a + 2, :]).then_inc(sem(f"w_loaded{a}"), 16)
            for t in range(1, 4):
                sp.dma_start(x_in[:, t, :], x_t[t]).then_inc(sem(f"x_loaded{t}"), 16)
            sp.dma_start(bias_b[:, :], b_ffn.rearrange("(a l) -> a l", a=1).to_broadcast([P, L])).then_inc(sem("bias_loaded"), 16)
            sp.wait_ge(sem("agg_ready"), 8)
            sp.dma_start(agg_dram, agg).then_inc(sem("agg_saved"), 16)
            sp.wait_ge(sem("agg_b_ready"), 1)
            sp.dma_start(aggb_dram.rearrange("(b o) -> b o", o=CH), agg_b[:, :]).then_inc(sem("agg_b_saved"), 16)
            sp.wait_ge(sem("agg_saved"), 16)
            sp.wait_ge(sem("mixT_zeroed"), 2)
            for e in range(2):
                sp.dma_start(mixT[e * CH:(e + 1) * CH, :, e * CH:(e + 1) * CH],
                             agg_dram.rearrange("(t e) i o -> e i t o", e=2)[e]).then_inc(sem("mixT_loaded"), 16)
            sp.wait_ge(sem("agg_b_saved"), 16)
            sp.dma_start(mixb_all[:, :, :].rearrange("p a t -> p (a t)"),
                         aggb_dram.rearrange("(a n) -> a n", a=1).to_broadcast([P, B * CH])).then_inc(sem("mixb_all_loaded"), 16)

            def step(i, c, load=True, xb_out=True, x2_out=True):
                if load:
                    wait(sp, "x1_ready", at(i, c, 2, -6))
                    sp.dma_start(x_in[:, c % 4, :], x_t[at(i, c)]).then_inc(sem(f"x_loaded{c % 4}"), 16)
                if x2_out:
                    wait(sp, "lo_ready", at(i, c, 2, -8))
                    sp.dma_start(x2_dram[at(i, c, 1, -5)],
                                 x2_cols[:, (c + 1) % 2].rearrange("p h c t -> p (h c t)")).then_inc(sem(f"x2_saved{(c + 1) % 2}"), 16)
                if xb_out:
                    wait(sp, "xb_ready", at(i, c, 1, -3))
                    sp.dma_start(xb_dram[at(i, c, 1, -4)], xb[:, c % 2, :]).then_inc(sem(f"xb_saved{c % 2}"), 16)

            for c in range(4):
                step(1, c, x2_out=c >= 1)
            with sp.Fori(2, NT // 4) as i:
                for c in range(4):
                    step(i, c)
            def fetch_x2(i, c):
                wait(sp, "dense_ready", at(i, c, 1, -3))
                sp.dma_start(x2_in[:, c % 4].rearrange("p h c t -> p (h c t)"), x2_dram[at(i, c)]).then_inc(sem(f"x2_loaded{c % 4}"), 16)

            def fetch_xb(i, c):
                wait(sp, "out_ready", at(i, c, 2, -6))
                sp.dma_start(xb_in[:, c % 4, :], xb_dram[at(i, c)]).then_inc(sem(f"xb_loaded{c % 4}"), 16)

            for c in range(5):
                step(NT // 4, c, load=False, xb_out=c < 4)
                if c < 4:
                    sp.wait_ge(sem("x1_ready"), 2 * (NT - 4 + c) + 2)
                    sp.wait_ge(sem(f"x2_saved{c % 2}"), 16 * (c // 2 + 1))
                    fetch_x2(0, c)
            sp.wait_ge(sem("u_ready"), 2 * NT)
            for c in range(4):
                sp.wait_ge(sem(f"xb_saved{c % 2}"), 16 * (c // 2 + 1))
                fetch_xb(0, c)
            for s in range(2):
                sp.wait_ge(sem(f"x2_saved{s}"), 16 * (NT // 2))
                sp.wait_ge(sem(f"xb_saved{s}"), 16 * (NT // 2))
            fetch_x2(1, 0)
            with sp.Fori(1, NT // 4 - 1) as i:
                for c in range(4):
                    fetch_x2(i, c + 1)
                    fetch_xb(i, c)
            for c in range(4):
                if c < 3:
                    fetch_x2(NT // 4 - 1, c + 1)
                fetch_xb(NT // 4 - 1, c)

        @block.tensor
        def _(pe):
            mm, tr = nc.tensor.matmul, nc.tensor.transpose
            pe.wait_ge(sem("ident_ready"), 3)
            pe.wait_ge(sem("conv_w_loaded"), 16)
            for k in range(TAPS):
                last = tr(ps_conv[0:CG, (TAPS - 1 - k) * CH:(TAPS - k) * CH], w_conv_nat[:, :, k], ident[0:CH, 0:CH])
            last.then_inc(sem("conv_wT_psum"), 1)
            pe.wait_ge(sem("cond_loaded"), 32)
            tr(ps_small[:, 0:B], cond_nat[:, :], ident[0:B, 0:B])
            tr(ps_small[:, B:B + CH], w_ctx_nat[:, :], ident[0:CH, 0:CH]).then_inc(sem("condT_psum"), 1)
            pe.wait_ge(sem("condT_ready"), 3)
            for g in range(GRP):
                last = mm(ps_small[:, 128 + g * B:128 + (g + 1) * B], w_ctx_rep[:, g].rearrange("p a c -> p (a c)"),
                          condT[:, :], start=True, stop=True)
            last.then_inc(sem("ctx_psum"), 1)
            pe.wait_ge(sem("mlp_loaded"), 16 * 6)
            mm(ps_mix[:, 0:B], mw0[:, :], condT[:, :], start=True, stop=True).then_inc(sem("mlp_psum"), 1)
            pe.wait_ge(sem("h_act"), 1)
            mm(ps_mix[:, 64:64 + B], mw1[:, :], h0[:, :], start=True, stop=True).then_inc(sem("mlp_psum"), 1)
            def wq_transposed(o):
                pe.wait_ge(sem("wq_ready"), o + 1)
                if o >= 2:
                    pe.wait_ge(sem("wqT_ready"), o - 1)
                bk = (ps_tr if o % 2 == 0 else ps_ph).bitcast(BF16)
                q = yq if o % 2 == 0 else yqT
                qv = q[:, :, :].rearrange("p a b -> p (a b)").rearrange("p (m e) -> p e m", e=PH)
                for p in range(PH):
                    last = tr(bk[:, p * P:(p + 1) * P], qv[:, p, :], identb[:, :])
                last.then_inc(sem("wqT_psum"), 1)

            def agg_weights(o):
                if o == NL - 1:
                    pe.wait_ge(sem("yb_ready"), 1)
                elif o >= 2:
                    pe.wait_ge(sem("agg_ready"), o - 1)
                mm(agg_bank(o), attT[:, :], kw[:, o * 512:(o + 1) * 512], start=True, stop=True).then_inc(sem("agg_psum"), 1)

            wq_transposed(0)
            pe.wait_ge(sem("h_act"), 2)
            mm(ps_mix[0:B, 128:128 + NK], h1[:, :], mw2[:, :], start=True, stop=True).then_inc(sem("mlp_psum"), 1)
            wq_transposed(1)
            pe.wait_ge(sem("att_ready"), 1)
            tr(ps_mix[0:NK, 192:192 + B], att[:, :], ident[0:B, 0:B]).then_inc(sem("mlp_psum"), 1)
            for o in range(2, NL):
                wq_transposed(o)
                if o == 2:
                    pe.wait_ge(sem("ybias_ready"), 1)
                    pe.wait_ge(sem("attT_ready"), 1)
                    pe.wait_ge(sem("kw_loaded"), 32)
                agg_weights(o - 2)

            def wsc_rows(os):
                for o in os:
                    last = mm(ps_acc[:, o * P:(o + 1) * P], wq_scale[:, o:o + 1].to_broadcast([P, P]), ident[:, :], start=True, stop=True)
                last.then_inc(sem("wsc_psum"), 1)

            def dense_weights(ns):
                for n in ns:
                    if n == 0:
                        for a in range(4):
                            pe.wait_ge(sem(f"w_loaded{a}"), 16)
                        pe.wait_ge(sem("wsc_ready"), 1)
                    if n == W_BANKS.index(5):
                        pe.wait_ge(sem("limesT_ready"), 1)
                    before = [m for m in range(n) if W_BANKS[m] == W_BANKS[n]]
                    if before:
                        pe.wait_ge(sem("w_lo_ready"), before[-1] + 1)
                    for o in range(4):
                        last = tr(w_bank(n)[:, o * P:(o + 1) * P],
                                  w_nat[:, 4 * (n % 2) + o, (n // 2) * P:(n // 2 + 1) * P], ident[:, :])
                    last.then_inc(sem("wT_psum"), 1)

            def phases(i, c, s):
                if s == 0:
                    wait(pe, "blk_ready", at(i, c, 1, 1))
                    wait(pe, "ph_ready", at(i, c, 4, 0))
                else:
                    wait(pe, "ph_ready", at(i, c, 4, 2))
                bk = ps_ph.rearrange("p (q m) -> p q m", q=4)
                for m in range(4):
                    last = tr(bk[:, :, m * 32:(m + 1) * 32], x_blk[:, m, s].rearrange("p e c -> p (e c)"), ident[:, :])
                last.then_inc(sem("ph_psum"), 1)

            def conv(i, c):
                wait(pe, "yb_ready", at(i, c))
                for g in (0, 2, 1, 3):
                    if g < 2:
                        wait(pe, "ph_ready", at(i, c, 4, 2 * g + 2))
                    o = ps_conv[:, g * 2 * MB:(g + 1) * 2 * MB]
                    w = conv_w[:, g].rearrange("p v c -> p (v c)")
                    xg = x_ph[:, g % 2, g // 2:GRP:2, :]
                    mm(o, w[:, P:2 * P], xg[:, :, 0:MB], start=True, stop=False)
                    last = mm(o, w[:, 0:P], xg[:, :, 1:MB + 1], start=False, stop=True)
                last.then_inc(sem("conv_ready"), 1)

            def max_rows(i, c):
                wait(pe, "rowmax_ready", at(i, c, 1, 1))
                wait(pe, "z_ready", at(i, c, 1, -3))
                tr(ps_small[0:8, 0:P], rowmax[:, :], ident[:, :]).then_inc(sem("rowmaxT_ready"), 1)

            def max_back(i, c):
                wait(pe, "chanmax_ready", at(i, c, 1, 1))
                mm(ps_small[:, 128:136], chanmax_rep[:, :, :].rearrange("p a c -> p (a c)"), ident[0:8, 0:8], start=True, stop=True)
                mm(ps_small[:, 144:144 + CG], set_rows[:, :], chanmax[:, :], start=True, stop=True).then_inc(sem("max_psum"), 1)

            def tokens_out(i, c):
                wait(pe, "yq_ready", at(i, c, 1, 1))
                for s in range(8):
                    last = tr(ps_trb[:, s * P:(s + 1) * P], yq[:, s, :], identb[:, :])
                last.then_inc(sem("yqT_psum"), 1)

            def int_product(i, c, h):
                wait(pe, "yqT_ready", at(i, c, 1, 1))
                if isinstance(i, int) and at(i, c) == 0 and h == 0:
                    pe.wait_ge(sem("w_lo_ready"), 2 * NL)
                wait(pe, "f_ready", at(i, c, 2, h - 1))
                for p in range(PH):
                    last = mm(ps_acc[:, h * HALF:(h + 1) * HALF], yqT[:, p, :], wqT[:, p, h * HALF:(h + 1) * HALF],
                              start=p == 0, stop=p == PH - 1)
                last.then_inc(sem("acc_ready"), 1)

            def mix(i, c, h):
                if isinstance(i, int) and at(i, c) == 0 and h == 0:
                    pe.wait_ge(sem("mixT_loaded"), 32)
                wait(pe, "x1_ready", at(i, c, 2, 1 + h))
                wait(pe, "u_ready", at(i, c, 2, h))
                for k in range(4):
                    ck = 4 * h + k
                    last = mm(ps_mix[:, k * P:(k + 1) * P], x1[:, c % 2, ck * P:(ck + 1) * P], mixT[:, at(i, c), :],
                              start=True, stop=True)
                last.then_inc(sem("mix_ready"), 1)

            def rank(i, c):
                if isinstance(i, int) and at(i, c) == 0:
                    pe.wait_ge(sem("z_w_ready"), 1)
                wait(pe, "lo_ready", at(i, c, 2, 2))
                steps = at(i, c, 1, 4)
                wait(pe, "tok_scale_ready", min(steps, NT) if isinstance(steps, int) else steps)
                wait(pe, "z_ready", at(i, c))
                for k in range(NL):
                    mm(ps_small[0:ZW, 256:384], z_w[:, k, :], x2_cols[:, c % 2, 0, k, :], start=k == 0, stop=False, skip_group_check=True)
                for k in range(NL):
                    last = mm(ps_small[0:R + E, 256:384], z_w[:, k, 0:R + E], x2_cols[:, c % 2, 1, k, :],
                              start=False, stop=k == NL - 1, skip_group_check=True)
                last.then_inc(sem("z_psum"), 1)

            def body(i, c, on):
                early = isinstance(i, int) and at(i, c) == 3
                if on(-3) and not early:
                    mix(i, c - 3, 0)
                if on(0):
                    conv(i, c)
                if on(-1):
                    max_rows(i, c - 1)
                if on(-3):
                    mix(i, c - 3, 0 if early else 1)
                if on(-1):
                    max_back(i, c - 1)
                if on(-2):
                    int_product(i, c - 2, 0)
                    if early:
                        mix(i, c - 3, 1)
                        phases(i, c + 1, 0)
                    int_product(i, c - 2, 1)
                if on(1):
                    phases(i, c + 1, 1 if early else 0)
                if on(-4):
                    rank(i, c - 4)
                if on(-1):
                    tokens_out(i, c - 1)
                if on(1) and not early:
                    phases(i, c + 1, 1)

            def dense_chunks(i, c, h, ks):
                if ks[0] == 0:
                    wait(pe, f"x2_loaded{c % 4}", i * 16 + 16 * (c // 4 + 1))
                    wait(pe, "folded", at(i, c, 2, h - 3))
                o = bank(2 * (c % 2) + h)
                for k in ks:
                    for n, (a, w) in enumerate(((0, 0), (0, 1), (1, 0))):
                        last = mm(o, x2_in[:, c % 4, a, k, :], ffn_wT[:, w, k, h * HALF:(h + 1) * HALF],
                                  start=k == 0 and n == 0, stop=k == NL - 1 and n == 2)
                if ks[-1] == NL - 1:
                    last.then_inc(sem("dense_half_ready" if h == 0 else "dense_ready"), 1)

            def dense_half(i, c, h):
                dense_chunks(i, c, h, range(NL))

            pe.wait_ge(sem("wqT_ready"), NL)
            phases(0, 0, 0)
            wsc_rows(range(0, NL // 2))
            phases(0, 0, 1)
            pe.wait_ge(sem("conv_w_ready"), 16 * PH)
            pe.wait_ge(sem("x_ph_zeroed"), 2)
            conv(0, 0)
            wsc_rows(range(NL // 2, NL))
            phases(0, 1, 0)
            agg_weights(NL - 2)
            dense_weights(range(0, 3))
            agg_weights(NL - 1)
            phases(0, 1, 1)
            max_rows(0, 0)
            dense_weights(range(3, 6))
            max_back(0, 0)
            pe.wait_ge(sem("agg_ready"), 8)
            mm(ps_mix[0:B, 256:256 + CH], attT[:, :], mixb_k[:, :], start=True, stop=True).then_inc(sem("agg_b_psum"), 1)
            conv(0, 1)
            pe.wait_ge(sem("limes_loaded"), 32)
            pe.wait_ge(sem("agg_b_ready"), 1)
            tr(ps_mix[0:R, 0:E], limes_nat[:, :], ident[0:E, 0:E]).then_inc(sem("limesT_psum"), 1)
            dense_weights(range(6, 9))
            phases(0, 2, 0)
            dense_weights(range(9, 12))
            phases(0, 2, 1)
            pe.wait_ge(sem("w_lo_ready"), 9)
            tokens_out(0, 0)
            dense_weights(range(12, 14))
            max_rows(0, 1)
            dense_weights(range(14, 16))
            max_back(0, 1)
            conv(0, 2)
            phases(0, 3, 0)
            int_product(0, 0, 0)
            int_product(0, 0, 1)
            phases(0, 3, 1)
            tokens_out(0, 1)
            bodies(pe, body, 3)

            mix(0, NT - 3, 0)
            pe.wait_ge(sem("ph_ready"), 4 * NT)
            dense_chunks(0, 0, 0, range(0, 2))
            max_rows(0, NT - 1)
            dense_chunks(0, 0, 0, range(2, 4))
            max_back(0, NT - 1)
            mix(0, NT - 3, 1)
            dense_chunks(0, 0, 0, range(4, 6))
            int_product(0, NT - 2, 0)
            int_product(0, NT - 2, 1)
            dense_chunks(0, 0, 0, range(6, 8))
            tokens_out(0, NT - 1)
            rank(0, NT - 4)
            mix(0, NT - 2, 0)
            int_product(0, NT - 1, 0)
            int_product(0, NT - 1, 1)
            mix(0, NT - 2, 1)
            pe.wait_ge(sem("yb_ready"), NT)
            dense_chunks(0, 0, 1, range(0, 4))
            mix(0, NT - 1, 0)
            rank(0, NT - 3)
            dense_chunks(0, 0, 1, range(4, 8))
            mix(0, NT - 1, 1)
            rank(0, NT - 2)
            dense_half(0, 1, 0)
            rank(0, NT - 1)
            pe.wait_ge(sem("f_ready"), 2 * NT)
            dense_chunks(0, 1, 1, range(0, 2))

            ps_g = bank(4, 4)
            pe.wait_ge(sem("z_ready"), NT)
            pe.wait_ge(sem("gate_w_ready"), 1)
            pe.wait_ge(sem("limesT_ready"), 1)
            anchors = zT.rearrange("p (j a e) -> p j a e", a=P, e=2)
            for j in range(NJ):
                if j % 2 == 0 and 2 + j // 2 < NL:
                    dense_chunks(0, 1, 1, range(2 + j // 2, 3 + j // 2))
                last = mm(ps_g[:, j * 2 * E:(j + 1) * 2 * E], anchors[0:R + E, j, :, 1], gate_w[:, :], start=True, stop=True)
            last.then_inc(sem("logits_psum"), 1)
            for h in range(2):
                dense_half(0, 2, h)
            pe.wait_ge(sem("gate_ready"), 1)
            pe.wait_ge(sem("u_ready"), 2 * NT)
            for j in range(NJ):
                if j % 4 == 0:
                    dense_chunks(0, 3, 0, range(j // 4, j // 4 + 1))
                last = tr(ps_g[0:E, j * P:(j + 1) * P], gate[:, 7, j, :], ident[:, :])
            last.then_inc(sem("gateT_psum"), 1)
            dense_chunks(0, 3, 0, range(NJ // 4, NL))
            pe.wait_ge(sem("gateT_ready"), 1)
            for k in range(4):
                mm(ps_g[0:R, k * 512:(k + 1) * 512], limes_n[:, :], gateT[:, k * 512:(k + 1) * 512],
                   start=True, stop=True).then_inc(sem("pmix_psum"), 1)
                dense_chunks(0, 3, 1, range(2 * k, 2 * k + 2))
            dense_half(1, 0, 0)

            def delta(i, c):
                wait(pe, "z_parts_ready", at(i, c, 1, 1))
                wait(pe, "out_ready", at(i, c, 2, -2))
                for h in range(2):
                    last = mm(bank(4 + 2 * (c % 2) + h), z_parts[:, c % 2, :], b_parts[:, h * HALF:(h + 1) * HALF], start=True, stop=True)
                last.then_inc(sem("delta_ready"), 1)

            delta(0, 0)
            delta(0, 1)
            dense_half(1, 0, 1)
            delta(0, 2)
            with pe.Fori(1, NT // 4 - 1) as i:
                for c in range(1, 5):
                    for h in range(2):
                        dense_half(i, c, h)
                    delta(i, c - 2)
            j = NT // 4 - 1
            for c in range(1, 3):
                for h in range(2):
                    dense_half(j, c, h)
                delta(j, c - 2)
            delta(j, 1)
            dense_half(j, 3, 0)
            delta(j, 2)
            delta(j, 3)
            dense_half(j, 3, 1)

        @block.scalar
        def _(act):
            A = nc.scalar.activation
            for dst, src in ((mw0[:, :], mlp_w0), (mw1[:, :], mlp_w1), (mw2[:, :], mlp_w2),
                             (mb01[:, 0:1], mlp_b0.rearrange("(p a) -> p a", a=1)),
                             (mb01[:, 1:2], mlp_b1.rearrange("(p a) -> p a", a=1))):
                act.dma_start(dst, src).then_inc(sem("mlp_loaded"), 16)

            act.wait_ge(sem("conv_wT_psum"), 1)
            A(conv_wT[:, :, 0:8, :].rearrange("p g k o -> p k g o"), ps_conv[0:CG, 0:512].rearrange("p (k g o) -> p k g o", k=8, g=GRP), ACT.Copy).then_inc(sem("conv_wT_ready"), 1)
            A(conv_wT[:, :, 8, :], ps_conv[0:CG, 512:576].rearrange("p (g o) -> p g o", g=GRP), ACT.Copy).then_inc(sem("conv_wT_ready"), 1)
            act.wait_ge(sem("condT_psum"), 1)
            A(condT[:, :], ps_small[:, 0:B], ACT.Copy).then_inc(sem("condT_ready"), 1)
            A(w_ctxT[:, :], ps_small[:, B:B + CH], ACT.Copy).then_inc(sem("w_ctxT_ready"), 1)
            act.wait_ge(sem("w_ctxT_ready"), 1)
            for g in range(GRP):
                last = A(w_ctx_rep[:, g], w_ctxT[:, g * CG:(g + 1) * CG].unsqueeze(1).to_broadcast([P, PH, CG]), ACT.Copy)
            last.then_inc(sem("condT_ready"), 2)
            def wq_scaled(o):
                act.wait_ge(sem("wq_inv_ready"), o + 1)
                if o >= 2:
                    act.wait_ge(sem("wq_ready"), o - 1)
                A(wq_buf(o), wq_nat[:, o * L:(o + 1) * L], ACT.Copy, scale=wq_inv[:, o:o + 1]).then_inc(sem("wq_scaled"), 1)

            def wq_out(o):
                act.wait_ge(sem("wqT_psum"), o + 1)
                bk = (ps_tr if o % 2 == 0 else ps_ph).bitcast(BF16)
                A(wqT[:, :, o * P:(o + 1) * P], bk.rearrange("p (e c) -> p e c", e=PH), ACT.Copy).then_inc(sem("wqT_ready"), 1)

            def agg_out(o):
                act.wait_ge(sem("agg_psum"), o + 1)
                A(agg[:, :, 8 * o:8 * o + 8].rearrange("b i o -> b o i"),
                  agg_bank(o).rearrange("b (o i) -> b o i", o=8), ACT.Copy).then_inc(sem("agg_ready"), 1)

            wq_scaled(0)
            act.wait_ge(sem("mlp_psum"), 1)
            A(h0[:, :], ps_mix[:, 0:B], ACT.Gelu, bias=mb01[:, 0:1]).then_inc(sem("h_act"), 1)
            wq_scaled(1)
            act.wait_ge(sem("mlp_psum"), 2)
            A(h1[:, :], ps_mix[:, 64:64 + B], ACT.Gelu, bias=mb01[:, 1:2]).then_inc(sem("h_act"), 1)
            wq_out(0)
            act.wait_ge(sem("att_logits_ready"), 2)
            A(att_e[:, :], att[:, :], ACT.Exp, bias=att_s[:, 0:1]).then_inc(sem("att_exp_ready"), 1)
            wq_scaled(2)
            wq_out(1)
            act.wait_ge(sem("mlp_psum"), 4)
            A(attT[:, :], ps_mix[0:NK, 192:192 + B], ACT.Copy).then_inc(sem("attT_ready"), 1)
            wq_scaled(3)
            for o in range(2, NL):
                wq_out(o)
                agg_out(o - 2)
                if o + 2 < NL:
                    wq_scaled(o + 2)
            def dense_weights(ns):
                for n in ns:
                    if n == 0:
                        act.wait_ge(sem("w_scale_ready"), 2)
                    act.wait_ge(sem("wT_psum"), n + 1)
                    h = slice((n % 2) * HALF, (n % 2 + 1) * HALF)
                    A(ffn_wT[:, 0, n // 2, h], w_bank(n), ACT.Copy, scale=w_up[:, 0:1]).then_inc(sem("w_hi_ready"), 1)

            def rank_weights():
                act.wait_ge(sem("z_w_zeroed"), 1)
                A(z_w[:, :, 0:R], a_nat[:, :, :], ACT.Copy, scale=w_up[:, 1:2]).then_inc(sem("rank_hi_ready"), 1)
                for n in (0, 2):
                    A(b_parts[n * R:(n + 1) * R, :], b_rank[:, :], ACT.Copy, scale=w_up[0:R, 3:4]).then_inc(sem("rank_hi_ready"), 1)

            def phase_rows(i, c, s):
                wait(act, "ph_psum", at(i, c, 2, s + 1))
                bk = ps_ph.rearrange("p (q m) -> p q m", q=4)
                A(x_ph[0:64, s, :, 0:MB], bk[0:64], ACT.Copy).then_inc(sem("ph_ready"), 1)
                A(x_ph[64:128, s, :, 1:MB + 1], bk[64:128], ACT.Copy).then_inc(sem("ph_ready"), 1)

            def scale_rows(i, c):
                wait(act, "yinv_ready", at(i, c, 1, 1))
                wait(act, "yq_ready", at(i, c))
                for s in range(8):
                    last = A(yv[:, s, :], yb[:, c % 2, s, :], ACT.Copy, scale=yinv[:, s:s + 1])
                last.then_inc(sem("yv_ready"), 1)

            def tokens_sb(i, c):
                wait(act, "yqT_psum", at(i, c, 1, 1))
                A(yqT[:, :, :].rearrange("m p (s c) -> m s p c", s=8),
                  ps_trb.rearrange("m (s p c) -> m s p c", s=8, p=PH), ACT.Copy).then_inc(sem("yqT_ready"), 1)

            def high(i, c, h):
                wait(act, "u_ready", at(i, c, 2, 1 + h))
                if h == 0:
                    wait(act, "t_ready", at(i, c, 1, 1))
                    if not isinstance(i, int) or 4 * i + c >= 2:
                        wait(act, f"x2_saved{c % 2}", i * 32 + 16 * (c // 2))
                    wait(act, "z_psum", at(i, c, 1, -1))
                A(x2_cols[:, c % 2, 0, 4 * h:4 * h + 4, :].rearrange("p c t -> p (c t)"), u[:, h * HALF:(h + 1) * HALF],
                  ACT.Copy, scale=t_pair[:, c % 4, 0:1]).then_inc(sem("hi_ready"), 1)

            def rank_low(i, c):
                wait(act, "z_psum", at(i, c, 1, 1))
                wait(act, "z_ready", at(i, c))
                A(z_lo[:, :], ps_small[64:ZW, 256:384], ACT.Copy, scale=t_pair[64:ZW, c % 4, 1:2]).then_inc(sem("z_lo_ready"), 1)

            def row_sums(i, c):
                wait(act, "x1_ready", at(i, c, 2, 2))
                wait(act, "x1max_all_ready", at(i, c))
                A(abs_junk[:, :], x1[:, c % 2, :], ACT.Abs, accum_out=x1max[:, :]).then_inc(sem("x1max_ready"), 1)

            def body(i, c, on):
                if on(-3):
                    row_sums(i, c - 3)
                if on(-2):
                    tokens_sb(i, c - 2)
                if on(-1):
                    scale_rows(i, c - 1)
                early = isinstance(i, int) and at(i, c) == 3
                if on(-3) and not early:
                    high(i, c - 3, 0)
                if on(1):
                    phase_rows(i, c + 1, 0)
                if early:
                    phase_rows(i, c + 1, 1)
                    high(i, c - 3, 0)
                if on(-3):
                    high(i, c - 3, 1)
                if on(-4):
                    rank_low(i, c - 4)
                if on(1) and not early:
                    phase_rows(i, c + 1, 1)

            act.wait_ge(sem("x_ph_zeroed"), 2)
            phase_rows(0, 0, 0)
            phase_rows(0, 0, 1)
            for n, junk in enumerate((abs_junk[:, :], f16[:, :], x1[:, 0, :])):
                act.wait_ge(sem(f"w_loaded{(5 + n) // 2}"), 16)
                A(junk, w_nat[:, 5 + n, :], ACT.Abs, accum_out=w_part[:, 3 + n:4 + n]).then_inc(sem("w_sums_ready"), 1)
            act.wait_ge(sem("wsc_psum"), 2)
            A(wsc_b[:, :], ps_acc, ACT.Copy).then_inc(sem("wsc_ready"), 1)
            phase_rows(0, 1, 0)
            dense_weights(range(0, 2))
            agg_out(NL - 2)
            dense_weights(range(2, 3))
            phase_rows(0, 1, 1)
            dense_weights(range(3, 5))
            agg_out(NL - 1)
            dense_weights(range(5, 6))
            scale_rows(0, 0)
            act.wait_ge(sem("limesT_psum"), 1)
            act.wait_ge(sem("gate_w_zeroed"), 1)
            A(gate_w[0:R, E:2 * E], ps_mix[0:R, 0:E], ACT.Copy).then_inc(sem("limesT_ready"), 1)
            dense_weights(range(6, 10))
            phase_rows(0, 2, 0)
            dense_weights(range(10, 13))
            phase_rows(0, 2, 1)
            dense_weights(range(13, 16))
            tokens_sb(0, 0)
            scale_rows(0, 1)
            phase_rows(0, 3, 0)
            rank_weights()
            phase_rows(0, 3, 1)
            bodies(act, body, 3)
            tokens_sb(0, NT - 2)
            row_sums(0, NT - 3)
            scale_rows(0, NT - 1)
            for h in range(2):
                high(0, NT - 3, h)
            tokens_sb(0, NT - 1)
            rank_low(0, NT - 4)
            row_sums(0, NT - 2)
            for h in range(2):
                high(0, NT - 2, h)
            rank_low(0, NT - 3)
            row_sums(0, NT - 1)
            for h in range(2):
                high(0, NT - 1, h)
            rank_low(0, NT - 2)
            rank_low(0, NT - 1)

            act.wait_ge(sem("gate_in_ready"), 1)
            A(gate[:, 3], gate[:, 2], ACT.Exp).then_inc(sem("gate_exp_ready"), 1)
            act.wait_ge(sem("gate_in_ready"), 2)
            A(gate[:, 5], gate[:, 5], ACT.Exp, scale=-2.0).then_inc(sem("gate_exp_ready"), 1)
            act.wait_ge(sem("gateT_psum"), 1)
            for s in range(2):
                act.wait_ge(sem(f"x2_saved{s}"), 16 * (NT // 2))
            A(gateT[:, :], bank(4, 4)[0:E, :], ACT.Copy).then_inc(sem("gateT_ready"), 1)

            def store(i, c):
                wait(act, "out_ready", at(i, c, 2, 2))
                act.dma_start(out_t[at(i, c)], o_sb[:, c % 2, :]).then_inc(sem(f"out_saved{c % 2}"), 16)

            with act.Fori(0, NT // 4 - 1) as i:
                for c in range(4):
                    store(i, c)
            for c in range(3):
                store(NT // 4 - 1, c)
            for h in range(2):
                act.wait_ge(sem("out_ready"), 2 * NT - 1 + h)
                act.dma_start(out_t[NT - 1][:, h * HALF:(h + 1) * HALF], o_sb[:, 1, h * HALF:(h + 1) * HALF]).then_inc(sem("out_saved1"), 16)
            for s in range(2):
                act.wait_ge(sem(f"out_saved{s}"), 16 * (NT // 2 + s))

        @block.gpsimd
        def _(pool):
            g = nc.gpsimd
            g.memset(ident[:, :], 0.0).then_inc(sem("ident_zero"), 1)
            g.memset(identb[:, :], 0.0).then_inc(sem("ident_zero"), 1)
            g.memset(set_rows[:, :], 1.0).then_inc(sem("ident_zero"), 1)
            pool.wait_ge(sem("ident_zero"), 3)
            for m in (ident, identb):
                g.affine_select(out=m[:, :], in_=m[:, :], compare_op=ALU.not_equal, fill=1.0, base=0,
                                pattern=[[-1, P]], channel_multiplier=1).then_inc(sem("ident_ready"), 1)
            g.affine_select(out=set_rows[:, :], in_=set_rows[:, :], compare_op=ALU.is_ge, fill=0.0, base=0,
                            pattern=[[1, P]], channel_multiplier=-CG).then_inc(sem("set_rows_half"), 1)
            pool.wait_ge(sem("set_rows_half"), 1)
            g.affine_select(out=set_rows[:, :], in_=set_rows[:, :], compare_op=ALU.is_ge, fill=0.0, base=CG - 1,
                            pattern=[[-1, P]], channel_multiplier=CG).then_inc(sem("ident_ready"), 1)
            g.memset(conv_w[:, :, :, :], 0.0).then_inc(sem("conv_w_zeroed"), 1)
            pool.wait_ge(sem("conv_w_zeroed"), 1)
            g.memset(x_ph[0:64, :, :, MB:MB + 1], 0.0).then_inc(sem("x_ph_zeroed"), 1)
            pool.wait_ge(sem("x_ph_zeroed"), 1)
            g.memset(x_ph[64:128, :, :, 0:1], 0.0).then_inc(sem("x_ph_zeroed"), 1)
            pool.wait_ge(sem("x_ph_zeroed"), 2)
            g.memset(z_w[:, :, :], 0.0).then_inc(sem("z_w_zeroed"), 1)
            def mixT_zero(e):
                g.memset(mixT[e * CH:(e + 1) * CH, :, (1 - e) * CH:(2 - e) * CH], 0.0).then_inc(sem("mixT_zeroed"), 1)

            pool.wait_ge(sem("z_w_zeroed"), 1)
            mixT_zero(1)
            pool.wait_ge(sem("w_max_ready"), 6)
            pool.wait_ge(sem("mixT_zeroed"), 1)
            g.partition_all_reduce(w_exp[:, :], w_max[:, :], P, RMAX).then_inc(sem("w_max_all"), 1)
            pool.wait_ge(sem("agg_psum"), 8)
            mixT_zero(0)
            pool.wait_ge(sem("mixT_zeroed"), 2)

            def tile_max(i, c):
                wait(pool, "x1max_ready", at(i, c, 1, 1))
                wait(pool, "t_ready", at(i, c))
                g.tensor_tensor(pool_turn[:, 1:2], pool_turn[:, 0:1], pool_turn[:, 0:1], ALU.add)
                g.partition_all_reduce(x1max_all[:, :], x1max[:, :], P, RMAX).then_inc(sem("x1max_all_ready"), 1)

            def with_bias(i, c):
                wait(pool, "x1_ready", at(i, c, 2, 2))
                if isinstance(i, int) and at(i, c) == 0:
                    pool.wait_ge(sem("w_lo_ready"), 2 * NL)
                if not isinstance(i, int) or 4 * i + c >= 2:
                    wait(pool, f"xb_saved{c % 2}", i * 32 + 16 * (c // 2))
                g.tensor_tensor(xb[:, c % 2, :], x1[:, c % 2, :], bias_b[:, :], ALU.add).then_inc(sem("xb_ready"), 1)

            def add_layer0(i, c, h):
                wait(pool, "f_ready", at(i, c, 2, h + 1))
                if isinstance(i, int) and at(i, c) == 1 and h == 0:
                    pool.wait_ge(sem("b_parts_ready"), 2)
                if h == 0:
                    wait(pool, "mix_ready", at(i, c, 2, -2))
                    wait(pool, "x1max_ready", at(i, c, 1, -1))
                s = slice(h * HALF, (h + 1) * HALF)
                g.tensor_tensor(x1[:, c % 2, s], x_in[:, c % 4, s], f16[:, s], ALU.add).then_inc(sem("x1_ready"), 1)

            def body(i, c, on):
                if on(-3):
                    tile_max(i, c - 3)
                    with_bias(i, c - 3)
                if on(-2):
                    add_layer0(i, c - 2, 0)
                    add_layer0(i, c - 2, 1)

            g.memset(pool_turn[:, :], 0.0).then_inc(sem("pool_turn_ready"), 1)
            pool.wait_ge(sem("pool_turn_ready"), 1)
            pool.wait_ge(sem("bias_loaded"), 16)
            bodies(pool, body)
            for t in (NT - 3, NT - 2, NT - 1):
                tile_max(0, t)
                if t < NT - 1:
                    pool.wait_ge(sem("xb_ready"), t)
                    add_layer0(0, t + 1, 0)
                    add_layer0(0, t + 1, 1)
                with_bias(0, t)

            pool.wait_ge(sem("gmax_ready"), 2)
            g.partition_all_reduce(gmx[:, 2:4], gmx[:, 0:2], P, RMAX).then_inc(sem("gmax_all"), 1)
            pool.wait_ge(sem("z_max_ready"), 4)
            g.partition_all_reduce(z_exp[:, :], z_max[:, :], P, RMAX).then_inc(sem("z_max_all_ready"), 1)

        @block.vector
        def _(dve):
            v = nc.vector
            chain = [0]

            def link(ins):
                chain[0] += 1
                ins.then_inc(sem("vector_chain"), 1)
                dve.wait_ge(sem("vector_chain"), chain[0])

            dve.wait_ge(sem("ident_ready"), 3)
            v.memset(gate_w[:, :], 0.0).then_inc(sem("gate_w_zeroed"), 1)
            dve.wait_ge(sem("gate_w_zeroed"), 1)
            v.tensor_copy(gate_w[R:R + E, 0:E], ident[R:R + E, R:R + E]).then_inc(sem("gate_w_ready"), 1)
            v.tensor_reduce(chan_mask[:, :], ident[:, :].rearrange("p (s c) -> p c s", c=CG), AX.X, ALU.add).then_inc(sem("masks_ready"), 1)
            def channel_bias():
                dve.wait_ge(sem("ctx_psum"), 1)
                dve.wait_ge(sem("fside_loaded"), 16 * GRP)
                v.tensor_tensor(ybias[:, :, :].rearrange("p b g -> p g b"), ps_small[:, 128:128 + GRP * B].rearrange("p (g b) -> p g b", g=GRP),
                                fside_b[:, :].unsqueeze(2).to_broadcast([P, GRP, B]), ALU.add).then_inc(sem("ybias_ready"), 1)

            def attention_logits():
                dve.wait_ge(sem("mlp_psum"), 3)
                v.tensor_tensor(att[:, :], ps_mix[0:B, 128:128 + NK], mb2_b[:, :], ALU.add).then_inc(sem("att_logits_ready"), 1)
                dve.wait_ge(sem("att_logits_ready"), 1)
                v.tensor_reduce(att_s[:, 0:1], att[:, :], AX.X, ALU.max, negate=True).then_inc(sem("att_logits_ready"), 1)

            def attention():
                dve.wait_ge(sem("att_exp_ready"), 1)
                link(v.tensor_reduce(att_s[:, 1:2], att_e[:, :], AX.X, ALU.add))
                link(v.reciprocal(att_s[:, 2:3], att_s[:, 1:2]))
                v.tensor_scalar(att[:, :], att_e[:, :], att_s[:, 2:3], None, ALU.mult).then_inc(sem("att_ready"), 1)

            def wq_scales(o):
                dve.wait_ge(sem(f"wq_loaded{o}"), 16)
                link(v.tensor_reduce(wq_max[:, o:o + 1], wq_nat[:, o * L:(o + 1) * L], AX.X, ALU.max, apply_absolute_value=True))
                link(v.tensor_scalar(wq_scale[:, o:o + 1], wq_max[:, o:o + 1], 1.0 / QMAX, 1e-30, ALU.mult, ALU.max))
                v.reciprocal(wq_inv[:, o:o + 1], wq_scale[:, o:o + 1]).then_inc(sem("wq_inv_ready"), 1)

            def wq_rounded(o):
                dve.wait_ge(sem("wq_scaled"), o + 1)
                if o >= 2:
                    dve.wait_ge(sem("wqT_psum"), o - 1)
                q = yq if o % 2 == 0 else yqT
                v.tensor_scalar(q[:, :, :].rearrange("p a b -> p (a b)"), wq_buf(o), MAGIC, -MAGIC, ALU.add, ALU.add).then_inc(sem("wq_ready"), 1)

            wq_scales(0)
            wq_scales(1)
            channel_bias()
            wq_rounded(0)
            wq_scales(2)
            attention_logits()
            wq_rounded(1)
            attention()
            wq_scales(3)
            for o in range(2, NL):
                wq_rounded(o)
                if o + 2 < NL:
                    wq_scales(o + 2)

            def mixing_bias():
                dve.wait_ge(sem("agg_b_psum"), 1)
                v.tensor_copy(agg_b[:, :], ps_mix[0:B, 256:256 + CH]).then_inc(sem("agg_b_ready"), 1)

            def small_maxima():
                link(v.memset(w_max[:, :], 0.0))
                dve.wait_ge(sem("limes_loaded"), 32)
                v.tensor_reduce(w_max[0:E, 2:3], limes_nat[:, :], AX.X, ALU.max, apply_absolute_value=True).then_inc(sem("w_max_ready"), 1)
                v.tensor_reduce(w_max[0:R, 3:4], b_rank[:, :], AX.X, ALU.max, apply_absolute_value=True).then_inc(sem("w_max_ready"), 1)
                dve.wait_ge(sem("a_loaded"), 16)
                v.tensor_reduce(w_max[:, 1:2], a_nat[:, :, :], AX.XY, ALU.max, apply_absolute_value=True).then_inc(sem("w_max_ready"), 1)
                dve.wait_ge(sem("kw_flat_loaded"), 16)
                dve.wait_ge(sem("kw_loaded"), 32)
                v.tensor_reduce(w_max[:, 4:5], kw_flat[:, :], AX.X, ALU.max, apply_absolute_value=True).then_inc(sem("w_max_ready"), 1)
                v.tensor_reduce(w_max[0:NK, 5:6], mixb_k[:, :], AX.X, ALU.max, apply_absolute_value=True).then_inc(sem("w_max_ready"), 1)

            def dense_maxima(n, chunks):
                dve.wait_ge(sem(f"w_loaded{chunks[0] // 2}"), 16)
                v.tensor_reduce(w_part[:, n:n + 1], w_nat[:, chunks[0]:chunks[-1] + 1, :], AX.XY, ALU.max, apply_absolute_value=True).then_inc(sem("w_part_ready"), 1)

            def dense_bound():
                dve.wait_ge(sem("w_part_ready"), 3)
                dve.wait_ge(sem("w_sums_ready"), 3)
                v.tensor_reduce(w_max[:, 0:1], w_part[:, :], AX.X, ALU.max).then_inc(sem("w_max_ready"), 1)

            def weight_scales():
                dve.wait_ge(sem("w_max_all"), 1)
                v.tensor_scalar(scal[:, 0:1], w_exp[:, 4:5], float(CH), None, ALU.mult)
                v.tensor_scalar(scal[:, 1:2], w_exp[:, 5:6], 1e-20, None, ALU.add)
                link(v.tensor_scalar(w_exp[:, 0:4], w_exp[:, 0:4], 1e-20, None, ALU.max))
                link(v.tensor_scalar(w_exp[:, 0:4].bitcast(U32), w_exp[:, 0:4].bitcast(U32), EXPMASK, None, ALU.bitwise_and))
                v.tensor_scalar(w_up[:, :].bitcast(I32), w_exp[:, 0:4].bitcast(I32), -1.0, float((254 + TOP) << 23),
                                ALU.mult, ALU.add).then_inc(sem("w_scale_ready"), 1)
                v.tensor_scalar(w_down[:, :].bitcast(I32), w_exp[:, 0:4].bitcast(I32), float(-(TOP << 23)), None,
                                ALU.add).then_inc(sem("w_scale_ready"), 1)
                dve.wait_ge(sem("w_scale_ready"), 2)

            def dense_weights(ns):
                for n in ns:
                    dve.wait_ge(sem("w_hi_ready"), n + 1)
                    h = slice((n % 2) * HALF, (n % 2 + 1) * HALF)
                    v.scalar_tensor_tensor(ffn_wT[:, 1, n // 2, h], w_bank(n), w_up[:, 0:1], ffn_wT[:, 0, n // 2, h],
                                           ALU.mult, ALU.subtract).then_inc(sem("w_lo_ready"), 1)

            def rank_weights():
                dve.wait_ge(sem("w_lo_ready"), 2 * NL)
                dve.wait_ge(sem("rank_hi_ready"), 3)
                v.scalar_tensor_tensor(z_w[:, :, 64:64 + R], a_nat[:, :, :], w_up[:, 1:2], z_w[:, :, 0:R], ALU.mult, ALU.subtract)
                v.tensor_copy(z_w[:, :, R:R + E], ffn_wT[:, 0, :, 0:E])
                v.tensor_copy(z_w[:, :, 64 + R:64 + R + E], ffn_wT[:, 1, :, 0:E]).then_inc(sem("z_w_ready"), 1)
                v.scalar_tensor_tensor(b_parts[R:2 * R, :], b_rank[:, :], w_up[0:R, 3:4], b_parts[0:R, :], ALU.mult, ALU.subtract).then_inc(sem("b_parts_ready"), 1)
                v.tensor_scalar(limes_n[:, :], limes_nat[:, :], w_up[0:E, 2:3], 2.0 ** -(TOP + 1), ALU.mult, ALU.mult).then_inc(sem("b_parts_ready"), 1)

            def blocks(i, c):
                wait(dve, f"x_loaded{c % 4}", i * 16 + 16 * (c // 4 + 1))
                wait(dve, "ph_psum", at(i, c, 2, 0))
                for a in range(4):
                    last = v.transpose(x_blk[:, a].rearrange("p s e c -> p e s c"),
                                       x_in[:, c % 4, a * 256:(a + 1) * 256].rearrange("p (m e) -> p e m", e=PH))
                last.then_inc(sem("blk_ready"), 1)

            def conv_bias(i, c):
                wait(dve, "conv_ready", at(i, c, 1, 1))
                wait(dve, "yv_ready", at(i, c, 1, -1))
                v.tensor_tensor(yb[:, c % 2].rearrange("p (b g) m -> p b g m", b=2), ps_conv.rearrange("p (g b m) -> p b g m", g=GRP, b=2),
                                ybias[:, bass.ds(at(i, c, 2), 2), :].unsqueeze(3).to_broadcast([P, 2, GRP, MB]), ALU.add).then_inc(sem("yb_ready"), 1)

            def row_max(i, c):
                wait(dve, "yb_ready", at(i, c, 1, 1))
                v.tensor_reduce(rowmax[:, :], yb[:, c % 2], AX.X, ALU.max, apply_absolute_value=True).then_inc(sem("rowmax_ready"), 1)

            def tile_scale(i, c):
                wait(dve, "x1max_all_ready", at(i, c, 1, 1))
                v.tensor_scalar(bound[:, 0:1], x1max_all[:, :], scal[:, 0:1], scal[:, 1:2], ALU.mult, ALU.add).then_inc(sem("bound_ready"), 1)
                wait(dve, "bound_ready", at(i, c, 2, 1))
                v.tensor_scalar(bound[:, 1:2].bitcast(U32), bound[:, 0:1].bitcast(U32), EXPMASK, None, ALU.bitwise_and).then_inc(sem("bound_ready"), 1)
                wait(dve, "bound_ready", at(i, c, 2, 2))
                v.tensor_scalar(t_pair[:, c % 4, 0:1].bitcast(I32), bound[:, 1:2].bitcast(I32), -1.0, float((254 + TOP) << 23), ALU.mult, ALU.add).then_inc(sem("t_half"), 1)
                v.tensor_scalar(t_pair[:, c % 4, 1:2].bitcast(I32), bound[:, 1:2].bitcast(I32), float(-(TOP << 23)), None, ALU.add).then_inc(sem("t_half"), 1)
                wait(dve, "t_half", at(i, c, 2, 2))
                v.tensor_copy(t_all[:, at(i, c), :], t_pair[:, c % 4, :]).then_inc(sem("t_ready"), 1)

            def rank_out(i, c):
                wait(dve, "z_lo_ready", at(i, c, 1, 1))
                v.scalar_tensor_tensor(zT[0:R + E, bass.ds(at(i, c, P), P)], ps_small[0:R + E, 256:384], t_pair[0:R + E, c % 4, 1:2],
                                       z_lo[:, :], ALU.mult, ALU.add).then_inc(sem("z_ready"), 1)

            def chan_max(i, c):
                wait(dve, "rowmaxT_ready", at(i, c, 1, 1))
                v.tensor_reduce(chanmax[:, :], ps_small[0:8, 0:P].rearrange("p (a c) -> p c a", a=PH), AX.X, ALU.max).then_inc(sem("chanmax_half"), 1)
                wait(dve, "chanmax_half", at(i, c, 1, 1))
                v.tensor_copy(chanmax_rep[:, :, :], chanmax[:, :].unsqueeze(1).to_broadcast([8, PH, CG])).then_inc(sem("chanmax_ready"), 1)

            def scales(i, c):
                wait(dve, "max_psum", at(i, c, 1, 1))
                v.tensor_scalar(yscale[:, :], ps_small[:, 128:136], 1.0 / QMAX, 1e-30, ALU.mult, ALU.max).then_inc(sem("yscale_ready"), 1)
                v.tensor_tensor_reduce(tok_junk[:, :], ps_small[:, 144:144 + CG], chan_mask[:, :], scale=1.0 / QMAX, scalar=0.0,
                                       op0=ALU.mult, op1=ALU.add, accum_out=tok_scale[:, c % 4:c % 4 + 1]).then_inc(sem("tok_scale_ready"), 1)
                wait(dve, "yscale_ready", at(i, c, 1, 1))
                wait(dve, "yv_ready", at(i, c))
                v.reciprocal(yinv[:, :], yscale[:, :]).then_inc(sem("yinv_ready"), 1)

            def mixed(i, c, h):
                if isinstance(i, int) and at(i, c) == 0 and h == 0:
                    dve.wait_ge(sem("mixb_all_loaded"), 16)
                wait(dve, "mix_ready", at(i, c, 2, h + 1))
                wait(dve, "lo_ready", at(i, c, 2, h - 1))
                v.tensor_tensor(u[:, h * HALF:(h + 1) * HALF].rearrange("p (k t) -> p k t", k=4),
                                ps_mix.rearrange("p (k t) -> p k t", k=4),
                                mixb_all[:, bass.ds(at(i, c), 1), :].to_broadcast([P, 4, P]), ALU.add).then_inc(sem("u_ready"), 1)

            def low(i, c, h):
                wait(dve, "hi_ready", at(i, c, 2, h + 1))
                v.scalar_tensor_tensor(x2_cols[:, c % 2, 1, 4 * h:4 * h + 4, :].rearrange("p k t -> p (k t)"), u[:, h * HALF:(h + 1) * HALF],
                                       t_pair[:, c % 4, 0:1], x2_cols[:, c % 2, 0, 4 * h:4 * h + 4, :].rearrange("p k t -> p (k t)"),
                                       ALU.mult, ALU.subtract).then_inc(sem("lo_ready"), 1)

            def layer0(i, c, h):
                wait(dve, "acc_ready", at(i, c, 2, h + 1))
                wait(dve, "tok_scale_ready", at(i, c, 1, 1))
                wait(dve, "x1_ready", at(i, c, 2, h - 1))
                s = slice(h * HALF, (h + 1) * HALF)
                v.scalar_tensor_tensor(f16[:, s], ps_acc[:, s], tok_scale[:, c % 4:c % 4 + 1], wsc_b[:, s], ALU.mult, ALU.mult).then_inc(sem("f_ready"), 1)

            def rounded(i, c):
                wait(dve, "yv_ready", at(i, c, 1, 1))
                wait(dve, "yqT_psum", at(i, c))
                v.tensor_scalar(yq[:, :, :].rearrange("p s m -> p (s m)"), yv[:, :, :].rearrange("p s m -> p (s m)"), MAGIC, -MAGIC,
                                ALU.add, ALU.add).then_inc(sem("yq_ready"), 1)

            def body(i, c, on):
                early = isinstance(i, int) and at(i, c) == 3
                if early:
                    rank_weights()
                    chan_max(i, c - 1)
                elif on(-1):
                    row_max(i, c - 1)
                if on(-5):
                    rank_out(i, c - 5)
                if on(-4):
                    low(i, c - 4, 0)
                    low(i, c - 4, 1)
                if on(-3):
                    mixed(i, c - 3, 0)
                    if not early:
                        tile_scale(i, c - 3)
                if on(-1):
                    if not early:
                        chan_max(i, c - 1)
                    scales(i, c - 1)
                if early:
                    blocks(i, c + 1)
                if on(0):
                    conv_bias(i, c)
                if on(1) and not early:
                    blocks(i, c + 1)
                if on(-2):
                    layer0(i, c - 2, 0)
                if on(-1):
                    rounded(i, c - 1)
                if on(-3):
                    mixed(i, c - 3, 1)
                if early:
                    tile_scale(i, c - 3)
                if on(-2):
                    layer0(i, c - 2, 1)

            blocks(0, 0)
            small_maxima()
            dense_maxima(0, (0, 1))
            dense_maxima(1, (2, 3))
            blocks(0, 1)
            dense_maxima(2, (4,))
            dense_bound()
            weight_scales()
            conv_bias(0, 0)
            row_max(0, 0)
            dense_weights(range(0, 3))
            chan_max(0, 0)
            dense_weights(range(3, 4))
            scales(0, 0)
            dense_weights(range(4, 6))
            mixing_bias()
            blocks(0, 2)
            rounded(0, 0)
            conv_bias(0, 1)
            dense_weights(range(6, 10))
            row_max(0, 1)
            dense_weights(range(10, 13))
            chan_max(0, 1)
            blocks(0, 3)
            dense_weights(range(13, 15))
            scales(0, 1)
            dense_weights(range(15, 16))
            conv_bias(0, 2)
            rounded(0, 1)
            layer0(0, 0, 0)
            row_max(0, 2)
            layer0(0, 0, 1)
            bodies(dve, body, 3)
            row_max(0, NT - 1)
            rank_out(0, NT - 5)
            low(0, NT - 4, 0)
            chan_max(0, NT - 1)
            low(0, NT - 4, 1)
            mixed(0, NT - 3, 0)
            scales(0, NT - 1)
            mixed(0, NT - 3, 1)
            tile_scale(0, NT - 3)
            layer0(0, NT - 2, 0)
            rounded(0, NT - 1)
            layer0(0, NT - 2, 1)
            rank_out(0, NT - 4)
            low(0, NT - 3, 0)
            low(0, NT - 3, 1)
            mixed(0, NT - 2, 0)
            layer0(0, NT - 1, 0)
            layer0(0, NT - 1, 1)
            mixed(0, NT - 2, 1)
            tile_scale(0, NT - 2)
            low(0, NT - 2, 0)
            low(0, NT - 2, 1)
            mixed(0, NT - 1, 0)
            rank_out(0, NT - 3)
            mixed(0, NT - 1, 1)
            tile_scale(0, NT - 1)
            low(0, NT - 1, 0)
            low(0, NT - 1, 1)
            rank_out(0, NT - 2)
            rank_out(0, NT - 1)

            def fold(i, c, hs=(0, 1)):
                wait(dve, f"xb_loaded{c % 4}", i * 16 + 16 * (c // 4 + 1))
                for h in hs:
                    s = slice(h * HALF, (h + 1) * HALF)
                    wait(dve, "dense_half_ready" if h == 0 else "dense_ready", at(i, c, 1, 1))
                    v.scalar_tensor_tensor(xb_in[:, c % 4, s], bank(2 * (c % 2) + h), unscale[:, bass.ds(at(i, c), 1)], xb_in[:, c % 4, s],
                                           ALU.mult, ALU.add).then_inc(sem("folded"), 1)

            ps_g = bank(4, 4)
            link(v.tensor_scalar(unscale[:, :], t_all[:, :, 1], w_down[:, 0:1], None, ALU.mult))
            fold(0, 0)
            fold(0, 1)
            dve.wait_ge(sem("logits_psum"), 1)
            logits = ps_g[:, 0:NJ * 2 * E].rearrange("p (j w e) -> p j w e", w=2, e=E)
            h_log, d_log, lg, ex, pr, mk, wt, gt = (gate[:, n] for n in range(8))
            flat = lambda a: a.rearrange("p j e -> p (j e)")
            link(v.tensor_scalar(h_log, logits[:, :, 0, :], w_down[:, 0:1], None, ALU.mult))
            link(v.tensor_tensor(h_log, h_log, bias_b[:, 0:E].unsqueeze(1).to_broadcast([P, NJ, E]), ALU.add))
            v.tensor_scalar(d_log, logits[:, :, 1, :], w_down[:, 1:2], None, ALU.mult).then_inc(sem("logits_read"), 1)
            v.tensor_reduce(gmx[:, 0:1], h_log, AX.XY, ALU.max, apply_absolute_value=True).then_inc(sem("gmax_ready"), 1)
            dve.wait_ge(sem("logits_read"), 1)
            v.tensor_reduce(gmx[:, 1:2], d_log, AX.XY, ALU.max, apply_absolute_value=True).then_inc(sem("gmax_ready"), 1)
            dve.wait_ge(sem("gmax_all"), 1)
            link(v.tensor_scalar(gmx[:, 4:6], gmx[:, 2:4], 1e-6, None, ALU.max))
            link(v.reciprocal(gmx[:, 6:8], gmx[:, 4:6]))
            link(v.tensor_scalar(flat(h_log), flat(h_log), gmx[:, 6:7], 0.5, ALU.mult, ALU.mult))
            link(v.tensor_scalar(flat(d_log), flat(d_log), gmx[:, 7:8], 0.5, ALU.mult, ALU.mult))
            link(v.tensor_tensor(lg, h_log, d_log, ALU.add))
            link(v.tensor_reduce(gsm[:, 0, :], lg, AX.X, ALU.max))
            v.tensor_tensor(lg, lg, gsm[:, 0, :].unsqueeze(2).to_broadcast([P, NJ, E]), ALU.subtract).then_inc(sem("gate_in_ready"), 1)
            dve.wait_ge(sem("gate_exp_ready"), 1)
            link(v.tensor_reduce(gsm[:, 1, :], ex, AX.X, ALU.add))
            link(v.reciprocal(gsm[:, 2, :], gsm[:, 1, :]))
            link(v.tensor_tensor(pr, ex, gsm[:, 2, :].unsqueeze(2).to_broadcast([P, NJ, E]), ALU.mult))
            for j in range(NJ):
                last = v.max(top8[:, j, :], pr[:, j, :])
            link(last)
            v.tensor_tensor(mk, pr, top8[:, :, 1:2].to_broadcast([P, NJ, E]), ALU.subtract).then_inc(sem("gate_in_ready"), 1)
            dve.wait_ge(sem("gate_exp_ready"), 2)
            link(v.tensor_scalar(flat(mk), flat(mk), 1.0, None, ALU.add))
            link(v.reciprocal(flat(mk), flat(mk)))
            link(v.tensor_tensor(wt, pr, mk, ALU.mult))
            link(v.tensor_reduce(gsm[:, 3, :], wt, AX.X, ALU.add))
            link(v.tensor_scalar(gsm[:, 4, :], gsm[:, 3, :], 1e-9, None, ALU.add))
            link(v.reciprocal(gsm[:, 5, :], gsm[:, 4, :]))
            v.tensor_tensor(gt, wt, gsm[:, 5, :].unsqueeze(2).to_broadcast([P, NJ, E]), ALU.mult).then_inc(sem("gate_ready"), 1)
            fold(0, 2)
            link(v.memset(z_max[:, :], 0.0))
            for k in range(4):
                dve.wait_ge(sem("pmix_psum"), k + 1)
                zk = zT[0:R, k * 1024:(k + 1) * 1024].rearrange("p (a e) -> p a e", e=2)
                link(v.tensor_tensor(zk, zk, ps_g[0:R, k * 512:(k + 1) * 512].unsqueeze(2).to_broadcast([R, 512, 2]), ALU.mult))
                v.tensor_reduce(z_max[0:R, 8 * k:8 * k + 8], zT[0:R, k * 1024:(k + 1) * 1024].rearrange("p (t c) -> p t c", c=P),
                                AX.X, ALU.max, apply_absolute_value=True).then_inc(sem("z_max_ready"), 1)
            dve.wait_ge(sem("z_max_all_ready"), 1)
            link(v.tensor_scalar(z_exp[:, :], z_exp[:, :], 1e-20, None, ALU.max))
            link(v.tensor_scalar(z_exp[:, :].bitcast(U32), z_exp[:, :].bitcast(U32), EXPMASK, None, ALU.bitwise_and))
            v.tensor_scalar(z_up[:, :].bitcast(I32), z_exp[:, :].bitcast(I32), -1.0, float((254 + TOP) << 23), ALU.mult, ALU.add)
            link(v.tensor_scalar(unscale_d[:, :].bitcast(I32), z_exp[:, :].bitcast(I32), float(-(TOP << 23)), None, ALU.add))
            link(v.tensor_scalar(unscale_d[:, :], unscale_d[:, :], w_down[:, 1:2], w_down[:, 2:3], ALU.mult, ALU.mult))
            link(v.tensor_scalar(unscale_d[:, :], unscale_d[:, :], w_down[:, 3:4], 2.0 ** (TOP + 1) * 16.0 / R, ALU.mult, ALU.mult))

            def rank_cols(i, c):
                wait(dve, "delta_ready", at(i, c, 1, -1))
                ztile, up = zT[0:R, bass.ds(at(i, c, P), P)], z_up[0:R, bass.ds(at(i, c), 1)]
                v.tensor_scalar(z_scaled[:, c % 2, :], ztile, up, None, ALU.mult).then_inc(sem("z_high"), 1)
                for n in range(2):
                    v.tensor_scalar(z_parts[n * R:(n + 1) * R, c % 2, :], ztile, up, None, ALU.mult).then_inc(sem("z_high"), 1)
                wait(dve, "z_high", at(i, c, 3, 3))
                v.tensor_tensor(z_parts[2 * R:3 * R, c % 2, :], z_scaled[:, c % 2, :], z_parts[0:R, c % 2, :], ALU.subtract).then_inc(sem("z_parts_ready"), 1)

            def finish(i, c, hs=(0, 1)):
                wait(dve, "delta_ready", at(i, c, 1, 1))
                if not isinstance(i, int) or 4 * i + c >= 2:
                    wait(dve, f"out_saved{c % 2}", i * 32 + 16 * (c // 2))
                for h in hs:
                    s = slice(h * HALF, (h + 1) * HALF)
                    wait(dve, "folded", at(i, c, 2, h + 1))
                    v.scalar_tensor_tensor(o_sb[:, c % 2, s], bank(4 + 2 * (c % 2) + h), unscale_d[:, bass.ds(at(i, c), 1)], xb_in[:, c % 4, s],
                                           ALU.mult, ALU.add).then_inc(sem("out_ready"), 1)

            rank_cols(0, 0)
            rank_cols(0, 1)
            fold(0, 3)
            for c in range(2):
                finish(0, c)
                rank_cols(0, c + 2)
            fold(1, 0)
            finish(0, 2)
            rank_cols(1, 0)
            with dve.Fori(1, NT // 4 - 1) as i:
                for c in range(1, 5):
                    fold(i, c)
                    finish(i, c - 2)
                    rank_cols(i, c)
            j = NT // 4 - 1
            for c in range(1, 3):
                fold(j, c)
                finish(j, c - 2)
                rank_cols(j, c)
            finish(j, 1)
            rank_cols(j, 3)
            fold(j, 3, (0,))
            finish(j, 2)
            finish(j, 3, (0,))
            s = slice(HALF, L)
            v.scalar_tensor_tensor(xb_in[:, 3, s], bank(7), unscale_d[:, NT - 1:NT], xb_in[:, 3, s], ALU.mult, ALU.add).then_inc(sem("folded"), 1)
            dve.wait_ge(sem("folded"), 2 * NT)
            dve.wait_ge(sem("dense_ready"), NT)
            v.scalar_tensor_tensor(o_sb[:, 1, s], bank(3), unscale[:, NT - 1:NT], xb_in[:, 3, s], ALU.mult, ALU.add).then_inc(sem("out_ready"), 1)


_INS = ['x', 'cond_128', 'fside_S_0', 'L0_cond_weight', 'L0_cond_c_weight', 'L0_ffn_weight', 'L1_cond_W0', 'L1_cond_b0',
        'L1_cond_W1', 'L1_cond_b1', 'L1_cond_W2', 'L1_cond_b2', 'L1_cond_weight', 'L1_cond_bias_k', 'L1_ffn_W', 'L1_ffn_b',
        'L1_ffn_A', 'L1_ffn_Bmat', 'L1_ffn_LiMEs']


def kernel(**inputs):
    import numpy as _np
    import concourse.bacc as _bacc
    from concourse import mybir as _mybir
    from concourse.bass_utils import run_bass_kernel_spmd as _run

    nc = _bacc.Bacc("TRN2", target_bir_lowering=False, num_devices=1)
    arrays, args = {}, []
    for name in _INS:
        a = _np.ascontiguousarray(inputs[name])
        arrays[f"in_{name}"] = a
        args.append(nc.dram_tensor(f"in_{name}", a.shape, _mybir.dt.from_np(a.dtype), kind="ExternalInput").ap())
    args.append(nc.dram_tensor("out", (B, CH, L), F32, kind="ExternalOutput").ap())
    program(nc, *args)
    r = _run(nc, [arrays], core_ids=[0])
    return r.results[0]["out"]
```
